# Optimizing a Trainium2 kernel written in Bass

```python
import numpy as np
import jax
import jax.numpy as jnp

def _softmax(x, axis=-1):
    return jax.nn.softmax(x, axis=axis)

def _gelu(x):
    return jax.nn.gelu(x, approximate=True)

def _silu(x):
    return jax.nn.silu(x)

def _sigmoid(x):
    return jax.nn.sigmoid(x)

def _layernorm(x, axis=-1, eps=1e-05):
    m = jnp.mean(x, axis=axis, keepdims=True)
    v = jnp.var(x, axis=axis, keepdims=True)
    return (x - m) / jnp.sqrt(v + eps)

def _scatter_add(tgt, idx, src, axis=0):
    return tgt.at[idx].add(src)

def _segment_sum(src, seg, n):
    return jax.ops.segment_sum(src, seg, n)
kernel_name = 'mk_decoder_preln_d1_seqx_r4_4fed4c'

def setup_inputs(seed: int=0):
    np.random.seed(seed)
    _w = jnp.asarray

    def _rec_inputs():
        import jax
        import jax.numpy as jnp
        _rk = jax.random.key(seed)
        x = -0.0003929 + 0.9999 * jax.random.normal(jax.random.fold_in(_rk, 1), (16, 128, 256), jnp.float32)
        _lenS = 128 - jax.random.randint(jax.random.fold_in(_rk, 7), (16,), 0, max(1, 128 // 4) + 1, jnp.int32)
        _lenS2 = 128 - jax.random.randint(jax.random.fold_in(_rk, 8), (16,), 0, max(1, 128 // 4) + 1, jnp.int32)
        _ctx_1024P = jax.random.normal(jax.random.fold_in(_rk, 11), (16, 16, 256), jnp.float32)
        _ctx_1024c = jax.random.dirichlet(jax.random.fold_in(_rk, 511), 0.3 * jnp.ones((16,), jnp.float32), (16, 128))
        _ctx_1024t = jnp.einsum('bsk,bkd->bsd', _ctx_1024c, _ctx_1024P)
        _ctx_1024t = _ctx_1024t * jax.lax.rsqrt(jnp.mean(jnp.square(_ctx_1024t)) + 1e-12) * 0.953939
        ctx_1024 = 2.81802e-05 + 1.00001 * (_ctx_1024t + 0.3 * jax.random.normal(jax.random.fold_in(_rk, 611), (16, 128, 256), jnp.float32))
        return (x, ctx_1024)
    x, ctx_1024 = _rec_inputs()

    def _L0_attn_setup():
        import jax, jax.numpy as jnp
        import numpy as np
        H = 256
        NH = 4
        KD = 128
        VD = 256
        DK = KD // NH
        DV = VD // NH
        C = 32
        PLR = 32
        GLR = 64
        B, L = (2, 512)
        EPS = 1e-05

        def chunk_rwkv6(q, k, v, w, u, chunk_size=C):
            b, h, Lt, dk = q.shape
            dv = v.shape[-1]
            n = Lt // chunk_size
            c = chunk_size
            resh = lambda x: x.reshape(b, h, n, c, -1).astype(jnp.float32)
            q, k, v, w = (resh(q), resh(k), resh(v), resh(w))
            wc = jnp.cumsum(w, axis=-2)
            kw = k * jnp.exp(wc[..., -1:, :] - wc)
            wkv = jnp.einsum('bhncd,bhncp->bhndp', kw, v)
            dec = jnp.exp(wc[:, :, :, -1, :])
            dec_s = jnp.moveaxis(dec, 2, 0)
            wkv_s = jnp.moveaxis(wkv, 2, 0)
            S0 = jnp.zeros((b, h, dk, dv), jnp.float32)

            def step(S, xs):
                d, kv = xs
                return (S * d[..., None] + kv, S)
            _, ys = jax.lax.scan(step, S0, (dec_s, wkv_s))
            wkv_new = jnp.moveaxis(ys, 0, 2)
            qe = q * jnp.exp(wc - w)
            o_inter = jnp.einsum('bhndp,bhncd->bhncp', wkv_new, qe)
            decay_ij = wc[:, :, :, :, None, :] - w[:, :, :, :, None, :] - wc[:, :, :, None, :, :]
            tri = jnp.arange(c)[:, None] > jnp.arange(c)[None, :]
            decay_ij = jnp.where(tri[None, None, None, :, :, None], decay_ij, -jnp.inf)
            attn = jnp.einsum('bhnid,bhnjd,bhnijd->bhnij', q, k, jnp.exp(decay_ij))
            o_intra = jnp.einsum('bhnij,bhnjp->bhnip', attn, v)
            diag = jnp.einsum('bhnid,hd,bhnid->bhni', q, u.astype(jnp.float32), k)[..., None] * v
            o = o_inter + o_intra + diag
            return o.reshape(b, h, Lt, dv)

        def rwkv6_forward(x, mu0, Wx0, Wx2, x_bias, rW, wA, wB, wb, kW, vW, gA, gB, gb, bonus, ln_g, ln_b, oW):
            b, l, hdim = x.shape
            shifted = jnp.pad(x[:, :-1], ((0, 0), (1, 0), (0, 0)))
            delta = shifted - x
            xx = jnp.tanh((x + delta * mu0) @ Wx0.T).reshape(b, l, 5, PLR)
            mix = jnp.einsum('blnr,hnr->blnh', xx, Wx2.reshape(hdim, 5, PLR)) + x_bias
            r_mu, w_mu, k_mu, v_mu, g_mu = [mix[:, :, i] for i in range(5)]
            r = (x + delta * r_mu) @ rW.T
            wv = x + delta * w_mu
            w_val = jnp.tanh(wv @ wA.T) @ wB.T + wb
            k = (x + delta * k_mu) @ kW.T
            v = (x + delta * v_mu) @ vW.T
            gv = x + delta * g_mu
            g = jnp.tanh(gv @ gA.T) @ gB.T + gb
            to_heads = lambda t, d: t.reshape(b, l, NH, d).transpose(0, 2, 1, 3)
            r_h, w_h, k_h = (to_heads(r, DK), to_heads(w_val, DK), to_heads(k, DK))
            v_h = to_heads(v, DV)
            w_h = -jnp.exp(w_h)
            o = chunk_rwkv6(r_h, k_h, v_h, w_h, bonus)
            o = o.transpose(0, 2, 1, 3).reshape(b, l, VD)
            mu = o.mean(-1, keepdims=True)
            var = ((o - mu) ** 2).mean(-1, keepdims=True)
            o = (o - mu) * jax.lax.rsqrt(var + EPS) * ln_g + ln_b
            o = o * (g * jax.nn.sigmoid(g))
            return o @ oW.T
        key = jax.random.key(seed)
        ks = jax.random.split(key, 18)
        s = 0.05
        n = lambda k, shape: jax.random.normal(k, shape, jnp.float32) * s
        return {'hidden_states': jax.random.normal(ks[0], (B, L, H), jnp.float32), 'mu0': n(ks[1], (H,)), 'Wx0': n(ks[2], (PLR * 5, H)), 'Wx2': n(ks[3], (H, PLR * 5)), 'x_bias': n(ks[4], (5, H)), 'rW': n(ks[5], (KD, H)), 'wA': n(ks[6], (GLR, H)), 'wB': n(ks[7], (KD, GLR)), 'wb': jnp.zeros((KD,), jnp.float32), 'kW': n(ks[8], (KD, H)), 'vW': n(ks[9], (VD, H)), 'gA': n(ks[10], (GLR, H)), 'gB': n(ks[11], (VD, GLR)), 'gb': jnp.zeros((VD,), jnp.float32), 'bonus': n(ks[12], (NH, DK)), 'ln_g': jnp.ones((VD,), jnp.float32), 'ln_b': jnp.zeros((VD,), jnp.float32), 'oW': n(ks[13], (VD, H))}
    _L0_attn_all = _L0_attn_setup()
    _L0_attn_in = {k: v for k, v in _L0_attn_all.items() if k in ('mu0', 'Wx0', 'Wx2', 'x_bias', 'rW', 'wA', 'wB', 'wb', 'kW', 'vW', 'gA', 'gB', 'gb', 'bonus', 'ln_g', 'ln_b', 'oW')}
    del _L0_attn_all

    def _L0_xattn_setup():
        import math
        import jax, jax.numpy as jnp
        import numpy as np
        D_MODEL, N_HEADS, D_K = (256, 16, 64)
        B, S = (4, 1024)
        key = jax.random.key(seed)
        ks = jax.random.split(key, 11)
        scale = 1.0 / math.sqrt(D_MODEL)
        hd = N_HEADS * D_K
        return {'query': jax.random.normal(ks[0], (B, S, D_MODEL), jnp.float32), 'key': jax.random.normal(ks[1], (B, S, D_MODEL), jnp.float32), 'value': jax.random.normal(ks[2], (B, S, D_MODEL), jnp.float32), 'Wq': jax.random.normal(ks[3], (hd, D_MODEL), jnp.float32) * scale, 'bq': jnp.zeros((hd,), jnp.float32), 'Wk': jax.random.normal(ks[4], (hd, D_MODEL), jnp.float32) * scale, 'bk': jnp.zeros((hd,), jnp.float32), 'Wv': jax.random.normal(ks[5], (hd, D_MODEL), jnp.float32) * scale, 'bv': jnp.zeros((hd,), jnp.float32), 'Wo': jax.random.normal(ks[6], (D_MODEL, hd), jnp.float32) * scale, 'bo': jnp.zeros((D_MODEL,), jnp.float32)}
    _L0_xattn_all = _L0_xattn_setup()
    _L0_xattn_in = {k: v for k, v in _L0_xattn_all.items() if k in ('Wq', 'bq', 'Wk', 'bk', 'Wv', 'bv', 'Wo', 'bo')}
    del _L0_xattn_all

    def _L0_ffn_setup():
        import jax, jax.numpy as jnp
        import numpy as np
        B, T, D, E, H = (4, 512, 256, 4, 8)
        EPS = 1e-05

        def _uniform(k, shape, bound):
            return jax.random.uniform(k, shape, jnp.float32, -bound, bound)

        def _layernorm(x, w, b):
            mu = jnp.mean(x, axis=-1, keepdims=True)
            var = jnp.mean(jnp.square(x - mu), axis=-1, keepdims=True)
            return (x - mu) * jax.lax.rsqrt(var + EPS) * w + b
        key = jax.random.key(seed)
        ks = jax.random.split(key, 12)
        wb = np.sqrt(6.0 / D) / np.sqrt(6.0)
        wb = 1.0 / np.sqrt(D)
        return {'x': jax.random.normal(ks[0], (B, T, D), jnp.float32), 'router_prob': jax.random.uniform(ks[1], (B, T, E), jnp.float32), 'norm_w': jnp.ones((D,), jnp.float32), 'norm_b': jnp.zeros((D,), jnp.float32), 'q_w': _uniform(ks[2], (D, D), wb), 'q_b': _uniform(ks[3], (D,), wb), 'k_w': _uniform(ks[4], (D, D), wb), 'k_b': _uniform(ks[5], (D,), wb), 'v_w': _uniform(ks[6], (D, D), wb), 'v_b': _uniform(ks[7], (D,), wb), 'o_w': _uniform(ks[8], (D, D), wb), 'o_b': _uniform(ks[9], (D,), wb)}
    _L0_ffn_all = _L0_ffn_setup()
    _L0_ffn_in = {k: v for k, v in _L0_ffn_all.items() if k in ('router_prob', 'norm_w', 'norm_b', 'q_w', 'q_b', 'k_w', 'k_b', 'v_w', 'v_b', 'o_w', 'o_b')}
    del _L0_ffn_all
    return {'x': x, 'ctx_1024': ctx_1024, 'L0_attn_mu0': _L0_attn_in['mu0'], 'L0_attn_Wx0': _L0_attn_in['Wx0'], 'L0_attn_Wx2': _L0_attn_in['Wx2'], 'L0_attn_x_bias': _L0_attn_in['x_bias'], 'L0_attn_rW': _L0_attn_in['rW'], 'L0_attn_wA': _L0_attn_in['wA'], 'L0_attn_wB': _L0_attn_in['wB'], 'L0_attn_wb': _L0_attn_in['wb'], 'L0_attn_kW': _L0_attn_in['kW'], 'L0_attn_vW': _L0_attn_in['vW'], 'L0_attn_gA': _L0_attn_in['gA'], 'L0_attn_gB': _L0_attn_in['gB'], 'L0_attn_gb': _L0_attn_in['gb'], 'L0_attn_bonus': _L0_attn_in['bonus'], 'L0_attn_ln_g': _L0_attn_in['ln_g'], 'L0_attn_ln_b': _L0_attn_in['ln_b'], 'L0_attn_oW': _L0_attn_in['oW'], 'L0_xattn_Wq': _L0_xattn_in['Wq'], 'L0_xattn_bq': _L0_xattn_in['bq'], 'L0_xattn_Wk': _L0_xattn_in['Wk'], 'L0_xattn_bk': _L0_xattn_in['bk'], 'L0_xattn_Wv': _L0_xattn_in['Wv'], 'L0_xattn_bv': _L0_xattn_in['bv'], 'L0_xattn_Wo': _L0_xattn_in['Wo'], 'L0_xattn_bo': _L0_xattn_in['bo'], 'L0_ffn_router_prob': _L0_ffn_in['router_prob'], 'L0_ffn_norm_w': _L0_ffn_in['norm_w'], 'L0_ffn_norm_b': _L0_ffn_in['norm_b'], 'L0_ffn_q_w': _L0_ffn_in['q_w'], 'L0_ffn_q_b': _L0_ffn_in['q_b'], 'L0_ffn_k_w': _L0_ffn_in['k_w'], 'L0_ffn_k_b': _L0_ffn_in['k_b'], 'L0_ffn_v_w': _L0_ffn_in['v_w'], 'L0_ffn_v_b': _L0_ffn_in['v_b'], 'L0_ffn_o_w': _L0_ffn_in['o_w'], 'L0_ffn_o_b': _L0_ffn_in['o_b']}

def reference(x, ctx_1024, L0_attn_mu0, L0_attn_Wx0, L0_attn_Wx2, L0_attn_x_bias, L0_attn_rW, L0_attn_wA, L0_attn_wB, L0_attn_wb, L0_attn_kW, L0_attn_vW, L0_attn_gA, L0_attn_gB, L0_attn_gb, L0_attn_bonus, L0_attn_ln_g, L0_attn_ln_b, L0_attn_oW, L0_xattn_Wq, L0_xattn_bq, L0_xattn_Wk, L0_xattn_bk, L0_xattn_Wv, L0_xattn_bv, L0_xattn_Wo, L0_xattn_bo, L0_ffn_router_prob, L0_ffn_norm_w, L0_ffn_norm_b, L0_ffn_q_w, L0_ffn_q_b, L0_ffn_k_w, L0_ffn_k_b, L0_ffn_v_w, L0_ffn_v_b, L0_ffn_o_w, L0_ffn_o_b):
    import jax
    import jax.numpy as jnp

    def _L0_attn_ref(hidden_states, mu0, Wx0, Wx2, x_bias, rW, wA, wB, wb, kW, vW, gA, gB, gb, bonus, ln_g, ln_b, oW):
        import jax, jax.numpy as jnp
        import numpy as np
        H = 256
        NH = 4
        KD = 128
        VD = 256
        DK = KD // NH
        DV = VD // NH
        C = 32
        PLR = 32
        GLR = 64
        B, L = (2, 512)
        EPS = 1e-05

        def chunk_rwkv6(q, k, v, w, u, chunk_size=C):
            b, h, Lt, dk = q.shape
            dv = v.shape[-1]
            n = Lt // chunk_size
            c = chunk_size
            resh = lambda x: x.reshape(b, h, n, c, -1).astype(jnp.float32)
            q, k, v, w = (resh(q), resh(k), resh(v), resh(w))
            wc = jnp.cumsum(w, axis=-2)
            kw = k * jnp.exp(wc[..., -1:, :] - wc)
            wkv = jnp.einsum('bhncd,bhncp->bhndp', kw, v)
            dec = jnp.exp(wc[:, :, :, -1, :])
            dec_s = jnp.moveaxis(dec, 2, 0)
            wkv_s = jnp.moveaxis(wkv, 2, 0)
            S0 = jnp.zeros((b, h, dk, dv), jnp.float32)

            def step(S, xs):
                d, kv = xs
                return (S * d[..., None] + kv, S)
            _, ys = jax.lax.scan(step, S0, (dec_s, wkv_s))
            wkv_new = jnp.moveaxis(ys, 0, 2)
            qe = q * jnp.exp(wc - w)
            o_inter = jnp.einsum('bhndp,bhncd->bhncp', wkv_new, qe)
            decay_ij = wc[:, :, :, :, None, :] - w[:, :, :, :, None, :] - wc[:, :, :, None, :, :]
            tri = jnp.arange(c)[:, None] > jnp.arange(c)[None, :]
            decay_ij = jnp.where(tri[None, None, None, :, :, None], decay_ij, -jnp.inf)
            attn = jnp.einsum('bhnid,bhnjd,bhnijd->bhnij', q, k, jnp.exp(decay_ij))
            o_intra = jnp.einsum('bhnij,bhnjp->bhnip', attn, v)
            diag = jnp.einsum('bhnid,hd,bhnid->bhni', q, u.astype(jnp.float32), k)[..., None] * v
            o = o_inter + o_intra + diag
            return o.reshape(b, h, Lt, dv)

        def rwkv6_forward(x, mu0, Wx0, Wx2, x_bias, rW, wA, wB, wb, kW, vW, gA, gB, gb, bonus, ln_g, ln_b, oW):
            b, l, hdim = x.shape
            shifted = jnp.pad(x[:, :-1], ((0, 0), (1, 0), (0, 0)))
            delta = shifted - x
            xx = jnp.tanh((x + delta * mu0) @ Wx0.T).reshape(b, l, 5, PLR)
            mix = jnp.einsum('blnr,hnr->blnh', xx, Wx2.reshape(hdim, 5, PLR)) + x_bias
            r_mu, w_mu, k_mu, v_mu, g_mu = [mix[:, :, i] for i in range(5)]
            r = (x + delta * r_mu) @ rW.T
            wv = x + delta * w_mu
            w_val = jnp.tanh(wv @ wA.T) @ wB.T + wb
            k = (x + delta * k_mu) @ kW.T
            v = (x + delta * v_mu) @ vW.T
            gv = x + delta * g_mu
            g = jnp.tanh(gv @ gA.T) @ gB.T + gb
            to_heads = lambda t, d: t.reshape(b, l, NH, d).transpose(0, 2, 1, 3)
            r_h, w_h, k_h = (to_heads(r, DK), to_heads(w_val, DK), to_heads(k, DK))
            v_h = to_heads(v, DV)
            w_h = -jnp.exp(w_h)
            o = chunk_rwkv6(r_h, k_h, v_h, w_h, bonus)
            o = o.transpose(0, 2, 1, 3).reshape(b, l, VD)
            mu = o.mean(-1, keepdims=True)
            var = ((o - mu) ** 2).mean(-1, keepdims=True)
            o = (o - mu) * jax.lax.rsqrt(var + EPS) * ln_g + ln_b
            o = o * (g * jax.nn.sigmoid(g))
            return o @ oW.T
        return rwkv6_forward(hidden_states, mu0, Wx0, Wx2, x_bias, rW, wA, wB, wb, kW, vW, gA, gB, gb, bonus, ln_g, ln_b, oW)

    def _L0_xattn_ref(query, key, value, Wq, bq, Wk, bk, Wv, bv, Wo, bo):
        import math
        import jax, jax.numpy as jnp
        import numpy as np
        D_MODEL, N_HEADS, D_K = (256, 16, 64)
        B, S = (4, 1024)
        b, s, _ = query.shape
        q = (query @ Wq.T + bq).reshape(b, s, N_HEADS, D_K)
        k = (key @ Wk.T + bk).reshape(b, s, N_HEADS, D_K)
        v = (value @ Wv.T + bv).reshape(b, s, N_HEADS, D_K)
        inv_sqrt_dk = 1.0 / math.sqrt(D_K)
        scores = jnp.einsum('bshd,bsgd->bshg', q, k) * inv_sqrt_dk
        attn = jax.nn.softmax(scores, axis=-1)
        out = jnp.einsum('bshg,bsgd->bshd', attn, v)
        out = jnp.transpose(out, (0, 2, 1, 3)).reshape(b, -1, N_HEADS * D_K)
        return out @ Wo.T + bo

    def _L0_ffn_ref(x, router_prob, norm_w, norm_b, q_w, q_b, k_w, k_b, v_w, v_b, o_w, o_b):
        import jax, jax.numpy as jnp
        import numpy as np
        B, T, D, E, H = (4, 512, 256, 4, 8)
        EPS = 1e-05

        def _uniform(k, shape, bound):
            return jax.random.uniform(k, shape, jnp.float32, -bound, bound)

        def _layernorm(x, w, b):
            mu = jnp.mean(x, axis=-1, keepdims=True)
            var = jnp.mean(jnp.square(x - mu), axis=-1, keepdims=True)
            return (x - mu) * jax.lax.rsqrt(var + EPS) * w + b
        e_cnt = router_prob.shape[2]
        b, t, d = x.shape
        n = t // e_cnt
        h = H
        scale = d ** (-0.5)
        qs, ks_, vs = ([], [], [])
        for e in range(e_cnt):
            xe = x[:, e * n:(e + 1) * n, :]
            xn = _layernorm(xe, norm_w, norm_b)
            m = d // 2 ** e
            xm = xn[..., :m]
            qs.append(jnp.einsum('bnm,dm->bnd', xm, q_w[:, :m]) + q_b)
            ks_.append(jnp.einsum('bnm,dm->bnd', xm, k_w[:, :m]) + k_b)
            vs.append(jnp.einsum('bnm,dm->bnd', xm, v_w[:, :m]) + v_b)
        q = jnp.concatenate(qs, axis=1)
        k = jnp.concatenate(ks_, axis=1)
        v = jnp.concatenate(vs, axis=1)
        dh = d // h
        q = q.reshape(b, t, h, dh).transpose(0, 2, 1, 3)
        k = k.reshape(b, t, h, dh).transpose(0, 2, 1, 3)
        v = v.reshape(b, t, h, dh).transpose(0, 2, 1, 3)
        attn = jnp.einsum('bhqd,bhkd->bhqk', q, k) * scale
        attn = jax.nn.softmax(attn, axis=-1)
        attn_out = jnp.einsum('bhqk,bhkd->bhqd', attn, v)
        attn_out = attn_out.transpose(0, 2, 1, 3).reshape(b, t, d)
        outs = []
        for e in range(e_cnt):
            sl = slice(e * n, (e + 1) * n)
            m = d // 2 ** e
            xm = attn_out[:, sl, :m]
            out = jnp.einsum('bnm,om->bno', xm, o_w[:m, :m]) + o_b[:m]
            pad = d - m
            if pad:
                out = jnp.pad(out, ((0, 0), (0, 0), (0, pad)))
            outs.append(out + x[:, sl, :])
        return jnp.concatenate(outs, axis=1)
    x = x + _L0_attn_ref(_layernorm(x, axis=-1), L0_attn_mu0, L0_attn_Wx0, L0_attn_Wx2, L0_attn_x_bias, L0_attn_rW, L0_attn_wA, L0_attn_wB, L0_attn_wb, L0_attn_kW, L0_attn_vW, L0_attn_gA, L0_attn_gB, L0_attn_gb, L0_attn_bonus, L0_attn_ln_g, L0_attn_ln_b, L0_attn_oW)
    x = x + _L0_xattn_ref(_layernorm(x, axis=-1), ctx_1024, ctx_1024, L0_xattn_Wq, L0_xattn_bq, L0_xattn_Wk, L0_xattn_bk, L0_xattn_Wv, L0_xattn_bv, L0_xattn_Wo, L0_xattn_bo)
    x = x + _L0_ffn_ref(_layernorm(x, axis=-1), L0_ffn_router_prob, L0_ffn_norm_w, L0_ffn_norm_b, L0_ffn_q_w, L0_ffn_q_b, L0_ffn_k_w, L0_ffn_k_b, L0_ffn_v_w, L0_ffn_v_b, L0_ffn_o_w, L0_ffn_o_b)
    return x

_drawn_inputs = setup_inputs


def setup_inputs(seed=0):
    import zlib

    import numpy as np

    out = dict(_drawn_inputs(seed))
    spreads = {'L0_attn_wb': (0.0, 0.8),
     'L0_attn_gb': (0.0, 0.1),
     'L0_attn_ln_g': (1.0, 0.6),
     'L0_attn_ln_b': (0.0, 0.773),
     'L0_xattn_bq': (0.0, 0.1),
     'L0_xattn_bk': (0.0, 0.1),
     'L0_xattn_bv': (0.0, 0.1),
     'L0_xattn_bo': (0.0, 0.1),
     'L0_ffn_norm_w': (1.0, 0.6),
     'L0_ffn_norm_b': (0.0, 0.8)}
    factors = {'L0_attn_mu0': 8.0,
     'L0_attn_x_bias': 3.888,
     'L0_attn_wA': 5.609,
     'L0_attn_wB': 5.6,
     'L0_attn_bonus': 6.386,
     'L0_ffn_q_w': 8.0,
     'L0_ffn_q_b': 8.0,
     'L0_ffn_k_w': 8.0,
     'L0_ffn_k_b': 8.0,
     'L0_ffn_v_w': 3.95,
     'L0_ffn_v_b': 8.0,
     'L0_ffn_o_w': 3.737,
     'L0_ffn_o_b': 4.956}
    for name, (base, spread) in spreads.items():
        noise = np.random.default_rng([zlib.crc32(name.encode()), seed]).standard_normal(out[name].shape)
        drawn = base * np.exp(spread * noise) if base else spread * noise
        out[name] = jnp.asarray(drawn.astype(out[name].dtype))
    for name, factor in factors.items():
        out[name] = (out[name] * factor).astype(out[name].dtype)
    return out
```

```python
from contextlib import ExitStack

import concourse.bass as bass
from concourse import mybir

F32 = mybir.dt.float32
I32 = mybir.dt.int32
ALU = mybir.AluOpType
ACT = mybir.ActivationFunctionType
AX_X = mybir.AxisListType.X

P = 128
B = 16
D = 256
KT = D // P
EPS = 1e-5
RSQRT_BITS = float(0x5F3759DF - 0x400000)
NEWTON = 3

NMIX, PLR, GLR = 5, 32, 64
KD, VD, NH_A = 128, 256, 4
DK_A, DV_A = KD // NH_A, VD // NH_A
CHUNK = 32
HALVES = [64, 32, 16, 8, 4, 2, 1]
NL = len(HALVES)

H, DH = 16, 64
HD = H * DH
SB, PAR, J = 8, 2, 8
PAIRS = 4
NG = SB * J // PAIRS

NE, NH_C = 4, 8
NTE = P // NE
DH_C = D // NH_C
WIDTH = [D >> e for e in range(NE)]

LAG_A, LAG_B, LAG_C = 0, 1, 2


class Signal:

    def __init__(self, sem, lag, per):
        self.sem, self.lag, self.per = sem, lag, per

    def now(self, step, k=None):
        return (step - self.lag) * self.per + (self.per if k is None else k)

    def before(self, step):
        return (step - self.lag) * self.per


def decoder_layer(nc, a, out):
    ctx = ExitStack()
    with ctx:
        def sb(name, shape, dt=F32):
            return ctx.enter_context(nc.sbuf_tensor(name, shape, dt))

        def psum(name, shape):
            return ctx.enter_context(nc.psum_tensor(name, shape, F32))

        def sig(name, lag, per=1):
            return Signal(ctx.enter_context(nc.semaphore(name)), lag, per)

        w_x0 = sb("w_x0", [P, KT, NMIX * PLR])
        w_mix = sb("w_mix", [P, NMIX, D])
        w_r = sb("w_r", [P, KT, KD])
        w_k = sb("w_k", [P, KT, KD])
        w_v = sb("w_v", [P, KT, VD])
        w_wa = sb("w_wa", [P, KT, GLR])
        w_ga = sb("w_ga", [P, KT, GLR])
        w_wgb = sb("w_wgb", [P, VD])
        w_oa = sb("w_oa", [P, KT, D])
        mu0 = sb("mu0", [P, KT])
        x_bias = sb("x_bias", [P, NMIX, KT])
        wb = sb("wb", [P, 1])
        bonus = sb("bonus", [P, 1])
        gb_bc = sb("gb_bc", [P, VD])
        lng_bc = sb("lng_bc", [P, VD])
        lnb_bc = sb("lnb_bc", [P, VD])
        w_q = sb("w_q", [P, KT, HD])
        w_kb = sb("w_kb", [P, KT, HD])
        w_vb = sb("w_vb", [P, KT, HD])
        w_ob = sb("w_ob", [P, J, D])
        bq = sb("bq", [P, H // 2])
        bk = sb("bk", [P, H // 2])
        bv_bc = sb("bv_bc", [P, HD])
        bo_bc = sb("bo_bc", [P, D])
        w_qc = sb("w_qc", [P, KT, D])
        w_kc = sb("w_kc", [P, KT, D])
        w_vc = sb("w_vc", [P, KT, D])
        w_oc = sb("w_oc", [P, KT, D])
        norm_w = sb("norm_w", [P, KT])
        norm_b = sb("norm_b", [P, KT])
        qb_c = sb("qb_c", [P, KT])
        kb_c = sb("kb_c", [P, KT])
        vb_bc = sb("vb_bc", [P, D])
        ob_valid = sb("ob_valid", [P, D])
        ident = sb("ident", [P, P])
        zeros = sb("zeros", [P, P])
        three_halves = sb("three_halves", [P, 1])
        level_mask = sb("level_mask", [P, NL, 2, P // 2], I32)
        head_ones = sb("head_ones", [P, NH_A])
        par_mask = sb("par_mask", [P, PAR])
        chunk_keep = sb("chunk_keep", [P, P])

        x_in = sb("x_in", [P, D])
        a_xn = sb("a_xn", [P, D])
        a_xT = sb("a_xT", [P, KT, P + 1])
        delta = sb("delta", [P, KT, P])
        z0 = sb("z0", [P, KT, P])
        xx = sb("xx", [P, 2, P])
        zb = sb("zb", [P, NMIX, KT, P])
        ud = sb("ud", [P, NMIX, KT, P])
        xv = sb("xv", [P, NMIX, KT, P])
        wg = sb("wg", [P, P])
        qT = sb("qT", [P, P]); kT = sb("kT", [P, P])
        v_a = sb("v_a", [P, VD])
        g_a = sb("g_a", [P, VD]); g_e = sb("g_e", [P, VD]); g_1 = sb("g_1", [P, VD]); g_r = sb("g_r", [P, VD])
        gate = sb("gate", [P, VD]); gate_g = sb("gate_g", [P, VD]); gate_b = sb("gate_b", [P, VD])
        nw = sb("nw", [P, P]); c_in = sb("c_in", [P, P]); c_ex = sb("c_ex", [P, P]); c_rest = sb("c_rest", [P, P])
        decay = sb("decay", [P, NL, P]); edec = sb("edec", [P, NL, P])
        f_q = sb("f_q", [P, NL, P]); f_k = sb("f_k", [P, NL, P])
        quk = sb("quk", [P, P]); dterm = sb("dterm", [P, NH_A])
        attT = sb("attT", [P, NH_A, P])
        dv = sb("dv", [P, VD]); o_a = sb("o_a", [P, VD])
        o_n = sb("o_n", [P, VD]); o_g = sb("o_g", [P, VD]); o_f = sb("o_f", [P, VD])
        o_T = sb("o_T", [P, KT, P])
        x1 = sb("x1", [P, D])

        ctxT = sb("ctxT", [P, KT, P])
        b_xn = sb("b_xn", [P, D])
        b_xT = sb("b_xT", [P, KT, P])
        x1_bo = sb("x1_bo", [P, D])
        q_blk = sb("q_blk", [P, SB, J, PAR, H])
        k_st = sb("k_st", [P, SB, J, H])
        v_tok = sb("v_tok", [P, H, DH])
        v_g = sb("v_g", [P, NG, DH])
        s_d = sb("s_d", [P, NG, H])
        s_mx = sb("s_mx", [P, NG]); s_sh = sb("s_sh", [P, NG, H]); s_e = sb("s_e", [P, NG, H])
        s_sum = sb("s_sum", [P, NG]); s_r = sb("s_r", [P, NG]); s_rm = sb("s_rm", [P, NG, PAR])
        p_m = sb("p_m", [P, NG, PAR, H])
        p_T = sb("p_T", [P, NG, PAIRS, PAR, H])
        o_B = sb("o_B", [P, J, H, SB])
        x2 = sb("x2", [P, D])

        x3 = sb("x3", [P, D])
        c_xn = sb("c_xn", [P, D])
        x23 = sb("x23", [P, D]); res = sb("res", [P, D])
        c_xT = sb("c_xT", [P, KT, P])
        q_c = sb("q_c", [P, KT, P])
        k_blk = sb("k_blk", [P, KT, 4, P])
        v_c = sb("v_c", [P, D])
        c_mx = sb("c_mx", [P, NH_C]); c_nm = sb("c_nm", [P, NH_C])
        c_e = sb("c_e", [P, NH_C, P]); c_sum = sb("c_sum", [P, NH_C]); c_r = sb("c_r", [P, NH_C])
        c_eT = sb("c_eT", [P, NH_C, P])
        c_o = sb("c_o", [P, NH_C, DH_C])
        c_oT = sb("c_oT", [P, KT, P])

        pA = psum("pA", [P, 2, 512])
        pC = psum("pC", [P, 2, 512])
        pB = psum("pB", [P, 2, 1024])

        loaded = sig("loaded", 0); zeroed = sig("zeroed", 0); made = sig("made", 0)
        MADE = 7 + NL * 5 + PAR * (3 + PAIRS)
        A, Bl, C = LAG_A, LAG_B, LAG_C
        x_loaded = sig("x_loaded", A, 16)
        a_normed = sig("a_normed", A)
        a_turned = sig("a_turned", A); a_xT_ready = sig("a_xT_ready", A)
        delta_ready = sig("delta_ready", A); z0_ready = sig("z0_ready", A, 2)
        xx_summed = sig("xx_summed", A); xx_ready = sig("xx_ready", A, 2)
        zb_ready = sig("zb_ready", A, NMIX * KT)
        mix_summed = sig("mix_summed", A, 3); ud_ready = sig("ud_ready", A, 3); zb_x = sig("zb_x", A, 3); xv_ready = sig("xv_ready", A, 3)
        rk_summed = sig("rk_summed", A); v_summed = sig("v_summed", A); wg_ready = sig("wg_ready", A)
        w_summed = sig("w_summed", A); g_summed = sig("g_summed", A)
        rk_ready = sig("rk_ready", A, 2); v_ready = sig("v_ready", A)
        w_exp = sig("w_exp", A); g_ready = sig("g_ready", A); g_exp = sig("g_exp", A)
        g_plus1 = sig("g_plus1", A); g_recip = sig("g_recip", A); gate_ready = sig("gate_ready", A); gates_ready = sig("gates_ready", A, 2)
        c_in_ready = sig("c_in_ready", A); c_parts = sig("c_parts", A, 2)
        decay_dve = sig("decay_dve", A, 12); decay_pool = sig("decay_pool", A, 4)
        edec_ready = sig("edec_ready", A); fq_ready = sig("fq_ready", A); fk_ready = sig("fk_ready", A)
        quk_ready = sig("quk_ready", A); att_summed = sig("att_summed", A, 2); att_kept = sig("att_kept", A, 2 * NL)
        dterm_ready = sig("dterm_ready", A); dv_ready = sig("dv_ready", A)
        oa_summed = sig("oa_summed", A); oa_ready = sig("oa_ready", A)
        o_normed = sig("o_normed", A)
        o_scaled = sig("o_scaled", A); o_final = sig("o_final", A); o_turned = sig("o_turned", A); oT_ready = sig("oT_ready", A)
        ya_summed = sig("ya_summed", A); x1_ready = sig("x1_ready", A)

        ctx_loaded = sig("ctx_loaded", Bl, 16)
        b_normed = sig("b_normed", Bl)
        b_turned = sig("b_turned", Bl); b_xT_ready = sig("b_xT_ready", Bl); x1bo_ready = sig("x1bo_ready", Bl)
        vb_summed = sig("vb_summed", Bl); vb_ready = sig("vb_ready", Bl); vg_moved = sig("vg_moved", Bl, 16 * NG)
        kb_summed = sig("kb_summed", Bl); kb_ready = sig("kb_ready", Bl); qb_summed = sig("qb_summed", Bl); qb_ready = sig("qb_ready", Bl)
        s_summed = sig("s_summed", Bl); s_dense = sig("s_dense", Bl); s_max = sig("s_max", Bl); s_shift = sig("s_shift", Bl)
        s_exp = sig("s_exp", Bl); s_total = sig("s_total", Bl); s_recip = sig("s_recip", Bl); s_scale = sig("s_scale", Bl)
        p_masked = sig("p_masked", Bl); p_turned = sig("p_turned", Bl)
        ob_summed = sig("ob_summed", Bl); ob_ready = sig("ob_ready", Bl)
        yb_summed = sig("yb_summed", Bl); x2_ready = sig("x2_ready", Bl)

        x3_ready = sig("x3_ready", C)
        c_normed = sig("c_normed", C)
        x23_ready = sig("x23_ready", C); res_begun = sig("res_begun", C)
        c_turned = sig("c_turned", C); c_xT_ready = sig("c_xT_ready", C)
        qk_summed = sig("qk_summed", C); vc_summed = sig("vc_summed", C)
        qc_ready = sig("qc_ready", C, 2); kc_ready = sig("kc_ready", C); vc_ready = sig("vc_ready", C)
        sc_summed = sig("sc_summed", C); sc_max = sig("sc_max", C); sc_nmax = sig("sc_nmax", C); sc_exp = sig("sc_exp", C)
        pc_turned = sig("pc_turned", C); pc_ready = sig("pc_ready", C); sc_recip = sig("sc_recip", C)
        oc_summed = sig("oc_summed", C); oc_ready = sig("oc_ready", C); oc_turned = sig("oc_turned", C); ocT_ready = sig("ocT_ready", C)
        yc_summed = sig("yc_summed", C); res_ready = sig("res_ready", C, NE); stored = sig("stored", C, 16)

        class Norm:

            def __init__(self, name, lag):
                self.st, self.mv = sb(name + "_st", [P, 6]), sb(name + "_mv", [P, 2])
                self.v, self.y, self.t = (sb(f"{name}_{x}", [P, 1]) for x in "vyt")
                self.bits = sb(name + "_bits", [P, 1], I32)
                self.stats, self.aggr = sig(name + "_stats", lag), sig(name + "_aggr", lag)
                self.var_eps, self.halved = sig(name + "_var_eps", lag), sig(name + "_halved", lag)
                self.guessed, self.newton = sig(name + "_guessed", lag), sig(name + "_newton", lag, 4 * NEWTON)

        norm_a, norm_of_b, norm_c, norm_d, norm_o = (Norm(*x) for x in (
            ("norm_a", A), ("norm_of_b", Bl), ("norm_c", C), ("norm_d", C), ("norm_o", A)))

        block = ctx.enter_context(nc.Block())

        def wait_apart(engine, sem, value):
            if not isinstance(value, int):
                value = engine.to_reg(value)
            engine.wait_ge(loaded.sem, ALL_LOADED)
            engine.wait_ge(sem, value)

        def run(engine, body):
            steps = B + LAG_C
            for step in range(LAG_C + 1):
                body(step, step >= LAG_A, step >= LAG_B, step >= LAG_C)
            with engine.Fori(LAG_C + 1, B) as step:
                body(step, True, True, True)
            for step in range(B, steps):
                body(step, False, step - LAG_B < B, step - LAG_C < B)

        resident = [
            (w_x0[:], a["Wx0"].rearrange("(k p) n -> p k n", p=P)),
            (w_mix[0:PLR, NMIX - 1, :], a["Wx2"][(NMIX - 1) * PLR:NMIX * PLR, :]),
            (w_r[:], a["rW"].rearrange("(k p) n -> p k n", p=P)),
            (w_k[:], a["kW"].rearrange("(k p) n -> p k n", p=P)),
            (w_v[:], a["vW"].rearrange("(k p) n -> p k n", p=P)),
            (w_wa[:], a["wA"].rearrange("(k p) n -> p k n", p=P)),
            (w_ga[:], a["gA"].rearrange("(k p) n -> p k n", p=P)),
            (w_wgb[0:GLR, 0:KD], a["wB"]), (w_wgb[GLR:2 * GLR, :], a["gB"]),
            (w_oa[:], a["oWa"].rearrange("(k p) n -> p k n", p=P)),
            (mu0[:], a["mu0"]), (x_bias[:], a["x_bias"].rearrange("p (i k) -> p i k", k=KT)),
            (wb[:], a["wb"]), (bonus[:], a["bonus"]),
            (gb_bc[:], a["gb"].to_broadcast([P, VD])),
            (lng_bc[:], a["ln_g"].to_broadcast([P, VD])), (lnb_bc[:], a["ln_b"].to_broadcast([P, VD])),
            (w_vb[:], a["Wv"].rearrange("(k p) n -> p k n", p=P)),
            (w_kb[:], a["Wk"].rearrange("(k p) n -> p k n", p=P)),
            (w_q[:], a["Wq"].rearrange("(k p) n -> p k n", p=P)),
            (w_ob[:], a["Wo"].rearrange("(j p) n -> p j n", p=P)),
            (bq[:], a["bq"]), (bk[:], a["bk"]),
            (bv_bc[:], a["bv"].to_broadcast([P, HD])), (bo_bc[:], a["bo"].to_broadcast([P, D])),
            (w_qc[:], a["q_w"].rearrange("(k p) n -> p k n", p=P)),
            (w_kc[:], a["k_w"].rearrange("(k p) n -> p k n", p=P)),
            (w_vc[:], a["v_w"].rearrange("(k p) n -> p k n", p=P)),
            (w_oc[:], a["o_w"].rearrange("(k p) n -> p k n", p=P)),
            (norm_w[:], a["norm_w"]), (norm_b[:], a["norm_b"]), (qb_c[:], a["q_b"]), (kb_c[:], a["k_b"]),
            (vb_bc[:], a["v_b"].to_broadcast([P, D])),
        ]
        into_zeroed = [(w_mix[i * PLR:(i + 1) * PLR, i, :], a["Wx2"][i * PLR:(i + 1) * PLR, :]) for i in range(NMIX - 1)]
        into_zeroed += [(ob_valid[e * NTE:(e + 1) * NTE, 0:WIDTH[e]], a["o_b"][:, 0:WIDTH[e]].to_broadcast([NTE, WIDTH[e]]))
                        for e in range(NE)]
        ALL_LOADED = 16 * (len(resident) + len(into_zeroed))
        zero_fill = [attT, q_blk, p_T, c_xT, k_blk, c_oT, w_mix[:, 0:NMIX - 1, :], ob_valid, zeros, ident,
                     a_xT, head_ones, par_mask]

        @block.sync
        def _(sp):
            for dst, src in resident:
                sp.dma_start(dst, src).then_inc(loaded.sem, 16)
            sp.wait_ge(zeroed.sem, len(zero_fill))
            for dst, src in into_zeroed:
                sp.dma_start(dst, src).then_inc(loaded.sem, 16)

            def body(it, in_a, in_b, in_c):
                if in_b:
                    sp.wait_ge(kb_summed.sem, kb_summed.before(it))
                    sp.dma_start(ctxT[:], a["ctxT"][it - LAG_B].rearrange("(k p) t -> p k t", p=P)).then_inc(ctx_loaded.sem, 16)
                if in_a:
                    sp.wait_ge(x1_ready.sem, x1_ready.before(it))
                    sp.dma_start(x_in[:], a["x"][it - LAG_A]).then_inc(x_loaded.sem, 16)
                if in_b:
                    sp.wait_ge(vb_ready.sem, vb_ready.now(it))
                    sp.wait_ge(ob_summed.sem, ob_summed.before(it))
                    for g in range(NG):
                        sp.dma_start(v_g[:, g, :], v_tok[g:P:NG, :, :]).then_inc(vg_moved.sem, 16)
                if in_c:
                    sp.wait_ge(res_ready.sem, res_ready.now(it))
                    sp.dma_start(out[it - LAG_C], res[:]).then_inc(stored.sem, 16)

            run(sp, body)
            sp.wait_ge(stored.sem, 16 * B)

        @block.gpsimd
        def _(pool):
            for t in zero_fill:
                nc.gpsimd.memset(t if isinstance(t, bass.AP) else t[:], 0.0).then_inc(zeroed.sem, 1)
            pool.wait_ge(zeroed.sem, len(zero_fill))
            count = [0]

            def step_(ins):
                count[0] += 1
                ins.then_inc(made.sem, 1)
                pool.wait_ge(made.sem, count[0])

            step_(nc.gpsimd.affine_select(out=ident[:], in_=ident[:], compare_op=ALU.not_equal, fill=1.0, base=0,
                                          pattern=[[-1, P]], channel_multiplier=1))
            step_(nc.gpsimd.memset(head_ones[:], 1.0))
            step_(nc.gpsimd.affine_select(out=head_ones[:], in_=head_ones[:], compare_op=ALU.is_ge, fill=0.0, base=0,
                                          pattern=[[-DK_A, NH_A]], channel_multiplier=1))
            step_(nc.gpsimd.affine_select(out=head_ones[:], in_=head_ones[:], compare_op=ALU.is_ge, fill=0.0,
                                          base=DK_A - 1, pattern=[[DK_A, NH_A]], channel_multiplier=-1))
            step_(nc.gpsimd.memset(three_halves[:], 1.5))
            step_(nc.gpsimd.memset(chunk_keep[:], 1.0))
            step_(nc.gpsimd.memset(chunk_keep[:].rearrange("p (c t) -> p c t", t=CHUNK)[:, :, 0:1], 0.0))
            for l, s in enumerate(HALVES):
                m = zeros[:, 0:P // 2].rearrange("p (b r) -> p b r", r=s)
                n = P // (2 * s)
                step_(nc.gpsimd.memset(zeros[:, 0:P // 2], 1.0))
                step_(nc.gpsimd.affine_select(out=m, in_=m, compare_op=ALU.is_ge, fill=0.0, base=0,
                                              pattern=[[-2 * s, n], [0, s]], channel_multiplier=1))
                step_(nc.gpsimd.affine_select(out=m, in_=m, compare_op=ALU.is_ge, fill=0.0, base=s - 1,
                                              pattern=[[2 * s, n], [0, s]], channel_multiplier=-1))
                for h in range(2):
                    step_(nc.gpsimd.tensor_copy(level_mask[:, l, h, :], zeros[:, 0:P // 2]))
            for par in range(PAR):
                m = zeros[:, 0:PAIRS]
                step_(nc.gpsimd.memset(m, 1.0))
                step_(nc.gpsimd.affine_select(out=m, in_=m, compare_op=ALU.is_ge, fill=0.0, base=-par * H,
                                              pattern=[[-PAR * H, PAIRS]], channel_multiplier=1))
                step_(nc.gpsimd.affine_select(out=m, in_=m, compare_op=ALU.is_ge, fill=0.0, base=par * H + H - 1,
                                              pattern=[[PAR * H, PAIRS]], channel_multiplier=-1))
                for pair in range(PAIRS):
                    step_(nc.gpsimd.tensor_tensor(par_mask[:, par:par + 1], par_mask[:, par:par + 1],
                                                  m[:, pair:pair + 1], ALU.add))
            assert count[0] == MADE
            pool.wait_ge(loaded.sem, ALL_LOADED)

            def rstd_of(it, n):
                pool.wait_ge(n.guessed.sem, n.guessed.now(it))
                for r in range(NEWTON):
                    steps = ((n.t, n.y, n.y, ALU.mult), (n.t, n.t, n.v, ALU.mult),
                             (n.t, three_halves, n.t, ALU.subtract), (n.y, n.y, n.t, ALU.mult))
                    for k, (o, p0, p1, op) in enumerate(steps):
                        if r or k:
                            pool.wait_ge(n.newton.sem, n.newton.now(it, 4 * r + k))
                        nc.gpsimd.tensor_tensor(o[:], p0[:], p1[:], op).then_inc(n.newton.sem, 1)

            def body(it, in_a, in_b, in_c):
                if in_a:
                    rstd_of(it, norm_a)
                if in_b:
                    rstd_of(it, norm_of_b)
                if in_c:
                    rstd_of(it, norm_c)
                    rstd_of(it, norm_d)
                if in_b:
                    pool.wait_ge(x1_ready.sem, x1_ready.before(it))
                    pool.wait_ge(x2_ready.sem, x2_ready.before(it))
                    nc.gpsimd.tensor_tensor(x1_bo[:], x1[:], bo_bc[:], ALU.add).then_inc(x1bo_ready.sem, 1)
                if in_c:
                    pool.wait_ge(x3_ready.sem, x3_ready.now(it))
                    nc.gpsimd.tensor_tensor(x23[:], x2[:], x3[:], ALU.add).then_inc(x23_ready.sem, 1)
                    pool.wait_ge(x23_ready.sem, x23_ready.now(it))
                    pool.wait_ge(stored.sem, stored.before(it))
                    nc.gpsimd.tensor_tensor(res[:], x23[:], ob_valid[:], ALU.add).then_inc(res_begun.sem, 1)
                if in_a:
                    pool.wait_ge(delta_ready.sem, delta_ready.now(it))
                    wait_apart(pool, xv_ready.sem, xv_ready.before(it))
                    for i in range(NMIX):
                        for k in range(KT):
                            nc.gpsimd.tensor_scalar(zb[:, i, k, :], delta[:, k, :], x_bias[:, i, k:k + 1], None,
                                                    ALU.mult).then_inc(zb_ready.sem, 1)
                    wait_apart(pool, c_parts.sem, c_parts.now(it))
                    pool.wait_ge(edec_ready.sem, edec_ready.before(it))
                    for l, src, c in ((1, c_ex, 1), (1, c_ex, 3), (0, c_rest, 1), (0, c_ex, 2)):
                        nc.gpsimd.tensor_copy(decay[:, l, c * CHUNK:(c + 1) * CHUNK],
                                              src[:, c * CHUNK:(c + 1) * CHUNK]).then_inc(decay_pool.sem, 1)
                    pool.wait_ge(gate_ready.sem, gate_ready.now(it))
                    pool.wait_ge(o_final.sem, o_final.before(it))
                    nc.gpsimd.tensor_tensor(gate_g[:], gate[:], lng_bc[:], ALU.mult).then_inc(gates_ready.sem, 1)
                    nc.gpsimd.tensor_tensor(gate_b[:], gate[:], lnb_bc[:], ALU.mult).then_inc(gates_ready.sem, 1)
                    pool.wait_ge(edec_ready.sem, edec_ready.now(it))
                    pool.wait_ge(rk_ready.sem, rk_ready.now(it))
                    pool.wait_ge(att_summed.sem, att_summed.before(it))
                    nc.gpsimd.tensor_tensor(f_k[:], edec[:], kT[:].unsqueeze(1).to_broadcast([P, NL, P]),
                                            ALU.mult).then_inc(fk_ready.sem, 1)
                    rstd_of(it, norm_o)

            run(pool, body)

        @block.tensor
        def _(pe):
            pe.wait_ge(loaded.sem, ALL_LOADED)
            pe.wait_ge(made.sem, MADE)
            mm = nc.tensor.matmul

            def turn(out_, in_, signal):
                for k in range(KT):
                    last = nc.tensor.transpose(out_[:, k * P:(k + 1) * P], in_[:, k * P:(k + 1) * P], ident[:])
                last.then_inc(signal.sem, 1)

            def project(out_, lhs, rhs, n=KT):
                for k in range(n):
                    last = mm(out_, lhs(k), rhs(k), start=(k == 0), stop=(k == n - 1))
                return last

            def body(it, in_a, in_b, in_c):
                if in_b:
                    pe.wait_ge(ctx_loaded.sem, ctx_loaded.now(it))
                    pe.wait_ge(x2_ready.sem, x2_ready.before(it))
                    for n in range(2):
                        for k in range(KT):
                            last = mm(pB[:, 0, n * 512:(n + 1) * 512], ctxT[:, k, :],
                                      w_vb[:, k, n * 512:(n + 1) * 512], start=(k == 0), stop=(k == KT - 1))
                    last.then_inc(vb_summed.sem, 1)
                if in_a:
                    pe.wait_ge(a_normed.sem, a_normed.now(it))
                    pe.wait_ge(x1_ready.sem, x1_ready.before(it))
                    turn(pA[:, 0, :], a_xn, a_turned)
                if in_b:
                    pe.wait_ge(b_normed.sem, b_normed.now(it))
                    pe.wait_ge(ob_ready.sem, ob_ready.before(it))
                    turn(pB[:, 1, :], b_xn, b_turned)
                if in_c:
                    pe.wait_ge(c_normed.sem, c_normed.now(it))
                    pe.wait_ge(res_ready.sem, res_ready.before(it))
                    turn(pC[:, 0, :], c_xn, c_turned)
                if in_b:
                    pe.wait_ge(vb_ready.sem, vb_ready.now(it))
                    for c in range(H // 2):
                        last = project(pB[:, 0, c * P:(c + 1) * P], lambda k: w_kb[:, k, c * P:(c + 1) * P],
                                       lambda k: ctxT[:, k, :])
                    last.then_inc(kb_summed.sem, 1)
                if in_a:
                    pe.wait_ge(z0_ready.sem, z0_ready.now(it))
                    project(pA[:, 1, 0:P], lambda k: w_x0[:, k, 0:P], lambda k: z0[:, k, :])
                    project(pA[0:PLR, 1, P:2 * P], lambda k: w_x0[:, k, P:P + PLR], lambda k: z0[:, k, :])\
                        .then_inc(xx_summed.sem, 1)
                if in_c:
                    pe.wait_ge(c_xT_ready.sem, c_xT_ready.now(it))
                    for w, o in ((w_qc, pC[:, 1, 0:256]), (w_kc, pC[:, 1, 256:512])):
                        for m in range(KT):
                            mm(o[:, m * P:(m + 1) * P], w[:, 0, m * P:(m + 1) * P], c_xT[:, 0, :], start=True, stop=False)
                            last = mm(o[:, m * P:m * P + NTE], w[:, 1, m * P:(m + 1) * P], c_xT[:, 1, 0:NTE],
                                      start=False, stop=True)
                    last.then_inc(qk_summed.sem, 1)
                    project(pC[:, 0, 256:512], lambda k: c_xT[:, k, :], lambda k: w_vc[:, k, :]).then_inc(vc_summed.sem, 1)
                if in_b:
                    pe.wait_ge(b_xT_ready.sem, b_xT_ready.now(it))
                    for c in range(H // 2):
                        last = project(pB[:, 1, c * P:(c + 1) * P], lambda k: w_q[:, k, c * P:(c + 1) * P],
                                       lambda k: b_xT[:, k, :])
                    last.then_inc(qb_summed.sem, 1)
                if in_a:
                    pe.wait_ge(xx_ready.sem, xx_ready.now(it))
                    for r, (bank, mixes) in enumerate(((0, (0, 1)), (1, (2, 3)), (0, (4,)))):
                        if r == 2:
                            pe.wait_ge(ud_ready.sem, ud_ready.now(it, 1))
                        for n, i in enumerate(mixes):
                            for k in range(KT):
                                col = (n * KT + k) * P
                                if i < NMIX - 1:
                                    last = mm(pA[:, bank, col:col + P], w_mix[:, i, k * P:(k + 1) * P], xx[:, 0, :],
                                              start=True, stop=True)
                                else:
                                    last = mm(pA[:, bank, col:col + P], w_mix[0:PLR, i, k * P:(k + 1) * P],
                                              xx[0:PLR, 1, :], start=True, stop=True)
                        last.then_inc(mix_summed.sem, 1)
                if in_c:
                    pe.wait_ge(qc_ready.sem, qc_ready.now(it))
                    pe.wait_ge(kc_ready.sem, kc_ready.now(it))
                    pe.wait_ge(vc_ready.sem, vc_ready.now(it))
                    for m in range(KT):
                        last = mm(pC[:, m, :], q_c[:, m, :], k_blk[:, m, :, :], start=True, stop=True)
                    last.then_inc(sc_summed.sem, 1)
                if in_b:
                    pe.wait_ge(kb_ready.sem, kb_ready.now(it))
                    pe.wait_ge(qb_ready.sem, qb_ready.now(it))
                    for g in range(NG):
                        s, jh = g // 2, g % 2
                        last = mm(pB[:, 0, g * 64:(g + 1) * 64], q_blk[:, s, jh * PAIRS:(jh + 1) * PAIRS, :, :],
                                  k_st[:, s, jh * PAIRS:(jh + 1) * PAIRS, :], start=True, stop=True)
                    last.then_inc(s_summed.sem, 1)
                if in_a:
                    pe.wait_ge(xv_ready.sem, xv_ready.now(it))
                    project(pA[:, 1, 0:P], lambda k: w_r[:, k, :], lambda k: xv[:, 0, k, :])
                    project(pA[:, 1, P:2 * P], lambda k: w_k[:, k, :], lambda k: xv[:, 2, k, :])
                    project(pA[0:GLR, 1, 2 * P:3 * P], lambda k: w_wa[:, k, :], lambda k: xv[:, 1, k, :])
                    project(pA[GLR:P, 1, 2 * P:3 * P], lambda k: w_ga[:, k, :], lambda k: xv[:, 4, k, :])\
                        .then_inc(rk_summed.sem, 1)
                    project(pA[:, 0, 0:VD], lambda k: xv[:, 3, k, :], lambda k: w_v[:, k, :]).then_inc(v_summed.sem, 1)
                if in_c:
                    pe.wait_ge(sc_exp.sem, sc_exp.now(it))
                    for h in range(NH_C):
                        last = nc.tensor.transpose(pC[:, h // 4, (h % 4) * P:(h % 4 + 1) * P], c_e[:, h, :], ident[:])
                    last.then_inc(pc_turned.sem, 1)
                if in_a:
                    pe.wait_ge(wg_ready.sem, wg_ready.now(it))
                    pe.wait_ge(rk_ready.sem, rk_ready.now(it))
                    mm(pA[:, 1, 3 * P:4 * P], w_wgb[0:GLR, 0:KD], wg[0:GLR, :], start=True, stop=True)\
                        .then_inc(w_summed.sem, 1)
                    pe.wait_ge(v_ready.sem, v_ready.now(it))
                    mm(pA[:, 0, VD:2 * VD], wg[GLR:P, :], w_wgb[GLR:P, :], start=True, stop=True)\
                        .then_inc(g_summed.sem, 1)
                if in_c:
                    pe.wait_ge(pc_ready.sem, pc_ready.now(it))
                    for h in range(NH_C):
                        last = mm(pC[:, 0, h * DH_C:(h + 1) * DH_C], c_eT[:, h, :], v_c[:, h * DH_C:(h + 1) * DH_C],
                                  start=True, stop=True)
                    last.then_inc(oc_summed.sem, 1)
                if in_b:
                    pe.wait_ge(p_turned.sem, p_turned.now(it))
                    pe.wait_ge(vg_moved.sem, vg_moved.now(it))
                    for g in range(NG):
                        for par in range(PAR):
                            last = mm(pB[par * DH:(par + 1) * DH, 1, g * 64:(g + 1) * 64], v_g[:, g, :],
                                      p_T[:, g, :, par, :], start=True, stop=True)
                    last.then_inc(ob_summed.sem, 1)
                if in_c:
                    pe.wait_ge(oc_ready.sem, oc_ready.now(it))
                    turn(pC[:, 1, :], c_o[:].rearrange("p h d -> p (h d)"), oc_turned)
                if in_a:
                    for r in range(2):
                        if r == 0:
                            pe.wait_ge(fq_ready.sem, fq_ready.now(it))
                            pe.wait_ge(fk_ready.sem, fk_ready.now(it))
                            pe.wait_ge(w_exp.sem, w_exp.now(it))
                            pe.wait_ge(g_ready.sem, g_ready.now(it))
                            pe.wait_ge(rk_ready.sem, rk_ready.now(it))
                            pe.wait_ge(v_ready.sem, v_ready.now(it))
                        else:
                            pe.wait_ge(att_kept.sem, att_kept.now(it, NL))
                        for l, s in enumerate(HALVES):
                            for b in range(2):
                                h = 2 * r + b
                                rows = slice(h * DK_A, (h + 1) * DK_A)
                                upper = f_q[rows, l, :].rearrange("p (n u s) -> p n u s", u=2, s=s)[:, :, 1, :]
                                last = mm(pA[:, b, l * 64:(l + 1) * 64], f_k[rows, l, :], upper,
                                          start=True, stop=True, tile_position=(h * DK_A, 0))
                        if r == 0:
                            pe.wait_ge(quk_ready.sem, quk_ready.now(it))
                            last = mm(pA[:, 1, 448:448 + NH_A], quk[:], head_ones[:], start=True, stop=True)
                        last.then_inc(att_summed.sem, 1)
                        if r == 0 and in_c:
                            pe.wait_ge(ocT_ready.sem, ocT_ready.now(it))
                            project(pC[:, 0, 256:512], lambda k: c_oT[:, k, :], lambda k: w_oc[:, k, :])\
                                .then_inc(yc_summed.sem, 1)
                    pe.wait_ge(att_kept.sem, att_kept.now(it))
                    for h in range(NH_A):
                        last = mm(pA[:, 0, h * DV_A:(h + 1) * DV_A], attT[:, h, :], v_a[:, h * DV_A:(h + 1) * DV_A],
                                  start=True, stop=True)
                    last.then_inc(oa_summed.sem, 1)
                elif in_c:
                    pe.wait_ge(ocT_ready.sem, ocT_ready.now(it))
                    project(pC[:, 0, 256:512], lambda k: c_oT[:, k, :], lambda k: w_oc[:, k, :]).then_inc(yc_summed.sem, 1)
                if in_b:
                    pe.wait_ge(ob_ready.sem, ob_ready.now(it))
                    pe.wait_ge(s_dense.sem, s_dense.now(it))
                    project(pB[:, 0, 0:D], lambda j: o_B[:, j, :, :], lambda j: w_ob[:, j, :], J).then_inc(yb_summed.sem, 1)
                if in_a:
                    pe.wait_ge(o_final.sem, o_final.now(it))
                    turn(pA[:, 1, :], o_f, o_turned)
                    pe.wait_ge(oT_ready.sem, oT_ready.now(it))
                    project(pA[:, 0, 256:512], lambda k: o_T[:, k, :], lambda k: w_oa[:, k, :]).then_inc(ya_summed.sem, 1)

            run(pe, body)

        @block.scalar
        def _(act):
            act.wait_ge(loaded.sem, ALL_LOADED)
            act.wait_ge(zeroed.sem, len(zero_fill))
            go = nc.scalar.activation

            def valid(dst, src, scale, bias):
                for k in range(KT):
                    e0 = 0
                    while e0 < NE and WIDTH[e0] > k * P:
                        rows = min(P, WIDTH[e0] - k * P)
                        e1 = e0
                        while e1 < NE and WIDTH[e1] > k * P and min(P, WIDTH[e1] - k * P) == rows:
                            e1 += 1
                        cols = slice(e0 * NTE, e1 * NTE)
                        psl = src[0:rows, k * P + e0 * NTE:k * P + e1 * NTE]
                        if scale is None:
                            last = go(dst[0:rows, k, cols], psl, ACT.Copy)
                        else:
                            last = go(dst[0:rows, k, cols], psl, ACT.Identity, scale=scale[0:rows, k:k + 1],
                                      bias=bias[0:rows, k:k + 1])
                        e0 = e1
                return last

            def body(it, in_a, in_b, in_c):
                if in_a:
                    act.wait_ge(a_turned.sem, a_turned.now(it))
                    act.wait_ge(z0_ready.sem, z0_ready.before(it))
                    go(a_xT[:, :, 1:P + 1], pA[:, 0, 0:2 * P].rearrange("p (k t) -> p k t", k=KT), ACT.Copy)\
                        .then_inc(a_xT_ready.sem, 1)
                if in_b:
                    act.wait_ge(b_turned.sem, b_turned.now(it))
                    go(b_xT[:], pB[:, 1, 0:2 * P].rearrange("p (k t) -> p k t", k=KT), ACT.Copy)\
                        .then_inc(b_xT_ready.sem, 1)
                if in_c:
                    act.wait_ge(c_turned.sem, c_turned.now(it))
                    valid(c_xT, pC[:, 0, :], norm_w, norm_b).then_inc(c_xT_ready.sem, 1)
                if in_a:
                    act.wait_ge(xx_summed.sem, xx_summed.now(it))
                    go(xx[:, 0, :], pA[:, 1, 0:P], ACT.Tanh).then_inc(xx_ready.sem, 1)
                    go(xx[0:PLR, 1, :], pA[0:PLR, 1, P:2 * P], ACT.Tanh).then_inc(xx_ready.sem, 1)
                if in_c:
                    act.wait_ge(qk_summed.sem, qk_summed.now(it))
                    for m in range(KT):
                        go(q_c[:, m, :], pC[:, 1, m * P:(m + 1) * P], ACT.Identity,
                           bias=qb_c[:, m:m + 1]).then_inc(qc_ready.sem, 1)
                    for m in range(KT):
                        for h in range(4):
                            rows = slice(h * DH_C, (h + 1) * DH_C)
                            last = go(k_blk[rows, m, h, :], pC[rows, 1, 256 + m * P:256 + (m + 1) * P], ACT.Identity,
                                      bias=kb_c[rows, m:m + 1])
                    last.then_inc(kc_ready.sem, 1)
                if in_b:
                    act.wait_ge(s_summed.sem, s_summed.now(it))
                    act.wait_ge(s_shift.sem, s_shift.before(it))
                    for pair in range(PAIRS):
                        rows = slice(pair * 32, (pair + 1) * 32)
                        last = go(s_d[rows, :, :],
                                  pB[rows, 0, :].rearrange("p (g q h) -> p g q h", q=PAIRS, h=H)[:, :, pair, :],
                                  ACT.Copy, scale=float(DH) ** -0.5)
                    last.then_inc(s_dense.sem, 1)
                if in_c:
                    act.wait_ge(sc_nmax.sem, sc_nmax.now(it))
                    act.wait_ge(sc_recip.sem, sc_recip.before(it))
                    for h in range(NH_C):
                        last = go(c_e[:, h, :], pC[:, h // 4, (h % 4) * P:(h % 4 + 1) * P], ACT.Exp,
                                  scale=float(D) ** -0.5, bias=c_nm[:, h:h + 1], accum_out=c_sum[:, h:h + 1])
                    last.then_inc(sc_exp.sem, 1)
                if in_b:
                    act.wait_ge(s_shift.sem, s_shift.now(it))
                    act.wait_ge(p_masked.sem, p_masked.before(it))
                    go(s_e[:], s_sh[:], ACT.Exp).then_inc(s_exp.sem, 1)
                if in_a:
                    act.wait_ge(rk_summed.sem, rk_summed.now(it))
                    act.wait_ge(g_summed.sem, g_summed.before(it))
                    go(wg[:], pA[:, 1, 2 * P:3 * P], ACT.Tanh).then_inc(wg_ready.sem, 1)
                    act.wait_ge(quk_ready.sem, quk_ready.before(it))
                    act.wait_ge(fq_ready.sem, fq_ready.before(it))
                    act.wait_ge(fk_ready.sem, fk_ready.before(it))
                    go(qT[:], pA[:, 1, 0:P], ACT.Copy).then_inc(rk_ready.sem, 1)
                    go(kT[:], pA[:, 1, P:2 * P], ACT.Copy).then_inc(rk_ready.sem, 1)
                    act.wait_ge(w_summed.sem, w_summed.now(it))
                    act.wait_ge(c_parts.sem, c_parts.before(it))
                    go(nw[:], pA[:, 1, 3 * P:4 * P], ACT.Exp, bias=wb[:, 0:1]).then_inc(w_exp.sem, 1)
                if in_c:
                    act.wait_ge(pc_turned.sem, pc_turned.now(it))
                    act.wait_ge(oc_summed.sem, oc_summed.before(it))
                    go(c_eT[:], pC[:].rearrange("p b (h q) -> p (b h) q", q=P), ACT.Copy).then_inc(pc_ready.sem, 1)
                if in_a:
                    act.wait_ge(g_ready.sem, g_ready.now(it))
                    act.wait_ge(g_plus1.sem, g_plus1.before(it))
                    go(g_e[:], g_a[:], ACT.Exp, scale=-1.0).then_inc(g_exp.sem, 1)
                    act.wait_ge(decay_dve.sem, decay_dve.now(it))
                    act.wait_ge(decay_pool.sem, decay_pool.now(it))
                    go(edec[:], decay[:], ACT.Exp, scale=-1.0).then_inc(edec_ready.sem, 1)
                if in_b:
                    act.wait_ge(ob_summed.sem, ob_summed.now(it))
                    act.wait_ge(yb_summed.sem, yb_summed.before(it))
                    go(o_B[:].rearrange("p j h s -> p s (j h)"), pB[:, 1, :].rearrange("p (s n) -> p s n", s=SB),
                       ACT.Copy).then_inc(ob_ready.sem, 1)
                if in_c:
                    act.wait_ge(oc_turned.sem, oc_turned.now(it))
                    valid(c_oT, pC[:, 1, :], None, None).then_inc(ocT_ready.sem, 1)
                if in_a:
                    act.wait_ge(o_turned.sem, o_turned.now(it))
                    go(o_T[:], pA[:, 1, 0:2 * P].rearrange("p (k t) -> p k t", k=KT), ACT.Copy).then_inc(oT_ready.sem, 1)

            run(act, body)

        @block.vector
        def _(dve):
            v = nc.vector
            dve.wait_ge(loaded.sem, ALL_LOADED)
            dve.wait_ge(made.sem, MADE)

            def layernorm(it, src, dst, n, normed):
                v.bn_stats(n.st[:], src[:]).then_inc(n.stats.sem, 1)
                wait_apart(dve, n.stats.sem, n.stats.now(it))
                v.bn_aggr(n.mv[:], n.st[:]).then_inc(n.aggr.sem, 1)
                dve.wait_ge(n.aggr.sem, n.aggr.now(it))
                v.tensor_scalar(n.v[:], n.mv[:, 1:2], EPS, 0.5, ALU.add, ALU.mult).then_inc(n.var_eps.sem, 1)
                dve.wait_ge(n.var_eps.sem, n.var_eps.now(it))
                v.tensor_scalar(n.bits[:], n.v[:].bitcast(I32), 1, None, ALU.logical_shift_right).then_inc(n.halved.sem, 1)
                dve.wait_ge(n.halved.sem, n.halved.now(it))
                v.tensor_scalar(n.y[:].bitcast(I32), n.bits[:], -1.0, RSQRT_BITS, ALU.mult, ALU.add).then_inc(n.guessed.sem, 1)

            def normalise(it, src, dst, n, normed):
                dve.wait_ge(n.newton.sem, n.newton.now(it))
                v.tensor_scalar(dst[:], src[:], n.mv[:, 0:1], n.y[:, 0:1], ALU.subtract, ALU.mult).then_inc(normed.sem, 1)

            def q_spread(it):
                dve.wait_ge(qb_summed.sem, qb_summed.now(it))
                for hh in range(2):
                    rows = slice(hh * DH, (hh + 1) * DH)
                    for par in range(PAR):
                        src = pB[rows, 1, :].rearrange("p (c s q j) -> p s q j c", c=H // 2, s=SB, q=PAR)[:, :, par]
                        dst = q_blk[par * DH:(par + 1) * DH, :, :, par, hh::2]
                        bias = bq[rows].unsqueeze(1).unsqueeze(1).to_broadcast([DH, SB, J, H // 2])
                        last = v.tensor_tensor(dst, src, bias, ALU.add)
                last.then_inc(qb_ready.sem, 1)

            def k_spread(it):
                dve.wait_ge(kb_summed.sem, kb_summed.now(it))
                for hh in range(2):
                    rows = slice(hh * DH, (hh + 1) * DH)
                    for par in range(PAR):
                        src = pB[rows, 0, :].rearrange("p (c r q g) -> p g r q c", c=H // 2, r=PAIRS, q=PAR)[:, :, :, par]
                        dst = k_st[par * DH:(par + 1) * DH].rearrange("p s (j r) h -> p (s j) r h", r=PAIRS)[:, :, :, hh::2]
                        bias = bk[rows].unsqueeze(1).unsqueeze(1).to_broadcast([DH, NG, PAIRS, H // 2])
                        last = v.tensor_tensor(dst, src, bias, ALU.add)
                last.then_inc(kb_ready.sem, 1)

            def body(it, in_a, in_b, in_c):
                if in_a:
                    dve.wait_ge(x_loaded.sem, x_loaded.now(it))
                    layernorm(it, x_in, a_xn, norm_a, a_normed)
                if in_b:
                    dve.wait_ge(x1_ready.sem, x1_ready.before(it))
                    layernorm(it, x1, b_xn, norm_of_b, b_normed)
                if in_c:
                    dve.wait_ge(x2_ready.sem, x2_ready.before(it))
                    layernorm(it, x2, x3, norm_c, x3_ready)
                if in_b:
                    dve.wait_ge(b_turned.sem, b_turned.before(it))
                    normalise(it, x1, b_xn, norm_of_b, b_normed)
                if in_c:
                    dve.wait_ge(x23_ready.sem, x23_ready.before(it))
                    normalise(it, x2, x3, norm_c, x3_ready)
                    dve.wait_ge(x3_ready.sem, x3_ready.now(it))
                    layernorm(it, x3, c_xn, norm_d, c_normed)
                if in_a:
                    dve.wait_ge(a_turned.sem, a_turned.before(it))
                    normalise(it, x_in, a_xn, norm_a, a_normed)
                if in_c:
                    dve.wait_ge(c_turned.sem, c_turned.before(it))
                    normalise(it, x3, c_xn, norm_d, c_normed)
                if in_b:
                    dve.wait_ge(vb_summed.sem, vb_summed.now(it))
                    dve.wait_ge(vg_moved.sem, vg_moved.before(it))
                    v.tensor_tensor(v_tok[:].rearrange("p h d -> p (h d)"), pB[:, 0, :], bv_bc[:], ALU.add)\
                        .then_inc(vb_ready.sem, 1)
                if in_a:
                    dve.wait_ge(a_xT_ready.sem, a_xT_ready.now(it))
                    dve.wait_ge(zb_ready.sem, zb_ready.before(it))
                    v.tensor_tensor(delta[:], a_xT[:, :, 0:P], a_xT[:, :, 1:P + 1], ALU.subtract).then_inc(delta_ready.sem, 1)
                    dve.wait_ge(delta_ready.sem, delta_ready.now(it))
                    dve.wait_ge(xx_summed.sem, xx_summed.before(it))
                    for k in range(KT):
                        v.scalar_tensor_tensor(z0[:, k, :], delta[:, k, :], mu0[:, k:k + 1], a_xT[:, k, 1:P + 1],
                                               ALU.mult, ALU.add).then_inc(z0_ready.sem, 1)
                if in_b:
                    dve.wait_ge(s_summed.sem, s_summed.before(it))
                    k_spread(it)
                if in_c:
                    dve.wait_ge(vc_summed.sem, vc_summed.now(it))
                    dve.wait_ge(oc_summed.sem, oc_summed.before(it))
                    v.tensor_tensor(v_c[:], pC[:, 0, 256:512], vb_bc[:], ALU.add).then_inc(vc_ready.sem, 1)
                if in_b:
                    q_spread(it)
                if in_a:
                    dve.wait_ge(zb_ready.sem, zb_ready.now(it))
                    for r, (bank, i0, n) in enumerate(((0, 0, 2), (1, 2, 2), (0, 4, 1))):
                        dve.wait_ge(mix_summed.sem, mix_summed.now(it, r + 1))
                        d_b = delta[:].unsqueeze(1).to_broadcast([P, n, KT, P])
                        x_b = a_xT[:, :, 1:P + 1].unsqueeze(1).to_broadcast([P, n, KT, P])
                        src = pA[:, bank, 0:n * KT * P].rearrange("p (i k t) -> p i k t", k=KT, t=P)
                        v.tensor_tensor(ud[:, i0:i0 + n], src, d_b, ALU.mult).then_inc(ud_ready.sem, 1)
                        if r == 0 and in_c:
                            dve.wait_ge(sc_summed.sem, sc_summed.now(it))
                            v.reduce_max(c_mx[:], pC[:].rearrange("p b (h k) -> p (b h) k", k=P), AX_X).then_inc(sc_max.sem, 1)
                            dve.wait_ge(sc_max.sem, sc_max.now(it))
                            v.tensor_scalar(c_nm[:], c_mx[:], -float(D) ** -0.5, None, ALU.mult).then_inc(sc_nmax.sem, 1)
                    for r, (i0, n) in enumerate(((0, 2), (2, 2), (4, 1))):
                        x_b = a_xT[:, :, 1:P + 1].unsqueeze(1).to_broadcast([P, n, KT, P])
                        dve.wait_ge(ud_ready.sem, ud_ready.now(it, r + 1))
                        v.tensor_tensor(zb[:, i0:i0 + n], zb[:, i0:i0 + n], x_b, ALU.add).then_inc(zb_x.sem, 1)
                    for r, (i0, n) in enumerate(((0, 2), (2, 2), (4, 1))):
                        dve.wait_ge(zb_x.sem, zb_x.now(it, r + 1))
                        v.tensor_tensor(xv[:, i0:i0 + n], ud[:, i0:i0 + n], zb[:, i0:i0 + n], ALU.add).then_inc(xv_ready.sem, 1)
                elif in_c:
                    dve.wait_ge(sc_summed.sem, sc_summed.now(it))
                    v.reduce_max(c_mx[:], pC[:].rearrange("p b (h k) -> p (b h) k", k=P), AX_X).then_inc(sc_max.sem, 1)
                    dve.wait_ge(sc_max.sem, sc_max.now(it))
                    v.tensor_scalar(c_nm[:], c_mx[:], -float(D) ** -0.5, None, ALU.mult).then_inc(sc_nmax.sem, 1)
                if in_b:
                    dve.wait_ge(s_dense.sem, s_dense.now(it))
                    v.reduce_max(s_mx[:], s_d[:], AX_X).then_inc(s_max.sem, 1)
                    dve.wait_ge(s_max.sem, s_max.now(it))
                    v.tensor_tensor(s_sh[:], s_d[:], s_mx[:].unsqueeze(2).to_broadcast([P, NG, H]), ALU.subtract)\
                        .then_inc(s_shift.sem, 1)
                if in_a:
                    dve.wait_ge(v_summed.sem, v_summed.now(it))
                    v.tensor_copy(v_a[:], pA[:, 0, 0:VD]).then_inc(v_ready.sem, 1)
                if in_b:
                    dve.wait_ge(s_exp.sem, s_exp.now(it))
                    v.reduce_sum(s_sum[:], s_e[:], AX_X).then_inc(s_total.sem, 1)
                    dve.wait_ge(s_total.sem, s_total.now(it))
                    v.reciprocal(s_r[:], s_sum[:]).then_inc(s_recip.sem, 1)
                    dve.wait_ge(s_recip.sem, s_recip.now(it))
                    v.tensor_tensor(s_rm[:], s_r[:].unsqueeze(2).to_broadcast([P, NG, PAR]),
                                    par_mask[:].unsqueeze(1).to_broadcast([P, NG, PAR]), ALU.mult).then_inc(s_scale.sem, 1)
                    dve.wait_ge(s_scale.sem, s_scale.now(it))
                    v.tensor_tensor(p_m[:], s_e[:].unsqueeze(2).to_broadcast([P, NG, PAR, H]),
                                    s_rm[:].unsqueeze(3).to_broadcast([P, NG, PAR, H]), ALU.mult).then_inc(p_masked.sem, 1)
                    dve.wait_ge(p_masked.sem, p_masked.now(it))
                    dve.wait_ge(ob_summed.sem, ob_summed.before(it))
                    for pair in range(PAIRS):
                        rows = slice(pair * 32, (pair + 1) * 32)
                        last = v.transpose(p_T[rows, :, pair, :, :].rearrange("p g a h -> p g (a h)"),
                                           p_m[rows].rearrange("p g a h -> p g (a h)"))
                    last.then_inc(p_turned.sem, 1)
                if in_a:
                    dve.wait_ge(g_summed.sem, g_summed.now(it))
                    dve.wait_ge(gate_ready.sem, gate_ready.before(it))
                    v.tensor_tensor(g_a[:], pA[:, 0, VD:2 * VD], gb_bc[:], ALU.add).then_inc(g_ready.sem, 1)
                    dve.wait_ge(w_exp.sem, w_exp.now(it))
                    v.tensor_tensor_scan(c_in[:], chunk_keep[:], nw[:], 0.0, ALU.mult, ALU.add).then_inc(c_in_ready.sem, 1)
                    dve.wait_ge(c_in_ready.sem, c_in_ready.now(it))
                    dve.wait_ge(decay_pool.sem, decay_pool.before(it))
                    tot = c_in[:].rearrange("p (c t) -> p c t", t=CHUNK)[:, :, CHUNK - 1:CHUNK]
                    v.tensor_tensor(c_ex[:], c_in[:], nw[:], ALU.subtract).then_inc(c_parts.sem, 1)
                    v.tensor_tensor(c_rest[:].rearrange("p (c t) -> p c t", t=CHUNK), tot.to_broadcast([P, P // CHUNK, CHUNK]),
                                    c_in[:].rearrange("p (c t) -> p c t", t=CHUNK), ALU.subtract).then_inc(c_parts.sem, 1)
                    dve.wait_ge(c_parts.sem, c_parts.now(it))
                    dve.wait_ge(edec_ready.sem, edec_ready.before(it))
                    C_ = CHUNK
                    v.tensor_copy(decay[:, 1, :].rearrange("p (n u t) -> p n u t", u=2, t=C_)[:, :, 0, :],
                                  c_rest[:].rearrange("p (n u t) -> p n u t", u=2, t=C_)[:, :, 0, :]).then_inc(decay_dve.sem, 1)
                    v.tensor_scalar(decay[:, 0, 0:C_], c_rest[:, 0:C_], c_in[:, 2 * C_ - 1:2 * C_], None, ALU.add)\
                        .then_inc(decay_dve.sem, 1)
                    v.tensor_scalar(decay[:, 0, 3 * C_:], c_ex[:, 3 * C_:], c_in[:, 3 * C_ - 1:3 * C_], None, ALU.add)\
                        .then_inc(decay_dve.sem, 1)
                    for l in range(2, NL):
                        s = HALVES[l]
                        n = P // (2 * s)
                        view = lambda t: t.rearrange("p (n u s) -> p n u s", u=2, s=s)
                        ref = view(c_in[:])[:, :, 0, s - 1:s].to_broadcast([P, n, s])
                        ins = v.tensor_tensor(view(decay[:, l, :])[:, :, 1, :], view(c_ex[:])[:, :, 1, :], ref, ALU.subtract)
                        ins2 = v.tensor_tensor(view(decay[:, l, :])[:, :, 0, :], ref, view(c_in[:])[:, :, 0, :], ALU.subtract)
                        ins2.then_inc(decay_dve.sem, 2 if l > 2 else 1)
                    dve.wait_ge(rk_ready.sem, rk_ready.now(it))
                    dve.wait_ge(att_summed.sem, att_summed.before(it))
                    v.scalar_tensor_tensor(quk[:], qT[:], bonus[:, 0:1], kT[:], ALU.mult, ALU.mult).then_inc(quk_ready.sem, 1)
                    dve.wait_ge(g_exp.sem, g_exp.now(it))
                    v.tensor_scalar(g_1[:], g_e[:], 1.0, None, ALU.add).then_inc(g_plus1.sem, 1)
                    dve.wait_ge(edec_ready.sem, edec_ready.now(it))
                    v.tensor_tensor(f_q[:], edec[:], qT[:].unsqueeze(1).to_broadcast([P, NL, P]), ALU.mult)\
                        .then_inc(fq_ready.sem, 1)
                    dve.wait_ge(g_plus1.sem, g_plus1.now(it))
                    v.reciprocal(g_r[:], g_1[:]).then_inc(g_recip.sem, 1)
                    dve.wait_ge(g_recip.sem, g_recip.now(it))
                    dve.wait_ge(gates_ready.sem, gates_ready.before(it))
                    v.tensor_tensor(gate[:], g_a[:], g_r[:], ALU.mult).then_inc(gate_ready.sem, 1)
                if in_c:
                    dve.wait_ge(sc_exp.sem, sc_exp.now(it))
                    v.reciprocal(c_r[:], c_sum[:]).then_inc(sc_recip.sem, 1)
                    dve.wait_ge(sc_recip.sem, sc_recip.now(it))
                    dve.wait_ge(oc_summed.sem, oc_summed.now(it))
                    v.tensor_tensor(c_o[:], pC[:, 0, 0:D].rearrange("p (h d) -> p h d", d=DH_C),
                                    c_r[:].unsqueeze(2).to_broadcast([P, NH_C, DH_C]), ALU.mult).then_inc(oc_ready.sem, 1)
                if in_a:
                    for r in range(2):
                        wait_apart(dve, att_summed.sem, att_summed.now(it, r + 1))
                        if r == 0:
                            v.tensor_copy(dterm[:], pA[:, 1, 448:448 + NH_A]).then_inc(dterm_ready.sem, 1)
                            wait_apart(dve, oa_summed.sem, oa_summed.before(it))
                        for l, s in enumerate(HALVES):
                            if l:
                                wait_apart(dve, att_kept.sem, att_kept.now(it, r * NL + l))
                            both = lambda t: t.rearrange("p h (n s) -> p h n s", s=s)
                            upper = attT[:, 2 * r:2 * r + 2, :].rearrange("p h (n u s) -> p h n u s", u=2, s=s)[:, :, :, 1, :]
                            v.copy_predicated(upper, both(level_mask[:, l, :, :]), both(pA[:, :, l * 64:(l + 1) * 64]))\
                                .then_inc(att_kept.sem, 1)
                    dve.wait_ge(dterm_ready.sem, dterm_ready.now(it))
                    dve.wait_ge(v_ready.sem, v_ready.now(it))
                    v.tensor_tensor(dv[:].rearrange("p (h d) -> p h d", h=NH_A), v_a[:].rearrange("p (h d) -> p h d", h=NH_A),
                                    dterm[:].unsqueeze(2).to_broadcast([P, NH_A, DV_A]), ALU.mult).then_inc(dv_ready.sem, 1)
                    dve.wait_ge(oa_summed.sem, oa_summed.now(it))
                    dve.wait_ge(dv_ready.sem, dv_ready.now(it))
                    v.tensor_tensor(o_a[:], pA[:, 0, 0:VD], dv[:], ALU.add).then_inc(oa_ready.sem, 1)
                    dve.wait_ge(oa_ready.sem, oa_ready.now(it))
                    layernorm(it, o_a, o_n, norm_o, o_normed)
                    normalise(it, o_a, o_n, norm_o, o_normed)
                    dve.wait_ge(o_normed.sem, o_normed.now(it))
                    dve.wait_ge(gates_ready.sem, gates_ready.now(it))
                    v.tensor_tensor(o_g[:], o_n[:], gate_g[:], ALU.mult).then_inc(o_scaled.sem, 1)
                    dve.wait_ge(o_scaled.sem, o_scaled.now(it))
                    dve.wait_ge(o_turned.sem, o_turned.before(it))
                    v.tensor_tensor(o_f[:], o_g[:], gate_b[:], ALU.add).then_inc(o_final.sem, 1)
                if in_c:
                    dve.wait_ge(yc_summed.sem, yc_summed.now(it))
                    dve.wait_ge(res_begun.sem, res_begun.now(it))
                    for e in range(NE):
                        rows = slice(e * NTE, (e + 1) * NTE)
                        v.tensor_tensor(res[rows, 0:WIDTH[e]], pC[rows, 0, 256:256 + WIDTH[e]], res[rows, 0:WIDTH[e]],
                                        ALU.add).then_inc(res_ready.sem, 1)
                if in_b:
                    dve.wait_ge(yb_summed.sem, yb_summed.now(it))
                    dve.wait_ge(x1bo_ready.sem, x1bo_ready.now(it))
                    if in_c:
                        dve.wait_ge(x23_ready.sem, x23_ready.now(it))
                    v.tensor_tensor(x2[:], pB[:, 0, 0:D], x1_bo[:], ALU.add).then_inc(x2_ready.sem, 1)
                if in_a:
                    dve.wait_ge(ya_summed.sem, ya_summed.now(it))
                    if in_b:
                        dve.wait_ge(x1bo_ready.sem, x1bo_ready.now(it))
                    v.tensor_tensor(x1[:], pA[:, 0, 256:512], x_in[:], ALU.add).then_inc(x1_ready.sem, 1)

            run(dve, body)


def kernel(**inputs):
    import numpy as _np
    import concourse.bacc as _bacc
    from concourse import mybir as _mybir
    from concourse.bass_utils import run_bass_kernel_spmd as _run

    p = {k.replace("L0_", ""): _np.asarray(v) for k, v in inputs.items()}
    con = _np.ascontiguousarray
    col = lambda t: con(t.reshape(-1, P).T)
    row = lambda t: con(t.reshape(1, -1))
    wo = p["xattn_Wo"].T.reshape(PAR, J, DH, D).transpose(1, 0, 2, 3).reshape(HD, D)
    laid = {
        "x": con(p["x"]), 
        "ctxT": con(p["ctx_1024"].reshape(B, SB, PAR, J // PAIRS, PAIRS, D).transpose(0, 5, 4, 2, 1, 3).reshape(B, D, P)),
        "mu0": col(p["attn_mu0"]), "Wx0": con(p["attn_Wx0"].T), "Wx2": con(p["attn_Wx2"].T),
        "x_bias": con(p["attn_x_bias"].reshape(NMIX * KT, P).T),
        "rW": con(p["attn_rW"].T), "kW": con(p["attn_kW"].T), "vW": con(p["attn_vW"].T),
        "wA": con(p["attn_wA"].T), "wB": con(p["attn_wB"].T), "wb": con(p["attn_wb"].reshape(P, 1)),
        "gA": con(p["attn_gA"].T), "gB": con(p["attn_gB"].T), "gb": row(p["attn_gb"]),
        "bonus": con(p["attn_bonus"].reshape(P, 1)), "ln_g": row(p["attn_ln_g"]), "ln_b": row(p["attn_ln_b"]),
        "oWa": con(p["attn_oW"].T),
        "Wq": con(p["xattn_Wq"].T), "Wk": con(p["xattn_Wk"].T), "Wv": con(p["xattn_Wv"].T), "Wo": con(wo),
        "bq": col(p["xattn_bq"]), "bk": col(p["xattn_bk"]), "bv": row(p["xattn_bv"]), "bo": row(p["xattn_bo"]),
        "norm_w": col(p["ffn_norm_w"]), "norm_b": col(p["ffn_norm_b"]),
        "q_w": con(p["ffn_q_w"].T), "k_w": con(p["ffn_k_w"].T), "v_w": con(p["ffn_v_w"].T), "o_w": con(p["ffn_o_w"].T),
        "q_b": col(p["ffn_q_b"]), "k_b": col(p["ffn_k_b"]), "v_b": row(p["ffn_v_b"]), "o_b": row(p["ffn_o_b"]),
    }
    nc = _bacc.Bacc("TRN2", target_bir_lowering=False, num_devices=1)
    arrays, args = {}, {}
    for name, t in laid.items():
        arrays[f"in_{name}"] = t
        args[name] = nc.dram_tensor(f"in_{name}", t.shape, _mybir.dt.from_np(t.dtype), kind="ExternalInput").ap()
    out = nc.dram_tensor("out_0", (B, P, D), _mybir.dt.float32, kind="ExternalOutput").ap()
    decoder_layer(nc, args, out)
    r = _run(nc, [arrays], core_ids=[0])
    return r.results[0]["out_0"]
```

```python
from contextlib import ExitStack

import concourse.bass as bass
from concourse import mybir

F32 = mybir.dt.float32
I32 = mybir.dt.int32
ALU = mybir.AluOpType
ACT = mybir.ActivationFunctionType
AX_X = mybir.AxisListType.X

P = 128
B = 16
D = 256
KT = D // P
EPS = 1e-5
RSQRT_BITS = float(0x5F3759DF - 0x400000)
NEWTON = 3

NMIX, PLR, GLR = 5, 32, 64
KD, VD, NH_A = 128, 256, 4
DK_A, DV_A = KD // NH_A, VD // NH_A
CHUNK = 32
HALVES = [64, 32, 16, 8, 4, 2, 1]
NL = len(HALVES)

H, DH = 16, 64
HD = H * DH
SB, PAR, J = 8, 2, 8
PAIRS = 4
NG = SB * J // PAIRS

NE, NH_C = 4, 8
NTE = P // NE
DH_C = D // NH_C
WIDTH = [D >> e for e in range(NE)]

LAG_A, LAG_B, LAG_C = 0, 1, 2


class Signal:

    def __init__(self, sem, lag, per):
        self.sem, self.lag, self.per = sem, lag, per

    def now(self, step, k=None):
        return (step - self.lag) * self.per + (self.per if k is None else k)

    def before(self, step):
        return (step - self.lag) * self.per


def decoder_layer(nc, a, out):
    ctx = ExitStack()
    with ctx:
        def sb(name, shape, dt=F32):
            return ctx.enter_context(nc.sbuf_tensor(name, shape, dt))

        def psum(name, shape):
            return ctx.enter_context(nc.psum_tensor(name, shape, F32))

        def sig(name, lag, per=1):
            return Signal(ctx.enter_context(nc.semaphore(name)), lag, per)

        w_x0 = sb("w_x0", [P, KT, NMIX * PLR])
        w_mix = sb("w_mix", [P, NMIX, D])
        w_r = sb("w_r", [P, KT, KD])
        w_k = sb("w_k", [P, KT, KD])
        w_v = sb("w_v", [P, KT, VD])
        w_wa = sb("w_wa", [P, KT, GLR])
        w_ga = sb("w_ga", [P, KT, GLR])
        w_wgb = sb("w_wgb", [P, VD])
        w_oa = sb("w_oa", [P, KT, D])
        mu0 = sb("mu0", [P, KT])
        x_bias = sb("x_bias", [P, NMIX, KT])
        wb = sb("wb", [P, 1])
        bonus = sb("bonus", [P, 1])
        gb_bc = sb("gb_bc", [P, VD])
        lng_bc = sb("lng_bc", [P, VD])
        lnb_bc = sb("lnb_bc", [P, VD])
        w_q = sb("w_q", [P, KT, HD])
        w_kb = sb("w_kb", [P, KT, HD])
        w_vb = sb("w_vb", [P, KT, HD])
        w_ob = sb("w_ob", [P, J, D])
        bq = sb("bq", [P, H // 2])
        bk = sb("bk", [P, H // 2])
        bv_bc = sb("bv_bc", [P, HD])
        bo_bc = sb("bo_bc", [P, D])
        w_qc = sb("w_qc", [P, KT, D])
        w_kc = sb("w_kc", [P, KT, D])
        w_vc = sb("w_vc", [P, KT, D])
        w_oc = sb("w_oc", [P, KT, D])
        norm_w = sb("norm_w", [P, KT])
        norm_b = sb("norm_b", [P, KT])
        qb_c = sb("qb_c", [P, KT])
        kb_c = sb("kb_c", [P, KT])
        vb_bc = sb("vb_bc", [P, D])
        ob_valid = sb("ob_valid", [P, D])
        ident = sb("ident", [P, P])
        zeros = sb("zeros", [P, P])
        three_halves = sb("three_halves", [P, 1])
        level_mask = sb("level_mask", [P, NL, NH_A, P // 2], I32)
        head_ones = sb("head_ones", [P, NH_A])
        par_mask = sb("par_mask", [P, PAR])
        chunk_keep = sb("chunk_keep", [P, P])

        x_in = sb("x_in", [P, D])
        a_xn = sb("a_xn", [P, D])
        a_xT = sb("a_xT", [P, KT, P + 1])
        delta = sb("delta", [P, KT, P])
        z0 = sb("z0", [P, KT, P])
        xx = sb("xx", [P, 2, P])
        mix = sb("mix", [P, NMIX, KT, P])
        ud = sb("ud", [P, NMIX, KT, P])
        xv = sb("xv", [P, NMIX, KT, P])
        wg = sb("wg", [P, P])
        qT = sb("qT", [P, P]); kT = sb("kT", [P, P])
        v_a = sb("v_a", [P, VD])
        g_a = sb("g_a", [P, VD]); g_e = sb("g_e", [P, VD]); g_1 = sb("g_1", [P, VD]); g_r = sb("g_r", [P, VD])
        gate = sb("gate", [P, VD]); gate_g = sb("gate_g", [P, VD]); gate_b = sb("gate_b", [P, VD])
        nw = sb("nw", [P, P]); c_in = sb("c_in", [P, P]); c_ex = sb("c_ex", [P, P]); c_rest = sb("c_rest", [P, P])
        decay = sb("decay", [P, NL, P]); edec = sb("edec", [P, NL, P])
        q_blkA = sb("q_blkA", [P, NH_A, P])
        f_q = sb("f_q", [P, NL, NH_A, P // 2]); f_k = sb("f_k", [P, NL, P])
        quk = sb("quk", [P, P]); dterm = sb("dterm", [P, NH_A])
        attT = sb("attT", [P, NH_A, P])
        dv = sb("dv", [P, VD]); o_a = sb("o_a", [P, VD])
        o_n = sb("o_n", [P, VD]); o_g = sb("o_g", [P, VD]); o_f = sb("o_f", [P, VD])
        o_T = sb("o_T", [P, KT, P])
        x1 = sb("x1", [P, D])

        ctxT = sb("ctxT", [P, KT, P])
        b_xn = sb("b_xn", [P, D])
        b_xT = sb("b_xT", [P, KT, P])
        x1_bo = sb("x1_bo", [P, D])
        q_blk = sb("q_blk", [P, SB, J, PAR, H])
        k_st = sb("k_st", [P, SB, J, H])
        v_raw = sb("v_raw", [P, HD])
        v_tok = sb("v_tok", [P, H, DH])
        v_g = sb("v_g", [P, NG, DH])
        s_d = sb("s_d", [P, NG, H])
        s_mx = sb("s_mx", [P, NG]); s_sh = sb("s_sh", [P, NG, H]); s_e = sb("s_e", [P, NG, H])
        s_sum = sb("s_sum", [P, NG]); s_r = sb("s_r", [P, NG]); s_rm = sb("s_rm", [P, NG, PAR])
        p_m = sb("p_m", [P, NG, PAR, H])
        p_T = sb("p_T", [P, NG, PAIRS, PAR, H])
        o_B = sb("o_B", [P, J, H, SB])
        x2 = sb("x2", [P, D])

        x3 = sb("x3", [P, D])
        c_xn = sb("c_xn", [P, D])
        x23 = sb("x23", [P, D]); res = sb("res", [P, D])
        c_xT = sb("c_xT", [P, KT, P])
        q_c = sb("q_c", [P, KT, P])
        k_blk = sb("k_blk", [P, KT, 4, P])
        v_c = sb("v_c", [P, D])
        c_mx = sb("c_mx", [P, NH_C]); c_nm = sb("c_nm", [P, NH_C])
        c_e = sb("c_e", [P, NH_C, P]); c_sum = sb("c_sum", [P, NH_C]); c_r = sb("c_r", [P, NH_C])
        c_eT = sb("c_eT", [P, NH_C, P])
        c_o = sb("c_o", [P, NH_C, DH_C])
        c_oT = sb("c_oT", [P, KT, P])

        pA = psum("pA", [P, 2, 512])
        pC = psum("pC", [P, 2, 512])
        pB = psum("pB", [P, 2, 1024])

        loaded = sig("loaded", 0); zeroed = sig("zeroed", 0); made = sig("made", 0)
        MADE = 7 + NL * (3 + NH_A) + PAR * (3 + PAIRS)
        A, Bl, C = LAG_A, LAG_B, LAG_C
        x_loaded = sig("x_loaded", A, 16)
        a_normed = sig("a_normed", A)
        a_turned = sig("a_turned", A); a_xT_ready = sig("a_xT_ready", A)
        delta_ready = sig("delta_ready", A); z0_ready = sig("z0_ready", A, 2)
        xx_summed = sig("xx_summed", A); xx_ready = sig("xx_ready", A, 2)
        mix_summed = sig("mix_summed", A, 3); mix_ready = sig("mix_ready", A, 3); ud_ready = sig("ud_ready", A, 3); xv_ready = sig("xv_ready", A, 3)
        rk_summed = sig("rk_summed", A); v_summed = sig("v_summed", A); wg_ready = sig("wg_ready", A)
        w_summed = sig("w_summed", A); g_summed = sig("g_summed", A)
        rk_ready = sig("rk_ready", A); v_ready = sig("v_ready", A)
        w_exp = sig("w_exp", A); g_ready = sig("g_ready", A); g_exp = sig("g_exp", A)
        g_plus1 = sig("g_plus1", A); g_recip = sig("g_recip", A); gate_ready = sig("gate_ready", A); gates_ready = sig("gates_ready", A, 2)
        c_in_ready = sig("c_in_ready", A); c_parts = sig("c_parts", A, 2)
        decay_dve = sig("decay_dve", A, 12); decay_pool = sig("decay_pool", A, 4)
        edec_ready = sig("edec_ready", A); fq_ready = sig("fq_ready", A, NL); fk_ready = sig("fk_ready", A, 2)
        quk_ready = sig("quk_ready", A); att_summed = sig("att_summed", A, 4); att_kept = sig("att_kept", A, NL)
        dterm_ready = sig("dterm_ready", A); dv_ready = sig("dv_ready", A)
        oa_summed = sig("oa_summed", A); oa_ready = sig("oa_ready", A)
        o_normed = sig("o_normed", A)
        o_scaled = sig("o_scaled", A); o_final = sig("o_final", A); o_turned = sig("o_turned", A); oT_ready = sig("oT_ready", A)
        ya_summed = sig("ya_summed", A); x1_ready = sig("x1_ready", A)

        ctx_loaded = sig("ctx_loaded", Bl, 16)
        b_normed = sig("b_normed", Bl)
        b_turned = sig("b_turned", Bl); b_xT_ready = sig("b_xT_ready", Bl); x1bo_ready = sig("x1bo_ready", Bl)
        vb_summed = sig("vb_summed", Bl); v_out = sig("v_out", Bl); vb_ready = sig("vb_ready", Bl); vg_moved = sig("vg_moved", Bl, 16 * NG)
        kb_summed = sig("kb_summed", Bl); kb_ready = sig("kb_ready", Bl); qb_summed = sig("qb_summed", Bl); qb_ready = sig("qb_ready", Bl)
        s_summed = sig("s_summed", Bl); s_dense = sig("s_dense", Bl); s_max = sig("s_max", Bl); s_shift = sig("s_shift", Bl)
        s_exp = sig("s_exp", Bl); s_total = sig("s_total", Bl); s_recip = sig("s_recip", Bl); s_scale = sig("s_scale", Bl)
        p_masked = sig("p_masked", Bl); p_turned = sig("p_turned", Bl)
        ob_summed = sig("ob_summed", Bl); ob_ready = sig("ob_ready", Bl)
        yb_summed = sig("yb_summed", Bl); x2_ready = sig("x2_ready", Bl)

        x3_ready = sig("x3_ready", C)
        c_normed = sig("c_normed", C)
        x23_ready = sig("x23_ready", C); res_begun = sig("res_begun", C)
        c_turned = sig("c_turned", C); c_xT_ready = sig("c_xT_ready", C)
        qk_summed = sig("qk_summed", C); vc_summed = sig("vc_summed", C)
        qc_ready = sig("qc_ready", C, 2); kc_ready = sig("kc_ready", C); vc_ready = sig("vc_ready", C)
        sc_summed = sig("sc_summed", C); sc_max = sig("sc_max", C); sc_nmax = sig("sc_nmax", C); sc_exp = sig("sc_exp", C)
        pc_turned = sig("pc_turned", C); pc_ready = sig("pc_ready", C); sc_recip = sig("sc_recip", C)
        oc_summed = sig("oc_summed", C); oc_ready = sig("oc_ready", C); oc_turned = sig("oc_turned", C); ocT_ready = sig("ocT_ready", C)
        yc_summed = sig("yc_summed", C); res_ready = sig("res_ready", C, NE); stored = sig("stored", C, 16)

        class Norm:

            def __init__(self, name, lag, per):
                self.st, self.mv = sb(name + "_st", [P, 6]), sb(name + "_mv", [P, 2])
                self.v, self.y, self.t = (sb(f"{name}_{x}", [P, 1]) for x in "vyt")
                self.bits = sb(name + "_bits", [P, 1], I32)
                self.stats, self.aggr = sig(name + "_stats", lag), sig(name + "_aggr", lag)
                self.var_eps, self.halved = sig(name + "_var_eps", lag), sig(name + "_halved", lag)
                self.guessed, self.newton = sig(name + "_guessed", lag), sig(name + "_newton", lag, per * NEWTON)

        norm_a, norm_of_b, norm_c, norm_d, norm_o = (Norm(*x) for x in (
            ("norm_a", A, 3), ("norm_of_b", Bl, 3), ("norm_c", C, 3), ("norm_d", C, 4), ("norm_o", A, 4)))

        block = ctx.enter_context(nc.Block())

        def wait_apart(engine, *waits):
            waits = [(sem, value if isinstance(value, int) else engine.to_reg(value)) for sem, value in waits]
            engine.wait_ge(loaded.sem, ALL_LOADED)
            for sem, value in waits:
                engine.wait_ge(sem, value)

        def run(engine, body):
            steps = B + LAG_C
            for step in range(LAG_C + 1):
                body(step, step >= LAG_A, step >= LAG_B, step >= LAG_C)
            with engine.Fori(LAG_C + 1, B) as step:
                body(step, True, True, True)
            for step in range(B, steps):
                body(step, False, step - LAG_B < B, step - LAG_C < B)

        resident = [
            (w_x0[:], a["Wx0"].rearrange("(k p) n -> p k n", p=P)),
            (w_mix[0:PLR, NMIX - 1, :], a["Wx2"][(NMIX - 1) * PLR:NMIX * PLR, :]),
            (w_r[:], a["rW"].rearrange("(k p) n -> p k n", p=P)),
            (w_k[:], a["kW"].rearrange("(k p) n -> p k n", p=P)),
            (w_v[:], a["vW"].rearrange("(k p) n -> p k n", p=P)),
            (w_wa[:], a["wA"].rearrange("(k p) n -> p k n", p=P)),
            (w_ga[:], a["gA"].rearrange("(k p) n -> p k n", p=P)),
            (w_wgb[0:GLR, 0:KD], a["wB"]), (w_wgb[GLR:2 * GLR, :], a["gB"]),
            (w_oa[:], a["oWa"].rearrange("(k p) n -> p k n", p=P)),
            (mu0[:], a["mu0"]), (x_bias[:], a["x_bias"].rearrange("p (i k) -> p i k", k=KT)),
            (wb[:], a["wb"]), (bonus[:], a["bonus"]),
            (gb_bc[:], a["gb"].to_broadcast([P, VD])),
            (lng_bc[:], a["ln_g"].to_broadcast([P, VD])), (lnb_bc[:], a["ln_b"].to_broadcast([P, VD])),
            (w_vb[:], a["Wv"].rearrange("(k p) n -> p k n", p=P)),
            (w_kb[:], a["Wk"].rearrange("(k p) n -> p k n", p=P)),
            (w_q[:], a["Wq"].rearrange("(k p) n -> p k n", p=P)),
            (w_ob[:], a["Wo"].rearrange("(j p) n -> p j n", p=P)),
            (bq[:], a["bq"]), (bk[:], a["bk"]),
            (bv_bc[:], a["bv"].to_broadcast([P, HD])), (bo_bc[:], a["bo"].to_broadcast([P, D])),
            (w_qc[:], a["q_w"].rearrange("(k p) n -> p k n", p=P)),
            (w_kc[:], a["k_w"].rearrange("(k p) n -> p k n", p=P)),
            (w_vc[:], a["v_w"].rearrange("(k p) n -> p k n", p=P)),
            (w_oc[:], a["o_w"].rearrange("(k p) n -> p k n", p=P)),
            (norm_w[:], a["norm_w"]), (norm_b[:], a["norm_b"]), (qb_c[:], a["q_b"]), (kb_c[:], a["k_b"]),
            (vb_bc[:], a["v_b"].to_broadcast([P, D])),
        ]
        into_zeroed = [(w_mix[i * PLR:(i + 1) * PLR, i, :], a["Wx2"][i * PLR:(i + 1) * PLR, :]) for i in range(NMIX - 1)]
        into_zeroed += [(ob_valid[e * NTE:(e + 1) * NTE, 0:WIDTH[e]], a["o_b"][:, 0:WIDTH[e]].to_broadcast([NTE, WIDTH[e]]))
                        for e in range(NE)]
        ALL_LOADED = 16 * (len(resident) + len(into_zeroed))
        zero_fill = [attT, q_blk, q_blkA, p_T, c_xT, k_blk, c_oT, w_mix[:, 0:NMIX - 1, :], ob_valid, zeros, ident,
                     a_xT, head_ones, par_mask]

        @block.sync
        def _(sp):
            for dst, src in resident:
                sp.dma_start(dst, src).then_inc(loaded.sem, 16)
            sp.wait_ge(zeroed.sem, len(zero_fill))
            for dst, src in into_zeroed:
                sp.dma_start(dst, src).then_inc(loaded.sem, 16)

            def body(it, in_a, in_b, in_c):
                if in_b:
                    sp.wait_ge(kb_summed.sem, kb_summed.before(it))
                    sp.dma_start(ctxT[:], a["ctxT"][it - LAG_B].rearrange("(k p) t -> p k t", p=P)).then_inc(ctx_loaded.sem, 16)
                if in_a:
                    sp.wait_ge(x1_ready.sem, x1_ready.before(it))
                    sp.dma_start(x_in[:], a["x"][it - LAG_A]).then_inc(x_loaded.sem, 16)
                if in_b:
                    sp.wait_ge(vb_ready.sem, vb_ready.now(it))
                    sp.wait_ge(ob_summed.sem, ob_summed.before(it))
                    for g in range(NG):
                        sp.dma_start(v_g[:, g, :], v_tok[g:P:NG, :, :]).then_inc(vg_moved.sem, 16)
                if in_c:
                    sp.wait_ge(res_ready.sem, res_ready.now(it))
                    sp.dma_start(out[it - LAG_C], res[:]).then_inc(stored.sem, 16)

            run(sp, body)
            sp.wait_ge(stored.sem, 16 * B)

        @block.gpsimd
        def _(pool):
            for t in zero_fill:
                nc.gpsimd.memset(t if isinstance(t, bass.AP) else t[:], 0.0).then_inc(zeroed.sem, 1)
            pool.wait_ge(zeroed.sem, len(zero_fill))
            count = [0]

            def step_(ins):
                count[0] += 1
                ins.then_inc(made.sem, 1)
                pool.wait_ge(made.sem, count[0])

            step_(nc.gpsimd.affine_select(out=ident[:], in_=ident[:], compare_op=ALU.not_equal, fill=1.0, base=0,
                                          pattern=[[-1, P]], channel_multiplier=1))
            step_(nc.gpsimd.memset(head_ones[:], 1.0))
            step_(nc.gpsimd.affine_select(out=head_ones[:], in_=head_ones[:], compare_op=ALU.is_ge, fill=0.0, base=0,
                                          pattern=[[-DK_A, NH_A]], channel_multiplier=1))
            step_(nc.gpsimd.affine_select(out=head_ones[:], in_=head_ones[:], compare_op=ALU.is_ge, fill=0.0,
                                          base=DK_A - 1, pattern=[[DK_A, NH_A]], channel_multiplier=-1))
            step_(nc.gpsimd.memset(three_halves[:], 1.5))
            step_(nc.gpsimd.memset(chunk_keep[:], 1.0))
            step_(nc.gpsimd.memset(chunk_keep[:].rearrange("p (c t) -> p c t", t=CHUNK)[:, :, 0:1], 0.0))
            for l, s in enumerate(HALVES):
                m = zeros[:, 0:P // 2].rearrange("p (b r) -> p b r", r=s)
                n = P // (2 * s)
                step_(nc.gpsimd.memset(zeros[:, 0:P // 2], 1.0))
                step_(nc.gpsimd.affine_select(out=m, in_=m, compare_op=ALU.is_ge, fill=0.0, base=0,
                                              pattern=[[-2 * s, n], [0, s]], channel_multiplier=1))
                step_(nc.gpsimd.affine_select(out=m, in_=m, compare_op=ALU.is_ge, fill=0.0, base=s - 1,
                                              pattern=[[2 * s, n], [0, s]], channel_multiplier=-1))
                for h in range(NH_A):
                    step_(nc.gpsimd.tensor_copy(level_mask[:, l, h, :], zeros[:, 0:P // 2]))
            for par in range(PAR):
                m = zeros[:, 0:PAIRS]
                step_(nc.gpsimd.memset(m, 1.0))
                step_(nc.gpsimd.affine_select(out=m, in_=m, compare_op=ALU.is_ge, fill=0.0, base=-par * H,
                                              pattern=[[-PAR * H, PAIRS]], channel_multiplier=1))
                step_(nc.gpsimd.affine_select(out=m, in_=m, compare_op=ALU.is_ge, fill=0.0, base=par * H + H - 1,
                                              pattern=[[PAR * H, PAIRS]], channel_multiplier=-1))
                for pair in range(PAIRS):
                    step_(nc.gpsimd.tensor_tensor(par_mask[:, par:par + 1], par_mask[:, par:par + 1],
                                                  m[:, pair:pair + 1], ALU.add))
            assert count[0] == MADE
            pool.wait_ge(loaded.sem, ALL_LOADED)

            def rstd_of(it, n):
                pool.wait_ge(n.guessed.sem, n.guessed.now(it))
                for r in range(NEWTON):
                    steps = ((n.t, n.y, n.y, ALU.mult), (n.t, n.t, n.v, ALU.mult),
                             (n.t, three_halves, n.t, ALU.subtract), (n.y, n.y, n.t, ALU.mult))
                    for k, (o, p0, p1, op) in enumerate(steps):
                        if r or k:
                            pool.wait_ge(n.newton.sem, n.newton.now(it, 4 * r + k))
                        nc.gpsimd.tensor_tensor(o[:], p0[:], p1[:], op).then_inc(n.newton.sem, 1)

            def body(it, in_a, in_b, in_c):
                if in_b:
                    pool.wait_ge(v_out.sem, v_out.now(it))
                    pool.wait_ge(vg_moved.sem, vg_moved.before(it))
                    nc.gpsimd.tensor_tensor(v_tok[:].rearrange("p h d -> p (h d)"), v_raw[:], bv_bc[:], ALU.add)\
                        .then_inc(vb_ready.sem, 1)
                if in_c:
                    rstd_of(it, norm_d)
                if in_b:
                    pool.wait_ge(x1_ready.sem, x1_ready.before(it))
                    pool.wait_ge(x2_ready.sem, x2_ready.before(it))
                    nc.gpsimd.tensor_tensor(x1_bo[:], x1[:], bo_bc[:], ALU.add).then_inc(x1bo_ready.sem, 1)
                if in_c:
                    pool.wait_ge(x3_ready.sem, x3_ready.now(it))
                    nc.gpsimd.tensor_tensor(x23[:], x2[:], x3[:], ALU.add).then_inc(x23_ready.sem, 1)
                    pool.wait_ge(x23_ready.sem, x23_ready.now(it))
                    pool.wait_ge(stored.sem, stored.before(it))
                    nc.gpsimd.tensor_tensor(res[:], x23[:], ob_valid[:], ALU.add).then_inc(res_begun.sem, 1)
                if in_a:
                    pool.wait_ge(edec_ready.sem, edec_ready.before(it))
                    wait_apart(pool, (c_parts.sem, c_parts.now(it)))
                    for l, src, c in ((1, c_ex, 1), (1, c_ex, 3), (0, c_rest, 1), (0, c_ex, 2)):
                        nc.gpsimd.tensor_copy(decay[:, l, c * CHUNK:(c + 1) * CHUNK],
                                              src[:, c * CHUNK:(c + 1) * CHUNK]).then_inc(decay_pool.sem, 1)
                    pool.wait_ge(edec_ready.sem, edec_ready.now(it))
                    pool.wait_ge(rk_ready.sem, rk_ready.now(it))
                    pool.wait_ge(att_summed.sem, att_summed.before(it))
                    for l0, l1 in ((0, NL // 2), (NL // 2, NL)):
                        nc.gpsimd.tensor_tensor(f_k[:, l0:l1], edec[:, l0:l1], kT[:].unsqueeze(1).to_broadcast([P, l1 - l0, P]),
                                                ALU.mult).then_inc(fk_ready.sem, 1)
                    pool.wait_ge(gate_ready.sem, gate_ready.now(it))
                    pool.wait_ge(o_final.sem, o_final.before(it))
                    nc.gpsimd.tensor_tensor(gate_g[:], gate[:], lng_bc[:], ALU.mult).then_inc(gates_ready.sem, 1)
                    nc.gpsimd.tensor_tensor(gate_b[:], gate[:], lnb_bc[:], ALU.mult).then_inc(gates_ready.sem, 1)
                    rstd_of(it, norm_o)

            run(pool, body)

        @block.tensor
        def _(pe):
            pe.wait_ge(loaded.sem, ALL_LOADED)
            pe.wait_ge(made.sem, MADE)
            mm = nc.tensor.matmul

            def turn(out_, in_, signal):
                for k in range(KT):
                    last = nc.tensor.transpose(out_[:, k * P:(k + 1) * P], in_[:, k * P:(k + 1) * P], ident[:])
                last.then_inc(signal.sem, 1)

            def project(out_, lhs, rhs, n=KT):
                for k in range(n):
                    last = mm(out_, lhs(k), rhs(k), start=(k == 0), stop=(k == n - 1))
                return last

            def b_project(bank, w, rhs, c0, c1):
                for c in range(c0, c1):
                    last = project(pB[:, bank, c * P:(c + 1) * P], lambda k: w[:, k, c * P:(c + 1) * P], rhs)
                return last

            def mixes(r, bank, which):
                for n, i in enumerate(which):
                    for k in range(KT):
                        rows, t = (slice(0, P), 0) if i < NMIX - 1 else (slice(0, PLR), 1)
                        last = mm(pA[:, bank, (n * KT + k) * P:(n * KT + k + 1) * P], w_mix[rows, i, k * P:(k + 1) * P],
                                  xx[rows, t, :], start=True, stop=True)
                last.then_inc(mix_summed.sem, 1)

            def levels(bank, which):
                for n, l in enumerate(which):
                    last = mm(pA[:, bank, n * 256:(n + 1) * 256], f_k[:, l, :], f_q[:, l, :, :], start=True, stop=True)
                return last

            def b_scores(g0, g1):
                for g in range(g0, g1):
                    s, jh = g // 2, g % 2
                    last = mm(pB[:, 0, g * 64:(g + 1) * 64], q_blk[:, s, jh * PAIRS:(jh + 1) * PAIRS, :, :],
                              k_st[:, s, jh * PAIRS:(jh + 1) * PAIRS, :], start=True, stop=True)
                return last

            def b_values(g0, g1):
                for g in range(g0, g1):
                    for par in range(PAR):
                        last = mm(pB[par * DH:(par + 1) * DH, 1, g * 64:(g + 1) * 64], v_g[:, g, :],
                                  p_T[:, g, :, par, :], start=True, stop=True)
                return last

            def b_out(j0, j1):
                for j in range(j0, j1):
                    last = mm(pB[:, 0, 0:D], o_B[:, j, :, :], w_ob[:, j, :], start=(j == 0), stop=(j == J - 1))
                return last

            ctx_of = lambda k: ctxT[:, k, :]
            x_of = lambda k: b_xT[:, k, :]

            def body(it, in_a, in_b, in_c):
                if in_b:
                    pe.wait_ge(ctx_loaded.sem, ctx_loaded.now(it))
                    pe.wait_ge(x2_ready.sem, x2_ready.before(it))
                    for n in range(2):
                        last = project(pB[:, 0, n * 512:(n + 1) * 512], ctx_of,
                                       lambda k: w_vb[:, k, n * 512:(n + 1) * 512])
                    last.then_inc(vb_summed.sem, 1)
                if in_a:
                    pe.wait_ge(a_normed.sem, a_normed.now(it))
                    pe.wait_ge(x1_ready.sem, x1_ready.before(it))
                    turn(pA[:, 0, :], a_xn, a_turned)
                if in_b:
                    pe.wait_ge(b_normed.sem, b_normed.now(it))
                    pe.wait_ge(ob_ready.sem, ob_ready.before(it))
                    turn(pB[:, 1, :], b_xn, b_turned)
                    pe.wait_ge(v_out.sem, v_out.now(it))
                    b_project(0, w_kb, ctx_of, 0, 4)
                if in_a:
                    pe.wait_ge(z0_ready.sem, z0_ready.now(it))
                    project(pA[:, 1, 0:P], lambda k: w_x0[:, k, 0:P], lambda k: z0[:, k, :])
                    project(pA[0:PLR, 1, P:2 * P], lambda k: w_x0[:, k, P:P + PLR], lambda k: z0[:, k, :])\
                        .then_inc(xx_summed.sem, 1)
                if in_b:
                    b_project(0, w_kb, ctx_of, 4, 8).then_inc(kb_summed.sem, 1)
                if in_a:
                    pe.wait_ge(xx_ready.sem, xx_ready.now(it))
                    mixes(0, 0, (0, 1))
                    mixes(1, 1, (2, 3))
                if in_b:
                    pe.wait_ge(b_xT_ready.sem, b_xT_ready.now(it))
                    b_project(1, w_q, x_of, 0, 4)
                if in_a:
                    pe.wait_ge(mix_ready.sem, mix_ready.now(it, 1))
                    mixes(2, 0, (4,))
                if in_c:
                    pe.wait_ge(c_normed.sem, c_normed.now(it))
                    pe.wait_ge(res_ready.sem, res_ready.before(it))
                    turn(pC[:, 0, :], c_xn, c_turned)
                if in_b:
                    b_project(1, w_q, x_of, 4, 8).then_inc(qb_summed.sem, 1)
                if in_c:
                    pe.wait_ge(c_xT_ready.sem, c_xT_ready.now(it))
                    for w, o in ((w_qc, pC[:, 1, 0:256]), (w_kc, pC[:, 1, 256:512])):
                        for m in range(KT):
                            mm(o[:, m * P:(m + 1) * P], w[:, 0, m * P:(m + 1) * P], c_xT[:, 0, :], start=True, stop=False)
                            last = mm(o[:, m * P:m * P + NTE], w[:, 1, m * P:(m + 1) * P], c_xT[:, 1, 0:NTE],
                                      start=False, stop=True)
                    last.then_inc(qk_summed.sem, 1)
                    project(pC[:, 0, 256:512], lambda k: c_xT[:, k, :], lambda k: w_vc[:, k, :]).then_inc(vc_summed.sem, 1)
                if in_a:
                    pe.wait_ge(xv_ready.sem, xv_ready.now(it))
                    project(pA[0:GLR, 1, 2 * P:3 * P], lambda k: w_wa[:, k, :], lambda k: xv[:, 1, k, :])
                    project(pA[GLR:P, 1, 2 * P:3 * P], lambda k: w_ga[:, k, :], lambda k: xv[:, 4, k, :])
                    project(pA[:, 1, 0:P], lambda k: w_r[:, k, :], lambda k: xv[:, 0, k, :])
                    project(pA[:, 1, P:2 * P], lambda k: w_k[:, k, :], lambda k: xv[:, 2, k, :])\
                        .then_inc(rk_summed.sem, 1)
                    project(pA[:, 0, 0:VD], lambda k: xv[:, 3, k, :], lambda k: w_v[:, k, :]).then_inc(v_summed.sem, 1)
                if in_b:
                    pe.wait_ge(kb_ready.sem, kb_ready.now(it))
                    pe.wait_ge(qb_ready.sem, qb_ready.now(it))
                    b_scores(0, NG).then_inc(s_summed.sem, 1)
                if in_a:
                    pe.wait_ge(wg_ready.sem, wg_ready.now(it))
                    pe.wait_ge(rk_ready.sem, rk_ready.now(it))
                    mm(pA[:, 1, 3 * P:4 * P], w_wgb[0:GLR, 0:KD], wg[0:GLR, :], start=True, stop=True)\
                        .then_inc(w_summed.sem, 1)
                    pe.wait_ge(v_ready.sem, v_ready.now(it))
                    mm(pA[:, 0, VD:2 * VD], wg[GLR:P, :], w_wgb[GLR:P, :], start=True, stop=True)\
                        .then_inc(g_summed.sem, 1)
                if in_c:
                    pe.wait_ge(qc_ready.sem, qc_ready.now(it))
                    pe.wait_ge(kc_ready.sem, kc_ready.now(it))
                    pe.wait_ge(vc_ready.sem, vc_ready.now(it))
                    for m in range(KT):
                        last = mm(pC[:, m, :], q_c[:, m, :], k_blk[:, m, :, :], start=True, stop=True)
                    last.then_inc(sc_summed.sem, 1)
                if in_a:
                    pe.wait_ge(g_ready.sem, g_ready.now(it))
                    pe.wait_ge(w_exp.sem, w_exp.now(it))
                    pe.wait_ge(fk_ready.sem, fk_ready.now(it, 1))
                    pe.wait_ge(fq_ready.sem, fq_ready.now(it, 2))
                    levels(0, (0, 1)).then_inc(att_summed.sem, 1)
                    pe.wait_ge(fk_ready.sem, fk_ready.now(it))
                    pe.wait_ge(fq_ready.sem, fq_ready.now(it, 4))
                    levels(1, (2, 3)).then_inc(att_summed.sem, 1)
                if in_b:
                    pe.wait_ge(p_turned.sem, p_turned.now(it))
                    pe.wait_ge(vg_moved.sem, vg_moved.now(it))
                    b_values(0, NG // 2)
                if in_a:
                    pe.wait_ge(fq_ready.sem, fq_ready.now(it))
                    pe.wait_ge(att_kept.sem, att_kept.now(it, 2))
                    levels(0, (4, 5)).then_inc(att_summed.sem, 1)
                    pe.wait_ge(att_kept.sem, att_kept.now(it, 4))
                    pe.wait_ge(quk_ready.sem, quk_ready.now(it))
                    levels(1, (6,))
                    mm(pA[:, 1, 256:256 + NH_A], quk[:], head_ones[:], start=True, stop=True).then_inc(att_summed.sem, 1)
                if in_b:
                    b_values(NG // 2, NG).then_inc(ob_summed.sem, 1)
                if in_c:
                    pe.wait_ge(sc_exp.sem, sc_exp.now(it))
                    for h in range(NH_C):
                        last = nc.tensor.transpose(pC[:, h // 4, (h % 4) * P:(h % 4 + 1) * P], c_e[:, h, :], ident[:])
                    last.then_inc(pc_turned.sem, 1)
                if in_a:
                    pe.wait_ge(att_kept.sem, att_kept.now(it))
                    for h in range(NH_A):
                        last = mm(pA[:, 0, h * DV_A:(h + 1) * DV_A], attT[:, h, :], v_a[:, h * DV_A:(h + 1) * DV_A],
                                  start=True, stop=True)
                    last.then_inc(oa_summed.sem, 1)
                if in_b:
                    pe.wait_ge(ob_ready.sem, ob_ready.now(it))
                    pe.wait_ge(s_dense.sem, s_dense.now(it))
                    b_out(0, 4)
                if in_c:
                    pe.wait_ge(pc_ready.sem, pc_ready.now(it))
                    for h in range(NH_C):
                        last = mm(pC[:, 0, h * DH_C:(h + 1) * DH_C], c_eT[:, h, :], v_c[:, h * DH_C:(h + 1) * DH_C],
                                  start=True, stop=True)
                    last.then_inc(oc_summed.sem, 1)
                if in_b:
                    b_out(4, 8).then_inc(yb_summed.sem, 1)
                if in_a:
                    pe.wait_ge(o_final.sem, o_final.now(it))
                    turn(pA[:, 1, :], o_f, o_turned)
                if in_c:
                    pe.wait_ge(oc_ready.sem, oc_ready.now(it))
                    turn(pC[:, 1, :], c_o[:].rearrange("p h d -> p (h d)"), oc_turned)
                if in_a:
                    pe.wait_ge(oT_ready.sem, oT_ready.now(it))
                    project(pA[:, 0, 256:512], lambda k: o_T[:, k, :], lambda k: w_oa[:, k, :]).then_inc(ya_summed.sem, 1)
                if in_c:
                    pe.wait_ge(ocT_ready.sem, ocT_ready.now(it))
                    project(pC[:, 0, 256:512], lambda k: c_oT[:, k, :], lambda k: w_oc[:, k, :]).then_inc(yc_summed.sem, 1)

            run(pe, body)

        @block.scalar
        def _(act):
            act.wait_ge(loaded.sem, ALL_LOADED)
            act.wait_ge(zeroed.sem, len(zero_fill))
            go = nc.scalar.activation

            def valid(dst, src, scale, bias):
                for k in range(KT):
                    e0 = 0
                    while e0 < NE and WIDTH[e0] > k * P:
                        rows = min(P, WIDTH[e0] - k * P)
                        e1 = e0
                        while e1 < NE and WIDTH[e1] > k * P and min(P, WIDTH[e1] - k * P) == rows:
                            e1 += 1
                        cols = slice(e0 * NTE, e1 * NTE)
                        psl = src[0:rows, k * P + e0 * NTE:k * P + e1 * NTE]
                        if scale is None:
                            last = go(dst[0:rows, k, cols], psl, ACT.Copy)
                        else:
                            last = go(dst[0:rows, k, cols], psl, ACT.Identity, scale=scale[0:rows, k:k + 1],
                                      bias=bias[0:rows, k:k + 1])
                        e0 = e1
                return last

            def mix_out(it, r, bank, which):
                act.wait_ge(mix_summed.sem, mix_summed.now(it, r + 1))
                act.wait_ge(ud_ready.sem, ud_ready.before(it))
                for n, i in enumerate(which):
                    for k in range(KT):
                        last = go(mix[:, i, k, :], pA[:, bank, (n * KT + k) * P:(n * KT + k + 1) * P], ACT.Identity,
                                  bias=x_bias[:, i, k:k + 1])
                last.then_inc(mix_ready.sem, 1)

            def body(it, in_a, in_b, in_c):
                if in_b:
                    act.wait_ge(vb_summed.sem, vb_summed.now(it))
                    act.wait_ge(vb_ready.sem, vb_ready.before(it))
                    go(v_raw[:], pB[:, 0, :], ACT.Copy).then_inc(v_out.sem, 1)
                if in_a:
                    act.wait_ge(a_turned.sem, a_turned.now(it))
                    act.wait_ge(z0_ready.sem, z0_ready.before(it))
                    act.wait_ge(xv_ready.sem, xv_ready.before(it))
                    go(a_xT[:, :, 1:P + 1], pA[:, 0, 0:2 * P].rearrange("p (k t) -> p k t", k=KT), ACT.Copy)\
                        .then_inc(a_xT_ready.sem, 1)
                if in_b:
                    act.wait_ge(b_turned.sem, b_turned.now(it))
                    go(b_xT[:], pB[:, 1, 0:2 * P].rearrange("p (k t) -> p k t", k=KT), ACT.Copy)\
                        .then_inc(b_xT_ready.sem, 1)
                if in_a:
                    act.wait_ge(xx_summed.sem, xx_summed.now(it))
                    go(xx[:, 0, :], pA[:, 1, 0:P], ACT.Tanh).then_inc(xx_ready.sem, 1)
                    go(xx[0:PLR, 1, :], pA[0:PLR, 1, P:2 * P], ACT.Tanh).then_inc(xx_ready.sem, 1)
                    mix_out(it, 0, 0, (0, 1))
                    mix_out(it, 1, 1, (2, 3))
                    mix_out(it, 2, 0, (4,))
                if in_c:
                    act.wait_ge(c_turned.sem, c_turned.now(it))
                    valid(c_xT, pC[:, 0, :], norm_w, norm_b).then_inc(c_xT_ready.sem, 1)
                    act.wait_ge(qk_summed.sem, qk_summed.now(it))
                    for m in range(KT):
                        go(q_c[:, m, :], pC[:, 1, m * P:(m + 1) * P], ACT.Identity,
                           bias=qb_c[:, m:m + 1]).then_inc(qc_ready.sem, 1)
                    for m in range(KT):
                        for h in range(4):
                            rows = slice(h * DH_C, (h + 1) * DH_C)
                            last = go(k_blk[rows, m, h, :], pC[rows, 1, 256 + m * P:256 + (m + 1) * P], ACT.Identity,
                                      bias=kb_c[rows, m:m + 1])
                    last.then_inc(kc_ready.sem, 1)
                if in_a:
                    act.wait_ge(rk_summed.sem, rk_summed.now(it))
                    act.wait_ge(g_summed.sem, g_summed.before(it))
                    go(wg[:], pA[:, 1, 2 * P:3 * P], ACT.Tanh).then_inc(wg_ready.sem, 1)
                    act.wait_ge(quk_ready.sem, quk_ready.before(it))
                    act.wait_ge(fq_ready.sem, fq_ready.before(it))
                    act.wait_ge(fk_ready.sem, fk_ready.before(it))
                    go(qT[:], pA[:, 1, 0:P], ACT.Copy)
                    for h in range(NH_A):
                        rows = slice(h * DK_A, (h + 1) * DK_A)
                        go(q_blkA[rows, h, :], pA[rows, 1, 0:P], ACT.Copy)
                    go(kT[:], pA[:, 1, P:2 * P], ACT.Copy).then_inc(rk_ready.sem, 1)
                    act.wait_ge(w_summed.sem, w_summed.now(it))
                    act.wait_ge(c_parts.sem, c_parts.before(it))
                    go(nw[:], pA[:, 1, 3 * P:4 * P], ACT.Exp, bias=wb[:, 0:1]).then_inc(w_exp.sem, 1)
                if in_b:
                    act.wait_ge(s_summed.sem, s_summed.now(it))
                    act.wait_ge(s_shift.sem, s_shift.before(it))
                    for pair in range(PAIRS):
                        rows = slice(pair * 32, (pair + 1) * 32)
                        last = go(s_d[rows, :, :],
                                  pB[rows, 0, :].rearrange("p (g q h) -> p g q h", q=PAIRS, h=H)[:, :, pair, :],
                                  ACT.Copy, scale=float(DH) ** -0.5)
                    last.then_inc(s_dense.sem, 1)
                if in_a:
                    act.wait_ge(g_ready.sem, g_ready.now(it))
                    act.wait_ge(g_plus1.sem, g_plus1.before(it))
                    go(g_e[:], g_a[:], ACT.Exp, scale=-1.0).then_inc(g_exp.sem, 1)
                    act.wait_ge(decay_dve.sem, decay_dve.now(it))
                    act.wait_ge(decay_pool.sem, decay_pool.now(it))
                    go(edec[:], decay[:], ACT.Exp, scale=-1.0).then_inc(edec_ready.sem, 1)
                if in_b:
                    act.wait_ge(s_shift.sem, s_shift.now(it))
                    act.wait_ge(p_masked.sem, p_masked.before(it))
                    go(s_e[:], s_sh[:], ACT.Exp).then_inc(s_exp.sem, 1)
                if in_c:
                    act.wait_ge(sc_nmax.sem, sc_nmax.now(it))
                    act.wait_ge(sc_recip.sem, sc_recip.before(it))
                    for h in range(NH_C):
                        last = go(c_e[:, h, :], pC[:, h // 4, (h % 4) * P:(h % 4 + 1) * P], ACT.Exp,
                                  scale=float(D) ** -0.5, bias=c_nm[:, h:h + 1], accum_out=c_sum[:, h:h + 1])
                    last.then_inc(sc_exp.sem, 1)
                if in_b:
                    act.wait_ge(ob_summed.sem, ob_summed.now(it))
                    act.wait_ge(yb_summed.sem, yb_summed.before(it))
                    go(o_B[:].rearrange("p j h s -> p s (j h)"), pB[:, 1, :].rearrange("p (s n) -> p s n", s=SB),
                       ACT.Copy).then_inc(ob_ready.sem, 1)
                if in_c:
                    act.wait_ge(pc_turned.sem, pc_turned.now(it))
                    act.wait_ge(oc_summed.sem, oc_summed.before(it))
                    go(c_eT[:], pC[:].rearrange("p b (h q) -> p (b h) q", q=P), ACT.Copy).then_inc(pc_ready.sem, 1)
                if in_a:
                    act.wait_ge(o_turned.sem, o_turned.now(it))
                    go(o_T[:], pA[:, 1, 0:2 * P].rearrange("p (k t) -> p k t", k=KT), ACT.Copy).then_inc(oT_ready.sem, 1)
                if in_c:
                    act.wait_ge(oc_turned.sem, oc_turned.now(it))
                    valid(c_oT, pC[:, 1, :], None, None).then_inc(ocT_ready.sem, 1)

            run(act, body)

        @block.vector
        def _(dve):
            v = nc.vector
            dve.wait_ge(loaded.sem, ALL_LOADED)
            dve.wait_ge(made.sem, MADE)

            def statistics(it, norms):
                for n, src in norms:
                    v.bn_stats(n.st[:], src[:]).then_inc(n.stats.sem, 1)
                for n, src in norms:
                    wait_apart(dve, (n.stats.sem, n.stats.now(it)))
                    v.bn_aggr(n.mv[:], n.st[:]).then_inc(n.aggr.sem, 1)
                for n, src in norms:
                    dve.wait_ge(n.aggr.sem, n.aggr.now(it))
                    v.tensor_scalar(n.v[:], n.mv[:, 1:2], EPS, 0.5, ALU.add, ALU.mult).then_inc(n.var_eps.sem, 1)
                for n, src in norms:
                    dve.wait_ge(n.var_eps.sem, n.var_eps.now(it))
                    v.tensor_scalar(n.bits[:], n.v[:].bitcast(I32), 1, None, ALU.logical_shift_right).then_inc(n.halved.sem, 1)
                for n, src in norms:
                    dve.wait_ge(n.halved.sem, n.halved.now(it))
                    v.tensor_scalar(n.y[:].bitcast(I32), n.bits[:], -1.0, RSQRT_BITS, ALU.mult, ALU.add).then_inc(n.guessed.sem, 1)

            def newton(it, norms):
                for r in range(NEWTON):
                    for n, src in norms:
                        if r:
                            dve.wait_ge(n.newton.sem, n.newton.now(it, 3 * r))
                        else:
                            dve.wait_ge(n.guessed.sem, n.guessed.now(it))
                        v.scalar_tensor_tensor(n.t[:], n.y[:], n.y[:, 0:1], n.v[:], ALU.mult, ALU.mult).then_inc(n.newton.sem, 1)
                    for n, src in norms:
                        dve.wait_ge(n.newton.sem, n.newton.now(it, 3 * r + 1))
                        v.tensor_scalar(n.t[:], n.t[:], -1.0, 1.5, ALU.mult, ALU.add).then_inc(n.newton.sem, 1)
                    for n, src in norms:
                        dve.wait_ge(n.newton.sem, n.newton.now(it, 3 * r + 2))
                        v.tensor_tensor(n.y[:], n.y[:], n.t[:], ALU.mult).then_inc(n.newton.sem, 1)

            def normalise(it, src, dst, n, normed):
                dve.wait_ge(n.newton.sem, n.newton.now(it))
                v.tensor_scalar(dst[:], src[:], n.mv[:, 0:1], n.y[:, 0:1], ALU.subtract, ALU.mult).then_inc(normed.sem, 1)

            def q_spread(it):
                dve.wait_ge(qb_summed.sem, qb_summed.now(it))
                for hh in range(2):
                    rows = slice(hh * DH, (hh + 1) * DH)
                    for par in range(PAR):
                        src = pB[rows, 1, :].rearrange("p (c s q j) -> p s q j c", c=H // 2, s=SB, q=PAR)[:, :, par]
                        dst = q_blk[par * DH:(par + 1) * DH, :, :, par, hh::2]
                        bias = bq[rows].unsqueeze(1).unsqueeze(1).to_broadcast([DH, SB, J, H // 2])
                        last = v.tensor_tensor(dst, src, bias, ALU.add)
                last.then_inc(qb_ready.sem, 1)

            def k_spread(it):
                dve.wait_ge(kb_summed.sem, kb_summed.now(it))
                for hh in range(2):
                    rows = slice(hh * DH, (hh + 1) * DH)
                    for par in range(PAR):
                        src = pB[rows, 0, :].rearrange("p (c r q g) -> p g r q c", c=H // 2, r=PAIRS, q=PAR)[:, :, :, par]
                        dst = k_st[par * DH:(par + 1) * DH].rearrange("p s (j r) h -> p (s j) r h", r=PAIRS)[:, :, :, hh::2]
                        bias = bk[rows].unsqueeze(1).unsqueeze(1).to_broadcast([DH, NG, PAIRS, H // 2])
                        last = v.tensor_tensor(dst, src, bias, ALU.add)
                last.then_inc(kb_ready.sem, 1)

            def shifted_mixes(it, r, i0, n):
                dve.wait_ge(mix_ready.sem, mix_ready.now(it, r + 1))
                d_b = delta[:].unsqueeze(1).to_broadcast([P, n, KT, P])
                v.tensor_tensor(ud[:, i0:i0 + n], mix[:, i0:i0 + n], d_b, ALU.mult).then_inc(ud_ready.sem, 1)
                x_b = a_xT[:, :, 1:P + 1].unsqueeze(1).to_broadcast([P, n, KT, P])
                dve.wait_ge(ud_ready.sem, ud_ready.now(it, r + 1))
                v.tensor_tensor(xv[:, i0:i0 + n], ud[:, i0:i0 + n], x_b, ALU.add).then_inc(xv_ready.sem, 1)

            def keep(it, which):
                for l in which:
                    s = HALVES[l]
                    if l:
                        wait_apart(dve, (att_kept.sem, att_kept.now(it, l)))
                    heads = lambda t: t.rearrange("p h (n s) -> p h n s", s=s)
                    upper = attT[:].rearrange("p h (n u s) -> p h n u s", u=2, s=s)[:, :, :, 1, :]
                    src = pA[:, (l // 2) % 2, (l % 2) * 256:(l % 2 + 1) * 256].rearrange("p (h n s) -> p h n s", h=NH_A, s=s)
                    v.copy_predicated(upper, heads(level_mask[:, l, :, :]), src).then_inc(att_kept.sem, 1)

            def body(it, in_a, in_b, in_c):
                norms = []
                if in_a:
                    dve.wait_ge(x_loaded.sem, x_loaded.now(it))
                    norms.append((norm_a, x_in))
                if in_b:
                    dve.wait_ge(x1_ready.sem, x1_ready.before(it))
                    norms.append((norm_of_b, x1))
                if in_c:
                    dve.wait_ge(x2_ready.sem, x2_ready.before(it))
                    norms.append((norm_c, x2))
                statistics(it, norms)
                newton(it, norms)
                if in_a:
                    dve.wait_ge(a_turned.sem, a_turned.before(it))
                    normalise(it, x_in, a_xn, norm_a, a_normed)
                if in_b:
                    dve.wait_ge(b_turned.sem, b_turned.before(it))
                    normalise(it, x1, b_xn, norm_of_b, b_normed)
                if in_c:
                    dve.wait_ge(x23_ready.sem, x23_ready.before(it))
                    normalise(it, x2, x3, norm_c, x3_ready)
                    dve.wait_ge(x3_ready.sem, x3_ready.now(it))
                    statistics(it, [(norm_d, x3)])
                if in_a:
                    dve.wait_ge(a_xT_ready.sem, a_xT_ready.now(it))
                    v.tensor_tensor(delta[:], a_xT[:, :, 0:P], a_xT[:, :, 1:P + 1], ALU.subtract).then_inc(delta_ready.sem, 1)
                    dve.wait_ge(delta_ready.sem, delta_ready.now(it))
                    dve.wait_ge(xx_summed.sem, xx_summed.before(it))
                    for k in range(KT):
                        v.scalar_tensor_tensor(z0[:, k, :], delta[:, k, :], mu0[:, k:k + 1], a_xT[:, k, 1:P + 1],
                                               ALU.mult, ALU.add).then_inc(z0_ready.sem, 1)
                if in_c:
                    dve.wait_ge(c_turned.sem, c_turned.before(it))
                    normalise(it, x3, c_xn, norm_d, c_normed)
                if in_b:
                    dve.wait_ge(s_summed.sem, s_summed.before(it))
                    k_spread(it)
                if in_a:
                    shifted_mixes(it, 0, 0, 2)
                    shifted_mixes(it, 1, 2, 2)
                    shifted_mixes(it, 2, 4, 1)
                if in_b:
                    q_spread(it)
                if in_c:
                    dve.wait_ge(vc_summed.sem, vc_summed.now(it))
                    dve.wait_ge(oc_summed.sem, oc_summed.before(it))
                    v.tensor_tensor(v_c[:], pC[:, 0, 256:512], vb_bc[:], ALU.add).then_inc(vc_ready.sem, 1)
                if in_a:
                    dve.wait_ge(v_summed.sem, v_summed.now(it))
                    v.tensor_copy(v_a[:], pA[:, 0, 0:VD]).then_inc(v_ready.sem, 1)
                    dve.wait_ge(rk_ready.sem, rk_ready.now(it))
                    dve.wait_ge(att_summed.sem, att_summed.before(it))
                    v.scalar_tensor_tensor(quk[:], qT[:], bonus[:, 0:1], kT[:], ALU.mult, ALU.mult).then_inc(quk_ready.sem, 1)
                    dve.wait_ge(g_summed.sem, g_summed.now(it))
                    dve.wait_ge(gate_ready.sem, gate_ready.before(it))
                    v.tensor_tensor(g_a[:], pA[:, 0, VD:2 * VD], gb_bc[:], ALU.add).then_inc(g_ready.sem, 1)
                    dve.wait_ge(w_exp.sem, w_exp.now(it))
                    v.tensor_tensor_scan(c_in[:], chunk_keep[:], nw[:], 0.0, ALU.mult, ALU.add).then_inc(c_in_ready.sem, 1)
                    dve.wait_ge(c_in_ready.sem, c_in_ready.now(it))
                    dve.wait_ge(decay_pool.sem, decay_pool.before(it))
                    tot = c_in[:].rearrange("p (c t) -> p c t", t=CHUNK)[:, :, CHUNK - 1:CHUNK]
                    v.tensor_tensor(c_ex[:], c_in[:], nw[:], ALU.subtract).then_inc(c_parts.sem, 1)
                    v.tensor_tensor(c_rest[:].rearrange("p (c t) -> p c t", t=CHUNK), tot.to_broadcast([P, P // CHUNK, CHUNK]),
                                    c_in[:].rearrange("p (c t) -> p c t", t=CHUNK), ALU.subtract).then_inc(c_parts.sem, 1)
                if in_b:
                    dve.wait_ge(s_dense.sem, s_dense.now(it))
                    v.reduce_max(s_mx[:], s_d[:], AX_X).then_inc(s_max.sem, 1)
                    dve.wait_ge(s_max.sem, s_max.now(it))
                    v.tensor_tensor(s_sh[:], s_d[:], s_mx[:].unsqueeze(2).to_broadcast([P, NG, H]), ALU.subtract)\
                        .then_inc(s_shift.sem, 1)
                if in_a:
                    dve.wait_ge(c_parts.sem, c_parts.now(it))
                    dve.wait_ge(edec_ready.sem, edec_ready.before(it))
                    C_ = CHUNK
                    v.tensor_copy(decay[:, 1, :].rearrange("p (n u t) -> p n u t", u=2, t=C_)[:, :, 0, :],
                                  c_rest[:].rearrange("p (n u t) -> p n u t", u=2, t=C_)[:, :, 0, :]).then_inc(decay_dve.sem, 1)
                    v.tensor_scalar(decay[:, 0, 0:C_], c_rest[:, 0:C_], c_in[:, 2 * C_ - 1:2 * C_], None, ALU.add)\
                        .then_inc(decay_dve.sem, 1)
                    v.tensor_scalar(decay[:, 0, 3 * C_:], c_ex[:, 3 * C_:], c_in[:, 3 * C_ - 1:3 * C_], None, ALU.add)\
                        .then_inc(decay_dve.sem, 1)
                    for l in range(2, NL):
                        s = HALVES[l]
                        n = P // (2 * s)
                        view = lambda t: t.rearrange("p (n u s) -> p n u s", u=2, s=s)
                        ref = view(c_in[:])[:, :, 0, s - 1:s].to_broadcast([P, n, s])
                        v.tensor_tensor(view(decay[:, l, :])[:, :, 1, :], view(c_ex[:])[:, :, 1, :], ref, ALU.subtract)
                        v.tensor_tensor(view(decay[:, l, :])[:, :, 0, :], ref, view(c_in[:])[:, :, 0, :], ALU.subtract)\
                            .then_inc(decay_dve.sem, 2 if l > 2 else 1)
                if in_c:
                    dve.wait_ge(sc_summed.sem, sc_summed.now(it))
                    v.reduce_max(c_mx[:], pC[:].rearrange("p b (h k) -> p (b h) k", k=P), AX_X).then_inc(sc_max.sem, 1)
                    dve.wait_ge(sc_max.sem, sc_max.now(it))
                    v.tensor_scalar(c_nm[:], c_mx[:], -float(D) ** -0.5, None, ALU.mult).then_inc(sc_nmax.sem, 1)
                if in_b:
                    dve.wait_ge(s_exp.sem, s_exp.now(it))
                    v.reduce_sum(s_sum[:], s_e[:], AX_X).then_inc(s_total.sem, 1)
                    dve.wait_ge(s_total.sem, s_total.now(it))
                    v.reciprocal(s_r[:], s_sum[:]).then_inc(s_recip.sem, 1)
                    dve.wait_ge(s_recip.sem, s_recip.now(it))
                    v.tensor_tensor(s_rm[:], s_r[:].unsqueeze(2).to_broadcast([P, NG, PAR]),
                                    par_mask[:].unsqueeze(1).to_broadcast([P, NG, PAR]), ALU.mult).then_inc(s_scale.sem, 1)
                    dve.wait_ge(s_scale.sem, s_scale.now(it))
                    v.tensor_tensor(p_m[:], s_e[:].unsqueeze(2).to_broadcast([P, NG, PAR, H]),
                                    s_rm[:].unsqueeze(3).to_broadcast([P, NG, PAR, H]), ALU.mult).then_inc(p_masked.sem, 1)
                if in_a:
                    dve.wait_ge(edec_ready.sem, edec_ready.now(it))
                    for l, s in enumerate(HALVES):
                        n = P // (2 * s)
                        upper = lambda t: t.rearrange("p h (n u s) -> p h n u s", u=2, s=s)[:, :, :, 1, :]
                        e_b = edec[:, l, :].rearrange("p (n u s) -> p n u s", u=2, s=s)[:, :, 1, :]
                        v.tensor_tensor(f_q[:, l, :, :].rearrange("p h (n s) -> p h n s", s=s),
                                        e_b.unsqueeze(1).to_broadcast([P, NH_A, n, s]), upper(q_blkA[:]), ALU.mult)\
                            .then_inc(fq_ready.sem, 1)
                if in_b:
                    dve.wait_ge(p_masked.sem, p_masked.now(it))
                    dve.wait_ge(ob_summed.sem, ob_summed.before(it))
                    for pair in range(PAIRS):
                        rows = slice(pair * 32, (pair + 1) * 32)
                        last = v.transpose(p_T[rows, :, pair, :, :].rearrange("p g a h -> p g (a h)"),
                                           p_m[rows].rearrange("p g a h -> p g (a h)"))
                    last.then_inc(p_turned.sem, 1)
                if in_a:
                    wait_apart(dve, (att_summed.sem, att_summed.now(it, 1)), (oa_summed.sem, oa_summed.before(it)))
                    keep(it, (0, 1))
                    dve.wait_ge(g_exp.sem, g_exp.now(it))
                    v.tensor_scalar(g_1[:], g_e[:], 1.0, None, ALU.add).then_inc(g_plus1.sem, 1)
                    wait_apart(dve, (att_summed.sem, att_summed.now(it, 2)))
                    keep(it, (2, 3))
                    dve.wait_ge(g_plus1.sem, g_plus1.now(it))
                    v.reciprocal(g_r[:], g_1[:]).then_inc(g_recip.sem, 1)
                    wait_apart(dve, (att_summed.sem, att_summed.now(it, 3)))
                    keep(it, (4, 5))
                    dve.wait_ge(g_recip.sem, g_recip.now(it))
                    dve.wait_ge(gates_ready.sem, gates_ready.before(it))
                    v.tensor_tensor(gate[:], g_a[:], g_r[:], ALU.mult).then_inc(gate_ready.sem, 1)
                    wait_apart(dve, (att_summed.sem, att_summed.now(it, 4)))
                    keep(it, (6,))
                    v.tensor_copy(dterm[:], pA[:, 1, 256:256 + NH_A]).then_inc(dterm_ready.sem, 1)
                    dve.wait_ge(dterm_ready.sem, dterm_ready.now(it))
                    dve.wait_ge(v_ready.sem, v_ready.now(it))
                    v.tensor_tensor(dv[:].rearrange("p (h d) -> p h d", h=NH_A), v_a[:].rearrange("p (h d) -> p h d", h=NH_A),
                                    dterm[:].unsqueeze(2).to_broadcast([P, NH_A, DV_A]), ALU.mult).then_inc(dv_ready.sem, 1)
                    dve.wait_ge(oa_summed.sem, oa_summed.now(it))
                    dve.wait_ge(dv_ready.sem, dv_ready.now(it))
                    v.tensor_tensor(o_a[:], pA[:, 0, 0:VD], dv[:], ALU.add).then_inc(oa_ready.sem, 1)
                    dve.wait_ge(oa_ready.sem, oa_ready.now(it))
                    statistics(it, [(norm_o, o_a)])
                if in_c:
                    dve.wait_ge(sc_exp.sem, sc_exp.now(it))
                    v.reciprocal(c_r[:], c_sum[:]).then_inc(sc_recip.sem, 1)
                    dve.wait_ge(sc_recip.sem, sc_recip.now(it))
                    dve.wait_ge(oc_summed.sem, oc_summed.now(it))
                    v.tensor_tensor(c_o[:], pC[:, 0, 0:D].rearrange("p (h d) -> p h d", d=DH_C),
                                    c_r[:].unsqueeze(2).to_broadcast([P, NH_C, DH_C]), ALU.mult).then_inc(oc_ready.sem, 1)
                if in_a:
                    normalise(it, o_a, o_n, norm_o, o_normed)
                    dve.wait_ge(o_normed.sem, o_normed.now(it))
                    dve.wait_ge(gates_ready.sem, gates_ready.now(it))
                    v.tensor_tensor(o_g[:], o_n[:], gate_g[:], ALU.mult).then_inc(o_scaled.sem, 1)
                    dve.wait_ge(o_scaled.sem, o_scaled.now(it))
                    dve.wait_ge(o_turned.sem, o_turned.before(it))
                    v.tensor_tensor(o_f[:], o_g[:], gate_b[:], ALU.add).then_inc(o_final.sem, 1)
                if in_b:
                    dve.wait_ge(yb_summed.sem, yb_summed.now(it))
                    dve.wait_ge(x1bo_ready.sem, x1bo_ready.now(it))
                    if in_c:
                        dve.wait_ge(x23_ready.sem, x23_ready.now(it))
                    v.tensor_tensor(x2[:], pB[:, 0, 0:D], x1_bo[:], ALU.add).then_inc(x2_ready.sem, 1)
                if in_a:
                    dve.wait_ge(ya_summed.sem, ya_summed.now(it))
                    if in_b:
                        dve.wait_ge(x1bo_ready.sem, x1bo_ready.now(it))
                    v.tensor_tensor(x1[:], pA[:, 0, 256:512], x_in[:], ALU.add).then_inc(x1_ready.sem, 1)
                if in_c:
                    dve.wait_ge(yc_summed.sem, yc_summed.now(it))
                    dve.wait_ge(res_begun.sem, res_begun.now(it))
                    for e in range(NE):
                        rows = slice(e * NTE, (e + 1) * NTE)
                        v.tensor_tensor(res[rows, 0:WIDTH[e]], pC[rows, 0, 256:256 + WIDTH[e]], res[rows, 0:WIDTH[e]],
                                        ALU.add).then_inc(res_ready.sem, 1)

            run(dve, body)


def kernel(**inputs):
    import numpy as _np
    import concourse.bacc as _bacc
    from concourse import mybir as _mybir
    from concourse.bass_utils import run_bass_kernel_spmd as _run

    p = {k.replace("L0_", ""): _np.asarray(v) for k, v in inputs.items()}
    con = _np.ascontiguousarray
    col = lambda t: con(t.reshape(-1, P).T)
    row = lambda t: con(t.reshape(1, -1))
    wo = p["xattn_Wo"].T.reshape(PAR, J, DH, D).transpose(1, 0, 2, 3).reshape(HD, D)
    laid = {
        "x": con(p["x"]), 
        "ctxT": con(p["ctx_1024"].reshape(B, SB, PAR, J // PAIRS, PAIRS, D).transpose(0, 5, 4, 2, 1, 3).reshape(B, D, P)),
        "mu0": col(p["attn_mu0"]), "Wx0": con(p["attn_Wx0"].T), "Wx2": con(p["attn_Wx2"].T),
        "x_bias": con(p["attn_x_bias"].reshape(NMIX * KT, P).T),
        "rW": con(p["attn_rW"].T), "kW": con(p["attn_kW"].T), "vW": con(p["attn_vW"].T),
        "wA": con(p["attn_wA"].T), "wB": con(p["attn_wB"].T), "wb": con(p["attn_wb"].reshape(P, 1)),
        "gA": con(p["attn_gA"].T), "gB": con(p["attn_gB"].T), "gb": row(p["attn_gb"]),
        "bonus": con(p["attn_bonus"].reshape(P, 1)), "ln_g": row(p["attn_ln_g"]), "ln_b": row(p["attn_ln_b"]),
        "oWa": con(p["attn_oW"].T),
        "Wq": con(p["xattn_Wq"].T), "Wk": con(p["xattn_Wk"].T), "Wv": con(p["xattn_Wv"].T), "Wo": con(wo),
        "bq": col(p["xattn_bq"]), "bk": col(p["xattn_bk"]), "bv": row(p["xattn_bv"]), "bo": row(p["xattn_bo"]),
        "norm_w": col(p["ffn_norm_w"]), "norm_b": col(p["ffn_norm_b"]),
        "q_w": con(p["ffn_q_w"].T), "k_w": con(p["ffn_k_w"].T), "v_w": con(p["ffn_v_w"].T), "o_w": con(p["ffn_o_w"].T),
        "q_b": col(p["ffn_q_b"]), "k_b": col(p["ffn_k_b"]), "v_b": row(p["ffn_v_b"]), "o_b": row(p["ffn_o_b"]),
    }
    nc = _bacc.Bacc("TRN2", target_bir_lowering=False, num_devices=1)
    arrays, args = {}, {}
    for name, t in laid.items():
        arrays[f"in_{name}"] = t
        args[name] = nc.dram_tensor(f"in_{name}", t.shape, _mybir.dt.from_np(t.dtype), kind="ExternalInput").ap()
    out = nc.dram_tensor("out_0", (B, P, D), _mybir.dt.float32, kind="ExternalOutput").ap()
    decoder_layer(nc, args, out)
    r = _run(nc, [arrays], core_ids=[0])
    return r.results[0]["out_0"]
```

```python
from contextlib import ExitStack

import concourse.bass as bass
from concourse import mybir

F32 = mybir.dt.float32
I32 = mybir.dt.int32
ALU = mybir.AluOpType
ACT = mybir.ActivationFunctionType
AX_X = mybir.AxisListType.X

P = 128
B = 16
D = 256
KT = D // P
EPS = 1e-5
RSQRT_BITS = float(0x5F3759DF - 0x400000)
NEWTON = 3

NMIX, PLR, GLR = 5, 32, 64
KD, VD, NH_A = 128, 256, 4
DK_A, DV_A = KD // NH_A, VD // NH_A
CHUNK = 32
HALVES = [64, 32, 16, 8, 4, 2, 1]
NL = len(HALVES)

H, DH = 16, 64
HD = H * DH
SB, PAR, J = 8, 2, 8
PAIRS = 4
NG = SB * J // PAIRS

NE, NH_C = 4, 8
NTE = P // NE
DH_C = D // NH_C
WIDTH = [D >> e for e in range(NE)]

LAG_N, LAG_A, LAG_B, LAG_C = 0, 1, 2, 3


class Signal:

    def __init__(self, sem, lag, per):
        self.sem, self.lag, self.per = sem, lag, per

    def now(self, step, k=None):
        return (step - self.lag) * self.per + (self.per if k is None else k)

    def before(self, step):
        return (step - self.lag) * self.per


def decoder_layer(nc, a, out):
    ctx = ExitStack()
    with ctx:
        def sb(name, shape, dt=F32):
            return ctx.enter_context(nc.sbuf_tensor(name, shape, dt))

        def psum(name, shape):
            return ctx.enter_context(nc.psum_tensor(name, shape, F32))

        def sig(name, lag, per=1):
            return Signal(ctx.enter_context(nc.semaphore(name)), lag, per)

        w_x0 = sb("w_x0", [P, KT, NMIX * PLR])
        w_mix = sb("w_mix", [P, NMIX, D])
        w_r = sb("w_r", [P, KT, KD])
        w_k = sb("w_k", [P, KT, KD])
        w_v = sb("w_v", [P, KT, VD])
        w_wa = sb("w_wa", [P, KT, GLR])
        w_ga = sb("w_ga", [P, KT, GLR])
        w_wgb = sb("w_wgb", [P, VD])
        w_oa = sb("w_oa", [P, KT, D])
        mu0 = sb("mu0", [P, KT])
        x_bias = sb("x_bias", [P, NMIX, KT])
        wb = sb("wb", [P, 1])
        bonus = sb("bonus", [P, 1])
        gb_bc = sb("gb_bc", [P, VD])
        lng_half = sb("lng_half", [P, VD])
        lnb_half = sb("lnb_half", [P, VD])
        w_q = sb("w_q", [P, KT, HD])
        w_kb = sb("w_kb", [P, KT, HD])
        w_vb = sb("w_vb", [P, KT, HD])
        w_ob = sb("w_ob", [P, J, D])
        bq = sb("bq", [P, H // 2])
        bk = sb("bk", [P, H])
        bv_bc = sb("bv_bc", [P, HD])
        bo_bc = sb("bo_bc", [P, D])
        w_qc = sb("w_qc", [P, KT, D])
        w_kc = sb("w_kc", [P, KT, D])
        w_vc = sb("w_vc", [P, KT, D])
        w_oc = sb("w_oc", [P, KT, D])
        norm_w = sb("norm_w", [P, KT])
        norm_b = sb("norm_b", [P, KT])
        qb_c = sb("qb_c", [P, KT])
        kb_c = sb("kb_c", [P, KT])
        vb_bc = sb("vb_bc", [P, D])
        ob_valid = sb("ob_valid", [P, D])
        ident = sb("ident", [P, P])
        zeros = sb("zeros", [P, P])
        three_halves = sb("three_halves", [P, 1])
        level_mask = sb("level_mask", [P, NL, NH_A, P // 2], I32)
        head_ones = sb("head_ones", [P, NH_A])
        par_mask = sb("par_mask", [P, PAR])
        chunk_keep = sb("chunk_keep", [P, P])

        x_in = sb("x_in", [P, D])
        x_keep = sb("x_keep", [P, D])
        a_xn = sb("a_xn", [P, D])
        a_xT = sb("a_xT", [P, KT, P + 1])
        delta = sb("delta", [P, KT, P])
        z0 = sb("z0", [P, KT, P])
        xx = sb("xx", [P, 2, P])
        mix = sb("mix", [P, NMIX, KT, P])
        ud = sb("ud", [P, NMIX, KT, P])
        xv = sb("xv", [P, NMIX, KT, P])
        wg = sb("wg", [P, P])
        qT = sb("qT", [P, P]); kT = sb("kT", [P, P])
        v_a = sb("v_a", [P, VD])
        g_a = sb("g_a", [P, VD]); g_t = sb("g_t", [P, VD]); g_gt = sb("g_gt", [P, VD])
        gate = sb("gate", [P, VD]); gate_g = sb("gate_g", [P, VD]); gate_b = sb("gate_b", [P, VD])
        nw = sb("nw", [P, P]); c_in = sb("c_in", [P, P]); c_ex = sb("c_ex", [P, P]); c_rest = sb("c_rest", [P, P])
        decay = sb("decay", [P, NL, P]); edec = sb("edec", [P, NL, P])
        q_blkA = sb("q_blkA", [P, NH_A, P])
        f_q = sb("f_q", [P, NL, NH_A, P // 2]); f_k = sb("f_k", [P, NL, P])
        quk = sb("quk", [P, P]); dterm = sb("dterm", [P, NH_A])
        attT = sb("attT", [P, NH_A, P])
        dv = sb("dv", [P, VD]); o_a = sb("o_a", [P, VD])
        o_n = sb("o_n", [P, VD]); o_g = sb("o_g", [P, VD]); o_f = sb("o_f", [P, VD])
        o_T = sb("o_T", [P, KT, P])
        x1 = sb("x1", [P, D])

        ctxT = sb("ctxT", [P, KT, P])
        b_xn = sb("b_xn", [P, D])
        b_xT = sb("b_xT", [P, KT, P])
        x1_bo = sb("x1_bo", [P, D])
        q_blk = sb("q_blk", [P, SB, J, PAR, H])
        k_st = sb("k_st", [P, SB, J, H])
        v_raw = sb("v_raw", [P, HD])
        v_tok = sb("v_tok", [P, H, DH])
        v_g = sb("v_g", [P, NG, DH])
        s_d = sb("s_d", [P, NG, H])
        s_mx = sb("s_mx", [P, NG]); s_sh = sb("s_sh", [P, NG, H]); s_e = sb("s_e", [P, NG, H])
        s_sum = sb("s_sum", [P, NG]); s_r = sb("s_r", [P, NG]); s_rm = sb("s_rm", [P, NG, PAR])
        p_m = sb("p_m", [P, NG, PAR, H])
        p_T = sb("p_T", [P, NG, PAIRS, PAR, H])
        o_B = sb("o_B", [P, J, H, SB])
        x2 = sb("x2", [P, D])

        x3 = sb("x3", [P, D])
        c_xn = sb("c_xn", [P, D])
        x23 = sb("x23", [P, D]); res = sb("res", [P, D])
        c_xT = sb("c_xT", [P, KT, P])
        q_c = sb("q_c", [P, KT, P])
        k_blk = sb("k_blk", [P, KT, 4, P])
        v_c = sb("v_c", [P, D])
        c_mx = sb("c_mx", [P, NH_C]); c_nm = sb("c_nm", [P, NH_C])
        c_e = sb("c_e", [P, NH_C, P]); c_sum = sb("c_sum", [P, NH_C]); c_r = sb("c_r", [P, NH_C])
        c_eT = sb("c_eT", [P, NH_C, P])
        c_o = sb("c_o", [P, NH_C, DH_C])
        c_oT = sb("c_oT", [P, KT, P])

        pA = psum("pA", [P, 2, 512])
        pC = psum("pC", [P, 2, 512])
        pB = psum("pB", [P, 2, 1024])

        loaded_a = sig("loaded_a", 0); loaded_bc = sig("loaded_bc", 0); ln_halved = sig("ln_halved", 0)
        zeroed = sig("zeroed", 0); zeroed_bc = sig("zeroed_bc", 0); made = sig("made", 0)
        MADE = 7 + NL * (3 + NH_A) + PAR * (3 + PAIRS)
        N, A, Bl, C = LAG_N, LAG_A, LAG_B, LAG_C
        x_loaded = sig("x_loaded", N, 16)
        a_normed = sig("a_normed", N)
        x_kept = sig("x_kept", A)
        a_turned = sig("a_turned", A); a_xT_ready = sig("a_xT_ready", A)
        delta_ready = sig("delta_ready", A); z0_ready = sig("z0_ready", A, 2)
        xx_summed = sig("xx_summed", A); xx_ready = sig("xx_ready", A, 2)
        mix_summed = sig("mix_summed", A, 3); mix_ready = sig("mix_ready", A, 3)
        ud_ready = sig("ud_ready", A, 2); xv_ready = sig("xv_ready", A, 2); ud_last = sig("ud_last", A); xv_last = sig("xv_last", A)
        rk_summed = sig("rk_summed", A); v_summed = sig("v_summed", A); w1_summed = sig("w1_summed", A); w1_ready = sig("w1_ready", A); g1_ready = sig("g1_ready", A)
        w_summed = sig("w_summed", A); g_summed = sig("g_summed", A)
        rk_ready = sig("rk_ready", A); v_ready = sig("v_ready", A)
        w_exp = sig("w_exp", A); g_ready = sig("g_ready", A); g_tanh = sig("g_tanh", A); g_times = sig("g_times", A)
        gate_ready = sig("gate_ready", A); gates_ready = sig("gates_ready", A, 2)
        c_in_ready = sig("c_in_ready", A); c_parts = sig("c_parts", A, 2)
        decay_dve = sig("decay_dve", A, 12); decay_pool = sig("decay_pool", A, 4)
        edec_ready = sig("edec_ready", A); fq_ready = sig("fq_ready", A, NL); fk_ready = sig("fk_ready", A, 2)
        quk_ready = sig("quk_ready", A); att_summed = sig("att_summed", A, 4); att_kept = sig("att_kept", A, NL)
        dterm_ready = sig("dterm_ready", A); dv_ready = sig("dv_ready", A)
        oa_summed = sig("oa_summed", A); oa_ready = sig("oa_ready", A)
        o_normed = sig("o_normed", A)
        o_scaled = sig("o_scaled", A); o_final = sig("o_final", A); o_turned = sig("o_turned", A); oT_ready = sig("oT_ready", A)
        ya_summed = sig("ya_summed", A); x1_ready = sig("x1_ready", A)

        ctx_loaded = sig("ctx_loaded", Bl, 16)
        b_normed = sig("b_normed", Bl)
        b_turned = sig("b_turned", Bl); b_xT_ready = sig("b_xT_ready", Bl); x1bo_ready = sig("x1bo_ready", Bl)
        vb_summed = sig("vb_summed", Bl); v_out = sig("v_out", Bl); vb_ready = sig("vb_ready", Bl); vg_moved = sig("vg_moved", Bl, 16 * NG)
        kb_summed = sig("kb_summed", Bl); k_moved = sig("k_moved", Bl); kb_ready = sig("kb_ready", Bl); qb_summed = sig("qb_summed", Bl, 2); qb_ready = sig("qb_ready", Bl, 2)
        s_summed = sig("s_summed", Bl); s_dense = sig("s_dense", Bl); s_max = sig("s_max", Bl); s_shift = sig("s_shift", Bl)
        s_exp = sig("s_exp", Bl); s_total = sig("s_total", Bl); s_recip = sig("s_recip", Bl); s_scale = sig("s_scale", Bl)
        p_masked = sig("p_masked", Bl); p_turned = sig("p_turned", Bl)
        ob_summed = sig("ob_summed", Bl); ob_ready = sig("ob_ready", Bl)
        yb_summed = sig("yb_summed", Bl); x2_ready = sig("x2_ready", Bl)

        x3_ready = sig("x3_ready", C)
        c_normed = sig("c_normed", C)
        x23_ready = sig("x23_ready", C); res_begun = sig("res_begun", C)
        c_turned = sig("c_turned", C); c_xT_ready = sig("c_xT_ready", C)
        qk_summed = sig("qk_summed", C); vc_summed = sig("vc_summed", C)
        qc_ready = sig("qc_ready", C, 2); kc_ready = sig("kc_ready", C); vc_ready = sig("vc_ready", C)
        sc_summed = sig("sc_summed", C); sc_max = sig("sc_max", C); sc_nmax = sig("sc_nmax", C); sc_exp = sig("sc_exp", C)
        pc_turned = sig("pc_turned", C); pc_ready = sig("pc_ready", C); sc_recip = sig("sc_recip", C)
        oc_summed = sig("oc_summed", C); oc_ready = sig("oc_ready", C); oc_turned = sig("oc_turned", C); ocT_ready = sig("ocT_ready", C)
        yc_summed = sig("yc_summed", C); res_ready = sig("res_ready", C, NE); stored = sig("stored", C, 16)

        class Norm:

            def __init__(self, name, lag, per):
                self.st, self.mv = sb(name + "_st", [P, 6]), sb(name + "_mv", [P, 2])
                self.v, self.y, self.t = (sb(f"{name}_{x}", [P, 1]) for x in "vyt")
                self.bits = sb(name + "_bits", [P, 1], I32)
                self.stats, self.aggr = sig(name + "_stats", lag), sig(name + "_aggr", lag)
                self.var_eps, self.halved = sig(name + "_var_eps", lag), sig(name + "_halved", lag)
                self.guessed, self.newton = sig(name + "_guessed", lag), sig(name + "_newton", lag, per * NEWTON)

        norm_a, norm_of_b, norm_c, norm_d, norm_o = (Norm(*x) for x in (
            ("norm_a", N, 3), ("norm_of_b", Bl, 3), ("norm_c", C, 3), ("norm_d", C, 4), ("norm_o", A, 4)))

        block = ctx.enter_context(nc.Block())

        def wait_apart(engine, *waits):
            waits = [(sem, value if isinstance(value, int) else engine.to_reg(value)) for sem, value in waits]
            engine.wait_ge(x_loaded.sem, 16)
            for sem, value in waits:
                engine.wait_ge(sem, value)

        def run(engine, body, computes=True):
            in_batch = lambda step: [lag <= step < B + lag for lag in (LAG_N, LAG_A, LAG_B, LAG_C)]
            for step in range(LAG_C + 1):
                if step == LAG_A and computes:
                    engine.wait_ge(loaded_a.sem, 16 * len(weights_a))
                    engine.wait_ge(made.sem, MADE)
                    engine.wait_ge(ln_halved.sem, 2)
                if step == LAG_B and computes:
                    engine.wait_ge(loaded_bc.sem, 16 * len(weights_bc))
                    engine.wait_ge(zeroed_bc.sem, len(zero_fill_bc))
                body(step, *in_batch(step))
            with engine.Fori(LAG_C + 1, B) as step:
                body(step, True, True, True, True)
            for step in range(B, B + LAG_C):
                body(step, *in_batch(step))

        weights_a = [
            (w_x0[:], a["Wx0"].rearrange("(k p) n -> p k n", p=P)),
            (mu0[:], a["mu0"]),
            (w_mix[0:PLR, NMIX - 1, :], a["Wx2"][(NMIX - 1) * PLR:NMIX * PLR, :]),
            (w_r[:], a["rW"].rearrange("(k p) n -> p k n", p=P)),
            (w_k[:], a["kW"].rearrange("(k p) n -> p k n", p=P)),
            (w_v[:], a["vW"].rearrange("(k p) n -> p k n", p=P)),
            (w_wa[:], a["wA"].rearrange("(k p) n -> p k n", p=P)),
            (w_ga[:], a["gA"].rearrange("(k p) n -> p k n", p=P)),
            (w_wgb[0:GLR, 0:KD], a["wB"]), (w_wgb[GLR:2 * GLR, :], a["gB"]),
            (w_oa[:], a["oWa"].rearrange("(k p) n -> p k n", p=P)),
            (x_bias[:], a["x_bias"].rearrange("p (i k) -> p i k", k=KT)),
            (wb[:], a["wb"]), (bonus[:], a["bonus"]),
            (gb_bc[:], a["gb"].to_broadcast([P, VD])),
            (lng_half[:], a["ln_g"].to_broadcast([P, VD])), (lnb_half[:], a["ln_b"].to_broadcast([P, VD])),
        ]
        weights_a[3:3] = [(w_mix[i * PLR:(i + 1) * PLR, i, :], a["Wx2"][i * PLR:(i + 1) * PLR, :]) for i in range(NMIX - 1)]
        weights_bc = [
            (w_vb[:], a["Wv"].rearrange("(k p) n -> p k n", p=P)),
            (w_kb[:], a["Wk"].rearrange("(k p) n -> p k n", p=P)),
            (w_q[:], a["Wq"].rearrange("(k p) n -> p k n", p=P)),
            (w_ob[:], a["Wo"].rearrange("(j p) n -> p j n", p=P)),
            (bq[:], a["bq"]), (bk[:], a["bk"]),
            (bv_bc[:], a["bv"].to_broadcast([P, HD])), (bo_bc[:], a["bo"].to_broadcast([P, D])),
            (w_qc[:], a["q_w"].rearrange("(k p) n -> p k n", p=P)),
            (w_kc[:], a["k_w"].rearrange("(k p) n -> p k n", p=P)),
            (w_vc[:], a["v_w"].rearrange("(k p) n -> p k n", p=P)),
            (w_oc[:], a["o_w"].rearrange("(k p) n -> p k n", p=P)),
            (norm_w[:], a["norm_w"]), (norm_b[:], a["norm_b"]), (qb_c[:], a["q_b"]), (kb_c[:], a["k_b"]),
            (vb_bc[:], a["v_b"].to_broadcast([P, D])),
        ]
        weights_bc += [(ob_valid[e * NTE:(e + 1) * NTE, 0:WIDTH[e]], a["o_b"][:, 0:WIDTH[e]].to_broadcast([NTE, WIDTH[e]]))
                       for e in range(NE)]
        zero_fill = [w_mix[:, 0:NMIX - 1, :], ident, a_xT, zeros, head_ones, par_mask, attT, q_blkA]
        zero_fill_bc = [ob_valid, q_blk, p_T, c_xT, k_blk, c_oT]

        @block.sync
        def _(sp):
            def load_weights():
                sp.wait_ge(zeroed.sem, 1)
                for dst, src in weights_a:
                    sp.dma_start(dst, src).then_inc(loaded_a.sem, 16)
                sp.wait_ge(zeroed_bc.sem, len(zero_fill_bc))
                for dst, src in weights_bc:
                    sp.dma_start(dst, src).then_inc(loaded_bc.sem, 16)

            def body(it, in_n, in_a, in_b, in_c):
                if in_b:
                    sp.wait_ge(kb_summed.sem, kb_summed.before(it))
                    sp.dma_start(ctxT[:], a["ctxT"][it - LAG_B].rearrange("(k p) t -> p k t", p=P)).then_inc(ctx_loaded.sem, 16)
                if in_n:
                    sp.wait_ge(a_normed.sem, a_normed.before(it))
                    if in_a:
                        sp.wait_ge(x_kept.sem, x_kept.now(it))
                    sp.dma_start(x_in[:], a["x"][it - LAG_N]).then_inc(x_loaded.sem, 16)
                if isinstance(it, int) and it == LAG_N:
                    load_weights()
                if not isinstance(it, int) or it > LAG_C:
                    sp.wait_ge(res_ready.sem, res_ready.before(it))
                    sp.dma_start(out[it - 1 - LAG_C], res[:]).then_inc(stored.sem, 16)
                if in_b:
                    sp.wait_ge(vb_ready.sem, vb_ready.now(it))
                    sp.wait_ge(ob_summed.sem, ob_summed.before(it))
                    for g in range(NG):
                        sp.dma_start(v_g[:, g, :], v_tok[g:P:NG, :, :]).then_inc(vg_moved.sem, 16)

            run(sp, body, computes=False)
            sp.wait_ge(res_ready.sem, NE * B)
            sp.dma_start(out[B - 1], res[:]).then_inc(stored.sem, 16)
            sp.wait_ge(stored.sem, 16 * B)

        @block.gpsimd
        def _(pool):
            for t in zero_fill:
                nc.gpsimd.memset(t if isinstance(t, bass.AP) else t[:], 0.0).then_inc(zeroed.sem, 1)
            pool.wait_ge(zeroed.sem, len(zero_fill))
            count = [0]

            def step_(ins):
                count[0] += 1
                ins.then_inc(made.sem, 1)
                pool.wait_ge(made.sem, count[0])

            step_(nc.gpsimd.affine_select(out=ident[:], in_=ident[:], compare_op=ALU.not_equal, fill=1.0, base=0,
                                          pattern=[[-1, P]], channel_multiplier=1))
            step_(nc.gpsimd.memset(head_ones[:], 1.0))
            step_(nc.gpsimd.affine_select(out=head_ones[:], in_=head_ones[:], compare_op=ALU.is_ge, fill=0.0, base=0,
                                          pattern=[[-DK_A, NH_A]], channel_multiplier=1))
            step_(nc.gpsimd.affine_select(out=head_ones[:], in_=head_ones[:], compare_op=ALU.is_ge, fill=0.0,
                                          base=DK_A - 1, pattern=[[DK_A, NH_A]], channel_multiplier=-1))
            step_(nc.gpsimd.memset(three_halves[:], 1.5))
            step_(nc.gpsimd.memset(chunk_keep[:], 1.0))
            step_(nc.gpsimd.memset(chunk_keep[:].rearrange("p (c t) -> p c t", t=CHUNK)[:, :, 0:1], 0.0))
            for l, s in enumerate(HALVES):
                m = zeros[:, 0:P // 2].rearrange("p (b r) -> p b r", r=s)
                n = P // (2 * s)
                step_(nc.gpsimd.memset(zeros[:, 0:P // 2], 1.0))
                step_(nc.gpsimd.affine_select(out=m, in_=m, compare_op=ALU.is_ge, fill=0.0, base=0,
                                              pattern=[[-2 * s, n], [0, s]], channel_multiplier=1))
                step_(nc.gpsimd.affine_select(out=m, in_=m, compare_op=ALU.is_ge, fill=0.0, base=s - 1,
                                              pattern=[[2 * s, n], [0, s]], channel_multiplier=-1))
                for h in range(NH_A):
                    step_(nc.gpsimd.tensor_copy(level_mask[:, l, h, :], zeros[:, 0:P // 2]))
            for par in range(PAR):
                m = zeros[:, 0:PAIRS]
                step_(nc.gpsimd.memset(m, 1.0))
                step_(nc.gpsimd.affine_select(out=m, in_=m, compare_op=ALU.is_ge, fill=0.0, base=-par * H,
                                              pattern=[[-PAR * H, PAIRS]], channel_multiplier=1))
                step_(nc.gpsimd.affine_select(out=m, in_=m, compare_op=ALU.is_ge, fill=0.0, base=par * H + H - 1,
                                              pattern=[[PAR * H, PAIRS]], channel_multiplier=-1))
                for pair in range(PAIRS):
                    step_(nc.gpsimd.tensor_tensor(par_mask[:, par:par + 1], par_mask[:, par:par + 1],
                                                  m[:, pair:pair + 1], ALU.add))
            assert count[0] == MADE
            def rstd_of(it, n):
                pool.wait_ge(n.guessed.sem, n.guessed.now(it))
                for r in range(NEWTON):
                    steps = ((n.t, n.y, n.y, ALU.mult), (n.t, n.t, n.v, ALU.mult),
                             (n.t, three_halves, n.t, ALU.subtract), (n.y, n.y, n.t, ALU.mult))
                    for k, (o, p0, p1, op) in enumerate(steps):
                        if r or k:
                            pool.wait_ge(n.newton.sem, n.newton.now(it, 4 * r + k))
                        nc.gpsimd.tensor_tensor(o[:], p0[:], p1[:], op).then_inc(n.newton.sem, 1)

            def body(it, in_n, in_a, in_b, in_c):
                if in_c:
                    rstd_of(it, norm_d)
                if in_b:
                    pool.wait_ge(v_out.sem, v_out.now(it))
                    pool.wait_ge(vg_moved.sem, vg_moved.before(it))
                    nc.gpsimd.tensor_tensor(v_tok[:].rearrange("p h d -> p (h d)"), v_raw[:], bv_bc[:], ALU.add)\
                        .then_inc(vb_ready.sem, 1)
                if in_a:
                    pool.wait_ge(edec_ready.sem, edec_ready.before(it))
                    wait_apart(pool, (c_parts.sem, c_parts.now(it)))
                    for l, src, c in ((1, c_ex, 1), (1, c_ex, 3), (0, c_rest, 1), (0, c_ex, 2)):
                        nc.gpsimd.tensor_copy(decay[:, l, c * CHUNK:(c + 1) * CHUNK],
                                              src[:, c * CHUNK:(c + 1) * CHUNK]).then_inc(decay_pool.sem, 1)
                if in_a:
                    last_mix = slice(NMIX - 1, NMIX)
                    pool.wait_ge(mix_ready.sem, mix_ready.now(it))
                    pool.wait_ge(delta_ready.sem, delta_ready.now(it))
                    nc.gpsimd.tensor_tensor(ud[:, last_mix], mix[:, last_mix], delta[:].unsqueeze(1), ALU.mult).then_inc(ud_last.sem, 1)
                    pool.wait_ge(ud_last.sem, ud_last.now(it))
                    pool.wait_ge(v_summed.sem, v_summed.before(it))
                    nc.gpsimd.tensor_tensor(xv[:, last_mix], ud[:, last_mix], a_xT[:, :, 1:P + 1].unsqueeze(1), ALU.add)\
                        .then_inc(xv_last.sem, 1)
                if in_a:
                    pool.wait_ge(edec_ready.sem, edec_ready.now(it))
                    pool.wait_ge(rk_ready.sem, rk_ready.now(it))
                    pool.wait_ge(att_summed.sem, att_summed.before(it))
                    nc.gpsimd.tensor_tensor(f_k[:, 0:2], edec[:, 0:2], kT[:].unsqueeze(1).to_broadcast([P, 2, P]),
                                            ALU.mult).then_inc(fk_ready.sem, 1)
                if in_b:
                    pool.wait_ge(k_moved.sem, k_moved.now(it))
                    nc.gpsimd.tensor_tensor(k_st[:], k_st[:], bk[:].unsqueeze(1).unsqueeze(1).to_broadcast([P, SB, J, H]),
                                            ALU.add).then_inc(kb_ready.sem, 1)
                if in_a:
                    nc.gpsimd.tensor_tensor(f_k[:, 2:NL], edec[:, 2:NL], kT[:].unsqueeze(1).to_broadcast([P, NL - 2, P]),
                                            ALU.mult).then_inc(fk_ready.sem, 1)
                if in_b:
                    pool.wait_ge(x1_ready.sem, x1_ready.before(it))
                    pool.wait_ge(x2_ready.sem, x2_ready.before(it))
                    nc.gpsimd.tensor_tensor(x1_bo[:], x1[:], bo_bc[:], ALU.add).then_inc(x1bo_ready.sem, 1)
                if in_c:
                    pool.wait_ge(x3_ready.sem, x3_ready.now(it))
                    nc.gpsimd.tensor_tensor(x23[:], x2[:], x3[:], ALU.add).then_inc(x23_ready.sem, 1)
                    pool.wait_ge(x23_ready.sem, x23_ready.now(it))
                    pool.wait_ge(stored.sem, stored.before(it))
                    nc.gpsimd.tensor_tensor(res[:], x23[:], ob_valid[:], ALU.add).then_inc(res_begun.sem, 1)
                if in_a:
                    pool.wait_ge(g_tanh.sem, g_tanh.now(it))
                    nc.gpsimd.tensor_tensor(g_gt[:], g_a[:], g_t[:], ALU.mult).then_inc(g_times.sem, 1)
                    pool.wait_ge(g_times.sem, g_times.now(it))
                    pool.wait_ge(gates_ready.sem, gates_ready.before(it))
                    nc.gpsimd.tensor_tensor(gate[:], g_a[:], g_gt[:], ALU.add).then_inc(gate_ready.sem, 1)
                    pool.wait_ge(gate_ready.sem, gate_ready.now(it))
                    pool.wait_ge(o_final.sem, o_final.before(it))
                    nc.gpsimd.tensor_tensor(gate_g[:], gate[:], lng_half[:], ALU.mult).then_inc(gates_ready.sem, 1)
                    nc.gpsimd.tensor_tensor(gate_b[:], gate[:], lnb_half[:], ALU.mult).then_inc(gates_ready.sem, 1)
                    rstd_of(it, norm_o)

            run(pool, body)

        @block.tensor
        def _(pe):
            mm = nc.tensor.matmul

            def turn(out_, in_, signal):
                for k in range(KT):
                    last = nc.tensor.transpose(out_[:, k * P:(k + 1) * P], in_[:, k * P:(k + 1) * P], ident[:])
                last.then_inc(signal.sem, 1)

            def project(out_, lhs, rhs, n=KT):
                for k in range(n):
                    last = mm(out_, lhs(k), rhs(k), start=(k == 0), stop=(k == n - 1))
                return last

            def b_project(bank, w, rhs, c0, c1):
                for c in range(c0, c1):
                    last = project(pB[:, bank, c * P:(c + 1) * P], lambda k: w[:, k, c * P:(c + 1) * P], rhs)
                return last

            def mixes(r, bank, which):
                for n, i in enumerate(which):
                    for k in range(KT):
                        rows, t = (slice(0, P), 0) if i < NMIX - 1 else (slice(0, PLR), 1)
                        last = mm(pA[:, bank, (n * KT + k) * P:(n * KT + k + 1) * P], w_mix[rows, i, k * P:(k + 1) * P],
                                  xx[rows, t, :], start=True, stop=True)
                last.then_inc(mix_summed.sem, 1)

            def levels(bank, which):
                for n, l in enumerate(which):
                    last = mm(pA[:, bank, n * 256:(n + 1) * 256], f_k[:, l, :], f_q[:, l, :, :], start=True, stop=True)
                return last

            def b_scores(g0, g1):
                for g in range(g0, g1):
                    s, jh = g // 2, g % 2
                    last = mm(pB[:, 1, g * 64:(g + 1) * 64], q_blk[:, s, jh * PAIRS:(jh + 1) * PAIRS, :, :],
                              k_st[:, s, jh * PAIRS:(jh + 1) * PAIRS, :], start=True, stop=True)
                return last

            def b_values(g0, g1):
                for g in range(g0, g1):
                    for par in range(PAR):
                        last = mm(pB[par * DH:(par + 1) * DH, 0, g * 64:(g + 1) * 64], v_g[:, g, :],
                                  p_T[:, g, :, par, :], start=True, stop=True)
                return last

            def b_out(j0, j1):
                for j in range(j0, j1):
                    last = mm(pB[:, 1, 0:D], o_B[:, j, :, :], w_ob[:, j, :], start=(j == 0), stop=(j == J - 1))
                return last

            ctx_of = lambda k: ctxT[:, k, :]
            x_of = lambda k: b_xT[:, k, :]

            def body(it, in_n, in_a, in_b, in_c):
                if in_a:
                    pe.wait_ge(a_normed.sem, a_normed.before(it))
                    pe.wait_ge(x1_ready.sem, x1_ready.before(it))
                    turn(pA[:, 0, :], a_xn, a_turned)
                if in_b:
                    pe.wait_ge(ctx_loaded.sem, ctx_loaded.now(it))
                    pe.wait_ge(ob_ready.sem, ob_ready.before(it))
                    project(pB[:, 0, 0:512], ctx_of, lambda k: w_vb[:, k, 0:512])
                if in_a:
                    pe.wait_ge(z0_ready.sem, z0_ready.now(it))
                    project(pA[:, 1, 0:P], lambda k: w_x0[:, k, 0:P], lambda k: z0[:, k, :])
                    project(pA[0:PLR, 1, P:2 * P], lambda k: w_x0[:, k, P:P + PLR], lambda k: z0[:, k, :])\
                        .then_inc(xx_summed.sem, 1)
                if in_b:
                    mm(pB[:, 0, 512:1024], ctx_of(0), w_vb[:, 0, 512:1024], start=True, stop=False)
                if in_a:
                    pe.wait_ge(xx_ready.sem, xx_ready.now(it))
                    mixes(0, 0, (0, 1))
                    mixes(1, 1, (2, 3))
                if in_b:
                    mm(pB[:, 0, 512:1024], ctx_of(1), w_vb[:, 1, 512:1024], start=False, stop=True).then_inc(vb_summed.sem, 1)
                    pe.wait_ge(b_normed.sem, b_normed.now(it))
                    if not isinstance(it, int) or it > LAG_C:
                        pe.wait_ge(ocT_ready.sem, ocT_ready.before(it))
                    turn(pC[:, 1, :], b_xn, b_turned)
                    pe.wait_ge(x2_ready.sem, x2_ready.before(it))
                    b_project(1, w_kb, ctx_of, 0, 4)
                if in_a:
                    pe.wait_ge(mix_ready.sem, mix_ready.now(it, 1))
                    mixes(2, 0, (4,))
                    pe.wait_ge(mix_ready.sem, mix_ready.now(it, 2))
                    pe.wait_ge(xv_ready.sem, xv_ready.now(it, 1))
                    project(pA[0:GLR, 1, 2 * P:3 * P], lambda k: w_wa[:, k, :], lambda k: xv[:, 1, k, :]).then_inc(w1_summed.sem, 1)
                if in_b:
                    b_project(1, w_kb, ctx_of, 4, 8).then_inc(kb_summed.sem, 1)
                if in_a:
                    pe.wait_ge(w1_ready.sem, w1_ready.now(it))
                    mm(pA[:, 1, 3 * P:4 * P], w_wgb[0:GLR, 0:KD], wg[0:GLR, :], start=True, stop=True)\
                        .then_inc(w_summed.sem, 1)
                if in_b:
                    pe.wait_ge(b_xT_ready.sem, b_xT_ready.now(it))
                    pe.wait_ge(v_out.sem, v_out.now(it))
                    b_project(0, w_q, x_of, 0, 4).then_inc(qb_summed.sem, 1)
                if in_c:
                    pe.wait_ge(c_normed.sem, c_normed.now(it))
                    pe.wait_ge(res_ready.sem, res_ready.before(it))
                    turn(pC[:, 0, :], c_xn, c_turned)
                if in_a:
                    pe.wait_ge(xv_ready.sem, xv_ready.now(it))
                    pe.wait_ge(mix_ready.sem, mix_ready.now(it))
                    project(pA[:, 0, 0:P], lambda k: w_r[:, k, :], lambda k: xv[:, 0, k, :])
                    project(pA[:, 0, P:2 * P], lambda k: w_k[:, k, :], lambda k: xv[:, 2, k, :])\
                        .then_inc(rk_summed.sem, 1)
                if in_b:
                    b_project(0, w_q, x_of, 4, 8).then_inc(qb_summed.sem, 1)
                if in_a:
                    pe.wait_ge(w_exp.sem, w_exp.now(it))
                    pe.wait_ge(xv_last.sem, xv_last.now(it))
                    project(pA[GLR:P, 1, 2 * P:3 * P], lambda k: w_ga[:, k, :], lambda k: xv[:, 4, k, :])
                    project(pA[:, 1, 0:VD], lambda k: xv[:, 3, k, :], lambda k: w_v[:, k, :]).then_inc(v_summed.sem, 1)
                if in_c:
                    pe.wait_ge(c_xT_ready.sem, c_xT_ready.now(it))
                    for w, o in ((w_qc, pC[:, 1, 0:256]), (w_kc, pC[:, 1, 256:512])):
                        for m in range(KT):
                            mm(o[:, m * P:(m + 1) * P], w[:, 0, m * P:(m + 1) * P], c_xT[:, 0, :], start=True, stop=False)
                            last = mm(o[:, m * P:m * P + NTE], w[:, 1, m * P:(m + 1) * P], c_xT[:, 1, 0:NTE],
                                      start=False, stop=True)
                    last.then_inc(qk_summed.sem, 1)
                    project(pC[:, 0, 256:512], lambda k: c_xT[:, k, :], lambda k: w_vc[:, k, :]).then_inc(vc_summed.sem, 1)
                if in_a:
                    pe.wait_ge(g1_ready.sem, g1_ready.now(it))
                    pe.wait_ge(v_ready.sem, v_ready.now(it))
                    mm(pA[:, 1, VD:2 * VD], wg[GLR:P, :], w_wgb[GLR:P, :], start=True, stop=True)\
                        .then_inc(g_summed.sem, 1)
                    pe.wait_ge(rk_ready.sem, rk_ready.now(it))
                    pe.wait_ge(fk_ready.sem, fk_ready.now(it, 1))
                    pe.wait_ge(fq_ready.sem, fq_ready.now(it, 2))
                    levels(0, (0, 1)).then_inc(att_summed.sem, 1)
                if in_b:
                    pe.wait_ge(kb_ready.sem, kb_ready.now(it))
                    pe.wait_ge(qb_ready.sem, qb_ready.now(it))
                    b_scores(0, NG).then_inc(s_summed.sem, 1)
                if in_a:
                    pe.wait_ge(g_ready.sem, g_ready.now(it))
                    pe.wait_ge(fk_ready.sem, fk_ready.now(it))
                    pe.wait_ge(fq_ready.sem, fq_ready.now(it, 4))
                    levels(1, (2, 3)).then_inc(att_summed.sem, 1)
                if in_c:
                    pe.wait_ge(qc_ready.sem, qc_ready.now(it))
                    pe.wait_ge(kc_ready.sem, kc_ready.now(it))
                    pe.wait_ge(vc_ready.sem, vc_ready.now(it))
                    for m in range(KT):
                        last = mm(pC[:, m, :], q_c[:, m, :], k_blk[:, m, :, :], start=True, stop=True)
                    last.then_inc(sc_summed.sem, 1)
                if in_a:
                    pe.wait_ge(fq_ready.sem, fq_ready.now(it))
                    pe.wait_ge(att_kept.sem, att_kept.now(it, 2))
                    levels(0, (4, 5)).then_inc(att_summed.sem, 1)
                    pe.wait_ge(att_kept.sem, att_kept.now(it, 4))
                    pe.wait_ge(quk_ready.sem, quk_ready.now(it))
                    levels(1, (6,))
                    mm(pA[:, 1, 256:256 + NH_A], quk[:], head_ones[:], start=True, stop=True).then_inc(att_summed.sem, 1)
                if in_a:
                    pe.wait_ge(att_kept.sem, att_kept.now(it))
                    for h in range(NH_A):
                        last = mm(pA[:, 0, h * DV_A:(h + 1) * DV_A], attT[:, h, :], v_a[:, h * DV_A:(h + 1) * DV_A],
                                  start=True, stop=True)
                    last.then_inc(oa_summed.sem, 1)
                if in_b:
                    pe.wait_ge(p_turned.sem, p_turned.now(it))
                    pe.wait_ge(vg_moved.sem, vg_moved.now(it))
                    b_values(0, NG).then_inc(ob_summed.sem, 1)
                if in_c:
                    pe.wait_ge(sc_exp.sem, sc_exp.now(it))
                    for h in range(NH_C):
                        last = nc.tensor.transpose(pC[:, h // 4, (h % 4) * P:(h % 4 + 1) * P], c_e[:, h, :], ident[:])
                    last.then_inc(pc_turned.sem, 1)
                if in_b:
                    pe.wait_ge(ob_ready.sem, ob_ready.now(it))
                    pe.wait_ge(s_dense.sem, s_dense.now(it))
                    b_out(0, 4)
                if in_c:
                    pe.wait_ge(pc_ready.sem, pc_ready.now(it))
                    for h in range(NH_C):
                        last = mm(pC[:, 0, h * DH_C:(h + 1) * DH_C], c_eT[:, h, :], v_c[:, h * DH_C:(h + 1) * DH_C],
                                  start=True, stop=True)
                    last.then_inc(oc_summed.sem, 1)
                if in_b:
                    b_out(4, 8).then_inc(yb_summed.sem, 1)
                if in_a:
                    pe.wait_ge(o_final.sem, o_final.now(it))
                    turn(pA[:, 1, :], o_f, o_turned)
                if in_c:
                    pe.wait_ge(oc_ready.sem, oc_ready.now(it))
                    turn(pC[:, 1, :], c_o[:].rearrange("p h d -> p (h d)"), oc_turned)
                if in_a:
                    pe.wait_ge(oT_ready.sem, oT_ready.now(it))
                    project(pA[:, 0, 256:512], lambda k: o_T[:, k, :], lambda k: w_oa[:, k, :]).then_inc(ya_summed.sem, 1)
                if in_c:
                    pe.wait_ge(ocT_ready.sem, ocT_ready.now(it))
                    project(pC[:, 0, 256:512], lambda k: c_oT[:, k, :], lambda k: w_oc[:, k, :]).then_inc(yc_summed.sem, 1)

            run(pe, body)

        @block.scalar
        def _(act):
            go = nc.scalar.activation

            def valid(dst, src, scale, bias):
                for k in range(KT):
                    e0 = 0
                    while e0 < NE and WIDTH[e0] > k * P:
                        rows = min(P, WIDTH[e0] - k * P)
                        e1 = e0
                        while e1 < NE and WIDTH[e1] > k * P and min(P, WIDTH[e1] - k * P) == rows:
                            e1 += 1
                        cols = slice(e0 * NTE, e1 * NTE)
                        psl = src[0:rows, k * P + e0 * NTE:k * P + e1 * NTE]
                        if scale is None:
                            last = go(dst[0:rows, k, cols], psl, ACT.Copy)
                        else:
                            last = go(dst[0:rows, k, cols], psl, ACT.Identity, scale=scale[0:rows, k:k + 1],
                                      bias=bias[0:rows, k:k + 1])
                        e0 = e1
                return last

            def k_spread(it):
                act.wait_ge(kb_summed.sem, kb_summed.now(it))
                act.wait_ge(s_summed.sem, s_summed.before(it))
                for hh in range(2):
                    for par in range(PAR):
                        src = pB[hh * DH:(hh + 1) * DH, 1, :].rearrange("p (c r q g) -> p g r q c", c=H // 2, r=PAIRS, q=PAR)
                        dst = k_st[par * DH:(par + 1) * DH].rearrange("p s (j r) h -> p (s j) r h", r=PAIRS)
                        last = go(dst[:, :, :, hh::2], src[:, :, :, par], ACT.Copy)
                last.then_inc(k_moved.sem, 1)

            def mix_out(it, r, bank, which):
                act.wait_ge(mix_summed.sem, mix_summed.now(it, r + 1))
                act.wait_ge(ud_ready.sem, ud_ready.before(it))
                act.wait_ge(ud_last.sem, ud_last.before(it))
                for n, i in enumerate(which):
                    for k in range(KT):
                        last = go(mix[:, i, k, :], pA[:, bank, (n * KT + k) * P:(n * KT + k + 1) * P], ACT.Identity,
                                  bias=x_bias[:, i, k:k + 1])
                last.then_inc(mix_ready.sem, 1)

            def body(it, in_n, in_a, in_b, in_c):
                if in_a:
                    act.wait_ge(a_turned.sem, a_turned.now(it))
                    act.wait_ge(z0_ready.sem, z0_ready.before(it))
                    act.wait_ge(xv_ready.sem, xv_ready.before(it))
                    act.wait_ge(xv_last.sem, xv_last.before(it))
                    go(a_xT[:, :, 1:P + 1], pA[:, 0, 0:2 * P].rearrange("p (k t) -> p k t", k=KT), ACT.Copy)\
                        .then_inc(a_xT_ready.sem, 1)
                    act.wait_ge(xx_summed.sem, xx_summed.now(it))
                    go(xx[:, 0, :], pA[:, 1, 0:P], ACT.Tanh).then_inc(xx_ready.sem, 1)
                    go(xx[0:PLR, 1, :], pA[0:PLR, 1, P:2 * P], ACT.Tanh).then_inc(xx_ready.sem, 1)
                    mix_out(it, 0, 0, (0, 1))
                    mix_out(it, 1, 1, (2, 3))
                if in_b:
                    act.wait_ge(b_turned.sem, b_turned.now(it))
                    act.wait_ge(qb_summed.sem, qb_summed.before(it))
                    go(b_xT[:], pC[:, 1, 0:2 * P].rearrange("p (k t) -> p k t", k=KT), ACT.Copy)\
                        .then_inc(b_xT_ready.sem, 1)
                    act.wait_ge(vb_summed.sem, vb_summed.now(it))
                    act.wait_ge(vb_ready.sem, vb_ready.before(it))
                    go(v_raw[:], pB[:, 0, :], ACT.Copy).then_inc(v_out.sem, 1)
                if in_a:
                    mix_out(it, 2, 0, (4,))
                    act.wait_ge(w1_summed.sem, w1_summed.now(it))
                    act.wait_ge(g_summed.sem, g_summed.before(it))
                    go(wg[0:GLR, :], pA[0:GLR, 1, 2 * P:3 * P], ACT.Tanh).then_inc(w1_ready.sem, 1)
                    act.wait_ge(x1_ready.sem, x1_ready.before(it))
                    act.wait_ge(x_loaded.sem, x_loaded.before(it))
                    go(x_keep[:], x_in[:], ACT.Copy).then_inc(x_kept.sem, 1)
                    act.wait_ge(w_summed.sem, w_summed.now(it))
                    act.wait_ge(c_parts.sem, c_parts.before(it))
                    go(nw[:], pA[:, 1, 3 * P:4 * P], ACT.Exp, bias=wb[:, 0:1]).then_inc(w_exp.sem, 1)
                if in_b:
                    k_spread(it)
                if in_c:
                    act.wait_ge(c_turned.sem, c_turned.now(it))
                    valid(c_xT, pC[:, 0, :], norm_w, norm_b).then_inc(c_xT_ready.sem, 1)
                if in_a:
                    act.wait_ge(rk_summed.sem, rk_summed.now(it))
                    act.wait_ge(quk_ready.sem, quk_ready.before(it))
                    act.wait_ge(fq_ready.sem, fq_ready.before(it))
                    act.wait_ge(fk_ready.sem, fk_ready.before(it))
                    go(qT[:], pA[:, 0, 0:P], ACT.Copy)
                    for h in range(NH_A):
                        rows = slice(h * DK_A, (h + 1) * DK_A)
                        go(q_blkA[rows, h, :], pA[rows, 0, 0:P], ACT.Copy)
                    go(kT[:], pA[:, 0, P:2 * P], ACT.Copy).then_inc(rk_ready.sem, 1)
                    act.wait_ge(decay_dve.sem, decay_dve.now(it))
                    act.wait_ge(decay_pool.sem, decay_pool.now(it))
                    act.wait_ge(fq_ready.sem, fq_ready.before(it))
                    go(edec[:], decay[:], ACT.Exp, scale=-1.0).then_inc(edec_ready.sem, 1)
                    act.wait_ge(v_summed.sem, v_summed.now(it))
                    act.wait_ge(oa_summed.sem, oa_summed.before(it))
                    act.wait_ge(dv_ready.sem, dv_ready.before(it))
                    go(v_a[:], pA[:, 1, 0:VD], ACT.Copy).then_inc(v_ready.sem, 1)
                    go(wg[GLR:P, :], pA[GLR:P, 1, 2 * P:3 * P], ACT.Tanh).then_inc(g1_ready.sem, 1)
                if in_c:
                    act.wait_ge(qk_summed.sem, qk_summed.now(it))
                    for m in range(KT):
                        go(q_c[:, m, :], pC[:, 1, m * P:(m + 1) * P], ACT.Identity,
                           bias=qb_c[:, m:m + 1]).then_inc(qc_ready.sem, 1)
                    for m in range(KT):
                        for h in range(4):
                            rows = slice(h * DH_C, (h + 1) * DH_C)
                            last = go(k_blk[rows, m, h, :], pC[rows, 1, 256 + m * P:256 + (m + 1) * P], ACT.Identity,
                                      bias=kb_c[rows, m:m + 1])
                    last.then_inc(kc_ready.sem, 1)
                if in_a:
                    act.wait_ge(g_ready.sem, g_ready.now(it))
                    act.wait_ge(g_times.sem, g_times.before(it))
                    go(g_t[:], g_a[:], ACT.Tanh, scale=0.5).then_inc(g_tanh.sem, 1)
                if in_b:
                    act.wait_ge(s_summed.sem, s_summed.now(it))
                    act.wait_ge(s_shift.sem, s_shift.before(it))
                    for pair in range(PAIRS):
                        rows = slice(pair * 32, (pair + 1) * 32)
                        last = go(s_d[rows, :, :],
                                  pB[rows, 1, :].rearrange("p (g q h) -> p g q h", q=PAIRS, h=H)[:, :, pair, :],
                                  ACT.Copy, scale=float(DH) ** -0.5)
                    last.then_inc(s_dense.sem, 1)
                if in_b:
                    act.wait_ge(s_shift.sem, s_shift.now(it))
                    act.wait_ge(p_masked.sem, p_masked.before(it))
                    go(s_e[:], s_sh[:], ACT.Exp).then_inc(s_exp.sem, 1)
                if in_c:
                    act.wait_ge(sc_nmax.sem, sc_nmax.now(it))
                    act.wait_ge(sc_recip.sem, sc_recip.before(it))
                    for h in range(NH_C):
                        last = go(c_e[:, h, :], pC[:, h // 4, (h % 4) * P:(h % 4 + 1) * P], ACT.Exp,
                                  scale=float(D) ** -0.5, bias=c_nm[:, h:h + 1], accum_out=c_sum[:, h:h + 1])
                    last.then_inc(sc_exp.sem, 1)
                if in_b:
                    act.wait_ge(ob_summed.sem, ob_summed.now(it))
                    act.wait_ge(yb_summed.sem, yb_summed.before(it))
                    go(o_B[:].rearrange("p j h s -> p s (j h)"), pB[:, 0, :].rearrange("p (s n) -> p s n", s=SB),
                       ACT.Copy).then_inc(ob_ready.sem, 1)
                if in_c:
                    act.wait_ge(pc_turned.sem, pc_turned.now(it))
                    act.wait_ge(oc_summed.sem, oc_summed.before(it))
                    go(c_eT[:], pC[:].rearrange("p b (h q) -> p (b h) q", q=P), ACT.Copy).then_inc(pc_ready.sem, 1)
                if in_a:
                    act.wait_ge(o_turned.sem, o_turned.now(it))
                    go(o_T[:], pA[:, 1, 0:2 * P].rearrange("p (k t) -> p k t", k=KT), ACT.Copy).then_inc(oT_ready.sem, 1)
                if in_c:
                    act.wait_ge(oc_turned.sem, oc_turned.now(it))
                    valid(c_oT, pC[:, 1, :], None, None).then_inc(ocT_ready.sem, 1)

            run(act, body)

        @block.vector
        def _(dve):
            v = nc.vector
            for t in zero_fill_bc:
                v.memset(t[:], 0.0).then_inc(zeroed_bc.sem, 1)

            def statistics(it, norms):
                for n, src in norms:
                    v.bn_stats(n.st[:], src[:]).then_inc(n.stats.sem, 1)
                for n, src in norms:
                    wait_apart(dve, (n.stats.sem, n.stats.now(it)))
                    v.bn_aggr(n.mv[:], n.st[:]).then_inc(n.aggr.sem, 1)
                for n, src in norms:
                    dve.wait_ge(n.aggr.sem, n.aggr.now(it))
                    v.tensor_scalar(n.v[:], n.mv[:, 1:2], EPS, 0.5, ALU.add, ALU.mult).then_inc(n.var_eps.sem, 1)
                for n, src in norms:
                    dve.wait_ge(n.var_eps.sem, n.var_eps.now(it))
                    v.tensor_scalar(n.bits[:], n.v[:].bitcast(I32), 1, None, ALU.logical_shift_right).then_inc(n.halved.sem, 1)
                for n, src in norms:
                    dve.wait_ge(n.halved.sem, n.halved.now(it))
                    v.tensor_scalar(n.y[:].bitcast(I32), n.bits[:], -1.0, RSQRT_BITS, ALU.mult, ALU.add).then_inc(n.guessed.sem, 1)

            def newton(it, norms):
                for r in range(NEWTON):
                    for n, src in norms:
                        if r:
                            dve.wait_ge(n.newton.sem, n.newton.now(it, 3 * r))
                        else:
                            dve.wait_ge(n.guessed.sem, n.guessed.now(it))
                        v.scalar_tensor_tensor(n.t[:], n.y[:], n.y[:, 0:1], n.v[:], ALU.mult, ALU.mult).then_inc(n.newton.sem, 1)
                    for n, src in norms:
                        dve.wait_ge(n.newton.sem, n.newton.now(it, 3 * r + 1))
                        v.tensor_scalar(n.t[:], n.t[:], -1.0, 1.5, ALU.mult, ALU.add).then_inc(n.newton.sem, 1)
                    for n, src in norms:
                        dve.wait_ge(n.newton.sem, n.newton.now(it, 3 * r + 2))
                        v.tensor_tensor(n.y[:], n.y[:], n.t[:], ALU.mult).then_inc(n.newton.sem, 1)

            def normalise(it, src, dst, n, normed):
                dve.wait_ge(n.newton.sem, n.newton.now(it))
                v.tensor_scalar(dst[:], src[:], n.mv[:, 0:1], n.y[:, 0:1], ALU.subtract, ALU.mult).then_inc(normed.sem, 1)

            def q_spread(it, half):
                dve.wait_ge(qb_summed.sem, qb_summed.now(it, half + 1))
                c0, c1 = half * H // 4, (half + 1) * H // 4
                for hh in range(2):
                    rows = slice(hh * DH, (hh + 1) * DH)
                    for par in range(PAR):
                        src = pB[rows, 0, c0 * P:c1 * P].rearrange("p (c s q j) -> p s q j c", c=H // 4, s=SB, q=PAR)[:, :, par]
                        dst = q_blk[par * DH:(par + 1) * DH, :, :, par, 2 * c0 + hh:2 * c1:2]
                        bias = bq[rows, c0:c1].unsqueeze(1).unsqueeze(1).to_broadcast([DH, SB, J, H // 4])
                        last = v.tensor_tensor(dst, src, bias, ALU.add)
                last.then_inc(qb_ready.sem, 1)

            def shifted_mixes(it, r, i0, n):
                dve.wait_ge(mix_ready.sem, mix_ready.now(it, r + 1))
                d_b = delta[:].unsqueeze(1).to_broadcast([P, n, KT, P])
                v.tensor_tensor(ud[:, i0:i0 + n], mix[:, i0:i0 + n], d_b, ALU.mult).then_inc(ud_ready.sem, 1)
                x_b = a_xT[:, :, 1:P + 1].unsqueeze(1).to_broadcast([P, n, KT, P])
                dve.wait_ge(ud_ready.sem, ud_ready.now(it, r + 1))
                v.tensor_tensor(xv[:, i0:i0 + n], ud[:, i0:i0 + n], x_b, ALU.add).then_inc(xv_ready.sem, 1)

            def keep(it, which):
                for l in which:
                    s = HALVES[l]
                    if l:
                        wait_apart(dve, (att_kept.sem, att_kept.now(it, l)))
                    heads = lambda t: t.rearrange("p h (n s) -> p h n s", s=s)
                    upper = attT[:].rearrange("p h (n u s) -> p h n u s", u=2, s=s)[:, :, :, 1, :]
                    src = pA[:, (l // 2) % 2, (l % 2) * 256:(l % 2 + 1) * 256].rearrange("p (h n s) -> p h n s", h=NH_A, s=s)
                    v.copy_predicated(upper, heads(level_mask[:, l, :, :]), src).then_inc(att_kept.sem, 1)

            def body(it, in_n, in_a, in_b, in_c):
                if in_a:
                    dve.wait_ge(a_xT_ready.sem, a_xT_ready.now(it))
                    dve.wait_ge(ud_last.sem, ud_last.before(it))
                    v.tensor_tensor(delta[:], a_xT[:, :, 0:P], a_xT[:, :, 1:P + 1], ALU.subtract).then_inc(delta_ready.sem, 1)
                    dve.wait_ge(delta_ready.sem, delta_ready.now(it))
                    dve.wait_ge(xx_summed.sem, xx_summed.before(it))
                    for k in range(KT):
                        v.scalar_tensor_tensor(z0[:, k, :], delta[:, k, :], mu0[:, k:k + 1], a_xT[:, k, 1:P + 1],
                                               ALU.mult, ALU.add).then_inc(z0_ready.sem, 1)
                norms = []
                if in_b:
                    dve.wait_ge(x1_ready.sem, x1_ready.before(it))
                    norms.append((norm_of_b, x1))
                if in_c:
                    dve.wait_ge(x2_ready.sem, x2_ready.before(it))
                    norms.append((norm_c, x2))
                statistics(it, norms)
                newton(it, norms)
                if in_b:
                    dve.wait_ge(b_turned.sem, b_turned.before(it))
                    normalise(it, x1, b_xn, norm_of_b, b_normed)
                if in_c:
                    dve.wait_ge(x23_ready.sem, x23_ready.before(it))
                    normalise(it, x2, x3, norm_c, x3_ready)
                    dve.wait_ge(x3_ready.sem, x3_ready.now(it))
                    statistics(it, [(norm_d, x3)])
                if in_a:
                    shifted_mixes(it, 0, 0, 2)
                    shifted_mixes(it, 1, 2, 2)
                if in_c:
                    dve.wait_ge(c_turned.sem, c_turned.before(it))
                    normalise(it, x3, c_xn, norm_d, c_normed)
                if in_a:
                    dve.wait_ge(w_exp.sem, w_exp.now(it))
                    v.tensor_tensor_scan(c_in[:], chunk_keep[:], nw[:], 0.0, ALU.mult, ALU.add).then_inc(c_in_ready.sem, 1)
                    dve.wait_ge(c_in_ready.sem, c_in_ready.now(it))
                    dve.wait_ge(decay_pool.sem, decay_pool.before(it))
                    tot = c_in[:].rearrange("p (c t) -> p c t", t=CHUNK)[:, :, CHUNK - 1:CHUNK]
                    v.tensor_tensor(c_ex[:], c_in[:], nw[:], ALU.subtract).then_inc(c_parts.sem, 1)
                    v.tensor_tensor(c_rest[:].rearrange("p (c t) -> p c t", t=CHUNK), tot.to_broadcast([P, P // CHUNK, CHUNK]),
                                    c_in[:].rearrange("p (c t) -> p c t", t=CHUNK), ALU.subtract).then_inc(c_parts.sem, 1)
                if in_a:
                    dve.wait_ge(c_parts.sem, c_parts.now(it))
                    dve.wait_ge(edec_ready.sem, edec_ready.before(it))
                    C_ = CHUNK
                    v.tensor_copy(decay[:, 1, :].rearrange("p (n u t) -> p n u t", u=2, t=C_)[:, :, 0, :],
                                  c_rest[:].rearrange("p (n u t) -> p n u t", u=2, t=C_)[:, :, 0, :]).then_inc(decay_dve.sem, 1)
                    v.tensor_scalar(decay[:, 0, 0:C_], c_rest[:, 0:C_], c_in[:, 2 * C_ - 1:2 * C_], None, ALU.add)\
                        .then_inc(decay_dve.sem, 1)
                    v.tensor_scalar(decay[:, 0, 3 * C_:], c_ex[:, 3 * C_:], c_in[:, 3 * C_ - 1:3 * C_], None, ALU.add)\
                        .then_inc(decay_dve.sem, 1)
                    for l in range(2, NL):
                        s = HALVES[l]
                        n = P // (2 * s)
                        view = lambda t: t.rearrange("p (n u s) -> p n u s", u=2, s=s)
                        ref = view(c_in[:])[:, :, 0, s - 1:s].to_broadcast([P, n, s])
                        v.tensor_tensor(view(decay[:, l, :])[:, :, 1, :], view(c_ex[:])[:, :, 1, :], ref, ALU.subtract)
                        v.tensor_tensor(view(decay[:, l, :])[:, :, 0, :], ref, view(c_in[:])[:, :, 0, :], ALU.subtract)\
                            .then_inc(decay_dve.sem, 2 if l > 2 else 1)
                if in_b:
                    dve.wait_ge(s_summed.sem, s_summed.before(it))
                    q_spread(it, 0)
                if in_a:
                    dve.wait_ge(edec_ready.sem, edec_ready.now(it))
                    for l in range(0, 2):
                        s = HALVES[l]
                        n = P // (2 * s)
                        upper = lambda t: t.rearrange("p h (n u s) -> p h n u s", u=2, s=s)[:, :, :, 1, :]
                        e_b = edec[:, l, :].rearrange("p (n u s) -> p n u s", u=2, s=s)[:, :, 1, :]
                        v.tensor_tensor(f_q[:, l, :, :].rearrange("p h (n s) -> p h n s", s=s),
                                        e_b.unsqueeze(1).to_broadcast([P, NH_A, n, s]), upper(q_blkA[:]), ALU.mult)\
                            .then_inc(fq_ready.sem, 1)
                if in_b:
                    q_spread(it, 1)
                if in_a:
                    dve.wait_ge(edec_ready.sem, edec_ready.now(it))
                    for l in range(2, NL):
                        s = HALVES[l]
                        n = P // (2 * s)
                        upper = lambda t: t.rearrange("p h (n u s) -> p h n u s", u=2, s=s)[:, :, :, 1, :]
                        e_b = edec[:, l, :].rearrange("p (n u s) -> p n u s", u=2, s=s)[:, :, 1, :]
                        v.tensor_tensor(f_q[:, l, :, :].rearrange("p h (n s) -> p h n s", s=s),
                                        e_b.unsqueeze(1).to_broadcast([P, NH_A, n, s]), upper(q_blkA[:]), ALU.mult)\
                            .then_inc(fq_ready.sem, 1)
                if in_a:
                    dve.wait_ge(g_summed.sem, g_summed.now(it))
                    dve.wait_ge(gate_ready.sem, gate_ready.before(it))
                    v.tensor_tensor(g_a[:], pA[:, 1, VD:2 * VD], gb_bc[:], ALU.add).then_inc(g_ready.sem, 1)
                if in_c:
                    dve.wait_ge(vc_summed.sem, vc_summed.now(it))
                    dve.wait_ge(oc_summed.sem, oc_summed.before(it))
                    v.tensor_tensor(v_c[:], pC[:, 0, 256:512], vb_bc[:], ALU.add).then_inc(vc_ready.sem, 1)
                if in_a:
                    dve.wait_ge(rk_ready.sem, rk_ready.now(it))
                    dve.wait_ge(att_summed.sem, att_summed.before(it))
                    v.scalar_tensor_tensor(quk[:], qT[:], bonus[:, 0:1], kT[:], ALU.mult, ALU.mult).then_inc(quk_ready.sem, 1)
                    wait_apart(dve, (att_summed.sem, att_summed.now(it, 1)), (oa_summed.sem, oa_summed.before(it)))
                    keep(it, (0, 1))
                if in_b:
                    dve.wait_ge(s_dense.sem, s_dense.now(it))
                    v.reduce_max(s_mx[:], s_d[:], AX_X).then_inc(s_max.sem, 1)
                    dve.wait_ge(s_max.sem, s_max.now(it))
                    v.tensor_tensor(s_sh[:], s_d[:], s_mx[:].unsqueeze(2).to_broadcast([P, NG, H]), ALU.subtract)\
                        .then_inc(s_shift.sem, 1)
                if in_a:
                    wait_apart(dve, (att_summed.sem, att_summed.now(it, 2)))
                    keep(it, (2, 3))
                if in_c:
                    dve.wait_ge(sc_summed.sem, sc_summed.now(it))
                    v.reduce_max(c_mx[:], pC[:].rearrange("p b (h k) -> p (b h) k", k=P), AX_X).then_inc(sc_max.sem, 1)
                    dve.wait_ge(sc_max.sem, sc_max.now(it))
                    v.tensor_scalar(c_nm[:], c_mx[:], -float(D) ** -0.5, None, ALU.mult).then_inc(sc_nmax.sem, 1)
                if in_a:
                    wait_apart(dve, (att_summed.sem, att_summed.now(it, 3)))
                    keep(it, (4, 5))
                if in_b:
                    dve.wait_ge(s_exp.sem, s_exp.now(it))
                    v.reduce_sum(s_sum[:], s_e[:], AX_X).then_inc(s_total.sem, 1)
                    dve.wait_ge(s_total.sem, s_total.now(it))
                    v.reciprocal(s_r[:], s_sum[:]).then_inc(s_recip.sem, 1)
                    dve.wait_ge(s_recip.sem, s_recip.now(it))
                    v.tensor_tensor(s_rm[:], s_r[:].unsqueeze(2).to_broadcast([P, NG, PAR]),
                                    par_mask[:].unsqueeze(1).to_broadcast([P, NG, PAR]), ALU.mult).then_inc(s_scale.sem, 1)
                    dve.wait_ge(s_scale.sem, s_scale.now(it))
                    v.tensor_tensor(p_m[:], s_e[:].unsqueeze(2).to_broadcast([P, NG, PAR, H]),
                                    s_rm[:].unsqueeze(3).to_broadcast([P, NG, PAR, H]), ALU.mult).then_inc(p_masked.sem, 1)
                if in_a:
                    wait_apart(dve, (att_summed.sem, att_summed.now(it, 4)))
                    keep(it, (6,))
                    v.tensor_copy(dterm[:], pA[:, 1, 256:256 + NH_A]).then_inc(dterm_ready.sem, 1)
                if in_b:
                    dve.wait_ge(p_masked.sem, p_masked.now(it))
                    dve.wait_ge(ob_summed.sem, ob_summed.before(it))
                    for pair in range(PAIRS):
                        rows = slice(pair * 32, (pair + 1) * 32)
                        last = v.transpose(p_T[rows, :, pair, :, :].rearrange("p g a h -> p g (a h)"),
                                           p_m[rows].rearrange("p g a h -> p g (a h)"))
                    last.then_inc(p_turned.sem, 1)
                if in_a:
                    dve.wait_ge(dterm_ready.sem, dterm_ready.now(it))
                    dve.wait_ge(v_ready.sem, v_ready.now(it))
                    v.tensor_tensor(dv[:].rearrange("p (h d) -> p h d", h=NH_A), v_a[:].rearrange("p (h d) -> p h d", h=NH_A),
                                    dterm[:].unsqueeze(2).to_broadcast([P, NH_A, DV_A]), ALU.mult).then_inc(dv_ready.sem, 1)
                    dve.wait_ge(oa_summed.sem, oa_summed.now(it))
                    dve.wait_ge(dv_ready.sem, dv_ready.now(it))
                    v.tensor_tensor(o_a[:], pA[:, 0, 0:VD], dv[:], ALU.add).then_inc(oa_ready.sem, 1)
                    dve.wait_ge(oa_ready.sem, oa_ready.now(it))
                    statistics(it, [(norm_o, o_a)])
                if in_n:
                    dve.wait_ge(x_loaded.sem, x_loaded.now(it))
                    statistics(it, [(norm_a, x_in)])
                    newton(it, [(norm_a, x_in)])
                    if in_a:
                        dve.wait_ge(a_turned.sem, a_turned.now(it))
                    normalise(it, x_in, a_xn, norm_a, a_normed)
                if isinstance(it, int) and it == LAG_N:
                    dve.wait_ge(loaded_a.sem, 16 * len(weights_a))
                    for t in (lng_half, lnb_half):
                        v.tensor_scalar(t[:], t[:], 0.5, None, ALU.mult).then_inc(ln_halved.sem, 1)
                if in_c:
                    dve.wait_ge(sc_exp.sem, sc_exp.now(it))
                    v.reciprocal(c_r[:], c_sum[:]).then_inc(sc_recip.sem, 1)
                    dve.wait_ge(sc_recip.sem, sc_recip.now(it))
                    dve.wait_ge(oc_summed.sem, oc_summed.now(it))
                    v.tensor_tensor(c_o[:], pC[:, 0, 0:D].rearrange("p (h d) -> p h d", d=DH_C),
                                    c_r[:].unsqueeze(2).to_broadcast([P, NH_C, DH_C]), ALU.mult).then_inc(oc_ready.sem, 1)
                if in_a:
                    normalise(it, o_a, o_n, norm_o, o_normed)
                    dve.wait_ge(o_normed.sem, o_normed.now(it))
                    dve.wait_ge(gates_ready.sem, gates_ready.now(it))
                    v.tensor_tensor(o_g[:], o_n[:], gate_g[:], ALU.mult).then_inc(o_scaled.sem, 1)
                    dve.wait_ge(o_scaled.sem, o_scaled.now(it))
                    dve.wait_ge(o_turned.sem, o_turned.before(it))
                    v.tensor_tensor(o_f[:], o_g[:], gate_b[:], ALU.add).then_inc(o_final.sem, 1)
                if in_b:
                    dve.wait_ge(yb_summed.sem, yb_summed.now(it))
                    dve.wait_ge(x1bo_ready.sem, x1bo_ready.now(it))
                    if in_c:
                        dve.wait_ge(x23_ready.sem, x23_ready.now(it))
                    v.tensor_tensor(x2[:], pB[:, 1, 0:D], x1_bo[:], ALU.add).then_inc(x2_ready.sem, 1)
                if in_a:
                    dve.wait_ge(ya_summed.sem, ya_summed.now(it))
                    if in_b:
                        dve.wait_ge(x1bo_ready.sem, x1bo_ready.now(it))
                    dve.wait_ge(x_kept.sem, x_kept.now(it))
                    v.tensor_tensor(x1[:], pA[:, 0, 256:512], x_keep[:], ALU.add).then_inc(x1_ready.sem, 1)
                if in_c:
                    dve.wait_ge(yc_summed.sem, yc_summed.now(it))
                    dve.wait_ge(res_begun.sem, res_begun.now(it))
                    for e in range(NE):
                        rows = slice(e * NTE, (e + 1) * NTE)
                        v.tensor_tensor(res[rows, 0:WIDTH[e]], pC[rows, 0, 256:256 + WIDTH[e]], res[rows, 0:WIDTH[e]],
                                        ALU.add).then_inc(res_ready.sem, 1)

            run(dve, body)


def kernel(**inputs):
    import numpy as _np
    import concourse.bacc as _bacc
    from concourse import mybir as _mybir
    from concourse.bass_utils import run_bass_kernel_spmd as _run

    p = {k.replace("L0_", ""): _np.asarray(v) for k, v in inputs.items()}
    con = _np.ascontiguousarray
    col = lambda t: con(t.reshape(-1, P).T)
    row = lambda t: con(t.reshape(1, -1))
    wo = p["xattn_Wo"].T.reshape(PAR, J, DH, D).transpose(1, 0, 2, 3).reshape(HD, D)
    laid = {
        "x": con(p["x"]), 
        "ctxT": con(p["ctx_1024"].reshape(B, SB, PAR, J // PAIRS, PAIRS, D).transpose(0, 5, 4, 2, 1, 3).reshape(B, D, P)),
        "mu0": col(p["attn_mu0"]), "Wx0": con(p["attn_Wx0"].T), "Wx2": con(p["attn_Wx2"].T),
        "x_bias": con(p["attn_x_bias"].reshape(NMIX * KT, P).T),
        "rW": con(p["attn_rW"].T), "kW": con(p["attn_kW"].T), "vW": con(p["attn_vW"].T),
        "wA": con(p["attn_wA"].T), "wB": con(p["attn_wB"].T), "wb": con(p["attn_wb"].reshape(P, 1)),
        "gA": con(p["attn_gA"].T), "gB": con(p["attn_gB"].T), "gb": row(p["attn_gb"]),
        "bonus": con(p["attn_bonus"].reshape(P, 1)), "ln_g": row(p["attn_ln_g"]), "ln_b": row(p["attn_ln_b"]),
        "oWa": con(p["attn_oW"].T),
        "Wq": con(p["xattn_Wq"].T), "Wk": con(p["xattn_Wk"].T), "Wv": con(p["xattn_Wv"].T), "Wo": con(wo),
        "bq": col(p["xattn_bq"]), "bk": con(_np.tile(p["xattn_bk"].reshape(H, DH).T, (PAR, 1))), "bv": row(p["xattn_bv"]), "bo": row(p["xattn_bo"]),
        "norm_w": col(p["ffn_norm_w"]), "norm_b": col(p["ffn_norm_b"]),
        "q_w": con(p["ffn_q_w"].T), "k_w": con(p["ffn_k_w"].T), "v_w": con(p["ffn_v_w"].T), "o_w": con(p["ffn_o_w"].T),
        "q_b": col(p["ffn_q_b"]), "k_b": col(p["ffn_k_b"]), "v_b": row(p["ffn_v_b"]), "o_b": row(p["ffn_o_b"]),
    }
    nc = _bacc.Bacc("TRN2", target_bir_lowering=False, num_devices=1)
    arrays, args = {}, {}
    for name, t in laid.items():
        arrays[f"in_{name}"] = t
        args[name] = nc.dram_tensor(f"in_{name}", t.shape, _mybir.dt.from_np(t.dtype), kind="ExternalInput").ap()
    out = nc.dram_tensor("out_0", (B, P, D), _mybir.dt.float32, kind="ExternalOutput").ap()
    decoder_layer(nc, args, out)
    r = _run(nc, [arrays], core_ids=[0])
    return r.results[0]["out_0"]
```
